# Optimizing a Trainium2 kernel written in Bass

```python
import numpy as np
import jax
import jax.numpy as jnp

def _softmax(x, axis=-1):
    return jax.nn.softmax(x, axis=axis)

def _gelu(x):
    return jax.nn.gelu(x, approximate=True)

def _silu(x):
    return jax.nn.silu(x)

def _sigmoid(x):
    return jax.nn.sigmoid(x)

def _layernorm(x, axis=-1, eps=1e-05):
    m = jnp.mean(x, axis=axis, keepdims=True)
    v = jnp.var(x, axis=axis, keepdims=True)
    return (x - m) / jnp.sqrt(v + eps)

def _scatter_add(tgt, idx, src, axis=0):
    return tgt.at[idx].add(src)

def _segment_sum(src, seg, n):
    return jax.ops.segment_sum(src, seg, n)
kernel_name = 'mk_conv_attn_hybrid_d4_conv_nchw256_r4_ad93f4'

def setup_inputs(seed: int=0):
    np.random.seed(seed)
    _w = jnp.asarray

    def _rec_inputs():
        import jax
        import jax.numpy as jnp
        _gk = jax.random.key(seed)
        x = 7.22e-05 + 1 * jax.random.normal(jax.random.fold_in(_gk, 1), (8, 64, 16, 16), jnp.float32)
        return x
    x = _rec_inputs()

    def _L0_conv_setup():
        import jax, jax.numpy as jnp
        import numpy as np
        IN_CH = 64
        OUT_CH = 64
        DIM = 8
        HEADS = IN_CH // DIM
        TOTAL = HEADS * DIM
        SCALE = 5
        EPS = 1e-15
        BN_EPS = 1e-05

        def conv2d(x, w, padding=0, groups=1):
            return jax.lax.conv_general_dilated(x, w, window_strides=(1, 1), padding=[(padding, padding), (padding, padding)], feature_group_count=groups, dimension_numbers=('NCHW', 'OIHW', 'NCHW'))

        def relu_linear_att(qkv):
            B, C, H, W = qkv.shape
            N = H * W
            G = C // (3 * DIM)
            qkv = qkv.astype(jnp.float32).reshape(B, G, 3 * DIM, N)
            q = jax.nn.relu(qkv[:, :, :DIM])
            k = jax.nn.relu(qkv[:, :, DIM:2 * DIM])
            v = qkv[:, :, 2 * DIM:]
            ones = jnp.ones((B, G, 1, N), qkv.dtype)
            v = jnp.concatenate([v, ones], axis=2)
            vk = jnp.einsum('bgdn,bgen->bgde', v, k)
            out = jnp.einsum('bgde,bgen->bgdn', vk, q)
            out = out[:, :, :DIM] / (out[:, :, DIM:] + EPS)
            return out.reshape(B, G * DIM, H, W)
        key = jax.random.key(seed)
        ks = jax.random.split(key, 8)
        B, H, W = (8, 16, 16)
        x = jax.random.normal(ks[0], (B, IN_CH, H, W), dtype=jnp.float32)
        w_qkv = jax.random.normal(ks[1], (3 * TOTAL, IN_CH, 1, 1), jnp.float32) * 0.05
        w_dw = jax.random.normal(ks[2], (3 * TOTAL, 1, SCALE, SCALE), jnp.float32) * 0.05
        w_pw = jax.random.normal(ks[3], (3 * TOTAL, DIM, 1, 1), jnp.float32) * 0.05
        w_proj = jax.random.normal(ks[4], (OUT_CH, 2 * TOTAL, 1, 1), jnp.float32) * 0.05
        bn_gamma = jnp.ones((OUT_CH,), jnp.float32)
        bn_beta = jnp.zeros((OUT_CH,), jnp.float32)
        bn_mean = jax.random.normal(ks[5], (OUT_CH,), jnp.float32) * 0.1
        bn_var = jax.random.uniform(ks[6], (OUT_CH,), jnp.float32, 0.5, 1.5)
        return {'x': x, 'w_qkv': w_qkv, 'w_dw': w_dw, 'w_pw': w_pw, 'w_proj': w_proj, 'bn_gamma': bn_gamma, 'bn_beta': bn_beta, 'bn_mean': bn_mean, 'bn_var': bn_var}
    _L0_conv_all = _L0_conv_setup()
    _L0_conv_in = {k: v for k, v in _L0_conv_all.items() if k in ('w_qkv', 'w_dw', 'w_pw', 'w_proj', 'bn_gamma', 'bn_beta', 'bn_mean', 'bn_var')}
    del _L0_conv_all

    def _L1_conv_setup():
        import jax, jax.numpy as jnp
        import numpy as np
        key = jax.random.key(seed)
        k1, k2 = jax.random.split(key)
        x = jax.random.normal(k1, (32, 64, 56, 56), dtype=jnp.float32)
        fan_in = 64 * 3 * 3
        bound = 1.0 / np.sqrt(fan_in)
        weight = jax.random.uniform(k2, (64, 64, 3, 3), dtype=jnp.float32, minval=-bound, maxval=bound)
        return {'x': x, 'weight': weight}
    _L1_conv_all = _L1_conv_setup()
    _L1_conv_in = {k: v for k, v in _L1_conv_all.items() if k in ('weight',)}
    del _L1_conv_all

    def _L2_attn_setup():
        import jax, jax.numpy as jnp
        import numpy as np
        N_HEAD = 16
        NOPE = 32
        ROPE = 16
        VDIM = 32
        HD = NOPE + ROPE
        WINDOW = 32
        KEEP = 128
        EPS = 1e-06

        def _freqs(T, dim=ROPE, theta=10000.0):
            f = 1.0 / theta ** (np.arange(0, dim, 2, dtype=np.float32) / dim)
            ang = np.outer(np.arange(T, dtype=np.float32), f)
            return (jnp.asarray(np.cos(ang)), jnp.asarray(np.sin(ang)))

        def _rms(x, w):
            return x * jax.lax.rsqrt(jnp.mean(x * x, -1, keepdims=True) + EPS) * w

        def _rope(x, cos, sin):
            T = x.shape[-2]
            c = cos[:T][None, None]
            s = sin[:T][None, None]
            xr, xi = jnp.split(x, 2, -1)
            return jnp.concatenate([xr * c - xi * s, xr * s + xi * c], -1)

        def _attn(q, k, v, mask=None):
            s = jnp.einsum('bhqd,bhkd->bhqk', q, k) / np.float32(np.sqrt(HD))
            if mask is not None:
                s = jnp.where(mask, s, jnp.float32(-1000000000.0))
            return jnp.einsum('bhqk,bhkd->bhqd', jax.nn.softmax(s, -1), v)
        key = jax.random.key(seed)
        ks = jax.random.split(key, 16)
        w = lambda k, shape: jax.random.normal(k, shape, jnp.float32) * 0.02
        B, T, C = (2, 512, 64)
        return {'x': jax.random.normal(ks[0], (B, T, C), jnp.float32), 'Wcq': w(ks[1], (C, 24)), 'q_norm_w': jnp.ones((24,), jnp.float32), 'Wq_nope': w(ks[2], (24, N_HEAD * NOPE)), 'Wq_rope': w(ks[3], (24, N_HEAD * ROPE)), 'Wckv': w(ks[4], (C, 32)), 'kv_norm_w': jnp.ones((32,), jnp.float32), 'Wk_nope': w(ks[5], (32, N_HEAD * NOPE)), 'Wv': w(ks[6], (32, N_HEAD * VDIM)), 'Wk_rope': w(ks[7], (C, ROPE)), 'W_imp': w(ks[8], (C, 1)), 'Wsel_k': w(ks[9], (C, N_HEAD * HD)), 'Wsel_v': w(ks[10], (C, N_HEAD * VDIM)), 'Wwin_k': w(ks[11], (C, N_HEAD * HD)), 'Wwin_v': w(ks[12], (C, N_HEAD * VDIM)), 'Wgate': w(ks[13], (C, 3)), 'Wproj': w(ks[14], (N_HEAD * VDIM, C))}
    _L2_attn_all = _L2_attn_setup()
    _L2_attn_in = {k: v for k, v in _L2_attn_all.items() if k in ('Wcq', 'q_norm_w', 'Wq_nope', 'Wq_rope', 'Wckv', 'kv_norm_w', 'Wk_nope', 'Wv', 'Wk_rope', 'W_imp', 'Wsel_k', 'Wsel_v', 'Wwin_k', 'Wwin_v', 'Wgate', 'Wproj')}
    del _L2_attn_all

    def _L2_ffn_setup():
        import jax, jax.numpy as jnp
        import numpy as np
        NUM_EXPERTS = 8
        TOP_K = 2
        B, S, D = (8, 2048, 64)

        def _moe(tokens, router_w, w1, b1, w2, b2):
            N = tokens.shape[0]
            E = router_w.shape[0]
            logits = tokens.astype(jnp.float32) @ router_w.astype(jnp.float32).T
            probs = jax.nn.softmax(logits, axis=-1)
            rw, re = jax.lax.top_k(probs, TOP_K)
            if TOP_K > 1:
                rw = rw / jnp.maximum(rw.sum(-1, keepdims=True), 1e-12)
            rw = rw.astype(tokens.dtype)
            combine = jnp.zeros((N, E), tokens.dtype).at[jnp.arange(N)[:, None], re].set(rw)
            out = tokens
            for e in range(E):
                h = jax.nn.gelu(tokens @ w1[e] + b1[e], approximate=False)
                y = h @ w2[e] + b2[e]
                out = out + combine[:, e:e + 1] * y
            return out
        key = jax.random.key(seed)
        ks = jax.random.split(key, 4)
        scale = 1.0 / np.sqrt(D).astype(np.float32)
        return {'input_embeddings': jax.random.normal(ks[0], (B, S, D), jnp.float32), 'router_w': jax.random.normal(ks[1], (NUM_EXPERTS, D), jnp.float32) * scale, 'w1': jax.random.normal(ks[2], (NUM_EXPERTS, D, D), jnp.float32) * scale, 'b1': jnp.zeros((NUM_EXPERTS, D), jnp.float32), 'w2': jax.random.normal(ks[3], (NUM_EXPERTS, D, D), jnp.float32) * scale, 'b2': jnp.zeros((NUM_EXPERTS, D), jnp.float32)}
    _L2_ffn_all = _L2_ffn_setup()
    _L2_ffn_in = {k: v for k, v in _L2_ffn_all.items() if k in ('router_w', 'w1', 'b1', 'w2', 'b2')}
    del _L2_ffn_all

    def _L3_attn_setup():
        import jax, jax.numpy as jnp
        import numpy as np
        HEADS = 8
        DIM_HEAD = 16
        EPS = 1e-05

        def _inst_norm(t):
            mu = jnp.mean(t, axis=-1, keepdims=True)
            var = jnp.var(t, axis=-1, keepdims=True)
            return (t - mu) / jnp.sqrt(var + EPS)
        key = jax.random.key(seed)
        k1, k2, k3, k4 = jax.random.split(key, 4)
        b, n, dim = (4, 2048, 64)
        inner = HEADS * DIM_HEAD
        x = jax.random.normal(k1, (b, n, dim), dtype=jnp.float32)
        w_qkv = jax.random.normal(k2, (dim, 3 * inner), dtype=jnp.float32) * (1.0 / DIM_HEAD)
        w_out = jax.random.normal(k3, (inner, dim), dtype=jnp.float32) * dim ** (-0.5)
        b_out = jax.random.normal(k4, (dim,), dtype=jnp.float32) * 0.01
        return {'x': x, 'w_qkv': w_qkv, 'w_out': w_out, 'b_out': b_out}
    _L3_attn_all = _L3_attn_setup()
    _L3_attn_in = {k: v for k, v in _L3_attn_all.items() if k in ('w_qkv', 'w_out', 'b_out')}
    del _L3_attn_all

    def _L3_ffn_setup():
        import math
        import jax, jax.numpy as jnp
        import numpy as np
        CAPACITY_FACTOR = 1.25
        TOP_K = 2
        LN_EPS = 1e-05

        def _layer_norm(x, gamma, beta):
            mu = jnp.mean(x, axis=-1, keepdims=True)
            var = jnp.var(x, axis=-1, keepdims=True)
            return (x - mu) * jax.lax.rsqrt(var + LN_EPS) * gamma + beta
        key = jax.random.key(seed)
        ks = jax.random.split(key, 4)
        B, S, D, F, E = (8, 1024, 64, 128, 8)
        x = jax.random.normal(ks[0], (B, S, D), dtype=jnp.float32)
        Wr = jax.random.normal(ks[1], (D, E), dtype=jnp.float32) / np.sqrt(D)
        br = jnp.zeros((E,), jnp.float32)
        W1 = jax.random.normal(ks[2], (E, D, F), dtype=jnp.float32) / np.sqrt(D)
        b1 = jnp.zeros((E, F), jnp.float32)
        W2 = jax.random.normal(ks[3], (E, F, D), dtype=jnp.float32) / np.sqrt(F)
        b2 = jnp.zeros((E, D), jnp.float32)
        gamma = jnp.ones((D,), jnp.float32)
        beta = jnp.zeros((D,), jnp.float32)
        return {'x': x, 'Wr': Wr, 'br': br, 'W1': W1, 'b1': b1, 'W2': W2, 'b2': b2, 'gamma': gamma, 'beta': beta}
    _L3_ffn_all = _L3_ffn_setup()
    _L3_ffn_in = {k: v for k, v in _L3_ffn_all.items() if k in ('Wr', 'br', 'W1', 'b1', 'W2', 'b2', 'gamma', 'beta')}
    del _L3_ffn_all
    return {'x': x, 'L0_conv_w_qkv': _L0_conv_in['w_qkv'], 'L0_conv_w_dw': _L0_conv_in['w_dw'], 'L0_conv_w_pw': _L0_conv_in['w_pw'], 'L0_conv_w_proj': _L0_conv_in['w_proj'], 'L0_conv_bn_gamma': _L0_conv_in['bn_gamma'], 'L0_conv_bn_beta': _L0_conv_in['bn_beta'], 'L0_conv_bn_mean': _L0_conv_in['bn_mean'], 'L0_conv_bn_var': _L0_conv_in['bn_var'], 'L1_conv_weight': _L1_conv_in['weight'], 'L2_attn_Wcq': _L2_attn_in['Wcq'], 'L2_attn_q_norm_w': _L2_attn_in['q_norm_w'], 'L2_attn_Wq_nope': _L2_attn_in['Wq_nope'], 'L2_attn_Wq_rope': _L2_attn_in['Wq_rope'], 'L2_attn_Wckv': _L2_attn_in['Wckv'], 'L2_attn_kv_norm_w': _L2_attn_in['kv_norm_w'], 'L2_attn_Wk_nope': _L2_attn_in['Wk_nope'], 'L2_attn_Wv': _L2_attn_in['Wv'], 'L2_attn_Wk_rope': _L2_attn_in['Wk_rope'], 'L2_attn_W_imp': _L2_attn_in['W_imp'], 'L2_attn_Wsel_k': _L2_attn_in['Wsel_k'], 'L2_attn_Wsel_v': _L2_attn_in['Wsel_v'], 'L2_attn_Wwin_k': _L2_attn_in['Wwin_k'], 'L2_attn_Wwin_v': _L2_attn_in['Wwin_v'], 'L2_attn_Wgate': _L2_attn_in['Wgate'], 'L2_attn_Wproj': _L2_attn_in['Wproj'], 'L2_ffn_router_w': _L2_ffn_in['router_w'], 'L2_ffn_w1': _L2_ffn_in['w1'], 'L2_ffn_b1': _L2_ffn_in['b1'], 'L2_ffn_w2': _L2_ffn_in['w2'], 'L2_ffn_b2': _L2_ffn_in['b2'], 'L3_attn_w_qkv': _L3_attn_in['w_qkv'], 'L3_attn_w_out': _L3_attn_in['w_out'], 'L3_attn_b_out': _L3_attn_in['b_out'], 'L3_ffn_Wr': _L3_ffn_in['Wr'], 'L3_ffn_br': _L3_ffn_in['br'], 'L3_ffn_W1': _L3_ffn_in['W1'], 'L3_ffn_b1': _L3_ffn_in['b1'], 'L3_ffn_W2': _L3_ffn_in['W2'], 'L3_ffn_b2': _L3_ffn_in['b2'], 'L3_ffn_gamma': _L3_ffn_in['gamma'], 'L3_ffn_beta': _L3_ffn_in['beta']}

def reference(x, L0_conv_w_qkv, L0_conv_w_dw, L0_conv_w_pw, L0_conv_w_proj, L0_conv_bn_gamma, L0_conv_bn_beta, L0_conv_bn_mean, L0_conv_bn_var, L1_conv_weight, L2_attn_Wcq, L2_attn_q_norm_w, L2_attn_Wq_nope, L2_attn_Wq_rope, L2_attn_Wckv, L2_attn_kv_norm_w, L2_attn_Wk_nope, L2_attn_Wv, L2_attn_Wk_rope, L2_attn_W_imp, L2_attn_Wsel_k, L2_attn_Wsel_v, L2_attn_Wwin_k, L2_attn_Wwin_v, L2_attn_Wgate, L2_attn_Wproj, L2_ffn_router_w, L2_ffn_w1, L2_ffn_b1, L2_ffn_w2, L2_ffn_b2, L3_attn_w_qkv, L3_attn_w_out, L3_attn_b_out, L3_ffn_Wr, L3_ffn_br, L3_ffn_W1, L3_ffn_b1, L3_ffn_W2, L3_ffn_b2, L3_ffn_gamma, L3_ffn_beta):
    import jax
    import jax.numpy as jnp

    def _L0_conv_ref(x, w_qkv, w_dw, w_pw, w_proj, bn_gamma, bn_beta, bn_mean, bn_var):
        import jax, jax.numpy as jnp
        import numpy as np
        IN_CH = 64
        OUT_CH = 64
        DIM = 8
        HEADS = IN_CH // DIM
        TOTAL = HEADS * DIM
        SCALE = 5
        EPS = 1e-15
        BN_EPS = 1e-05

        def conv2d(x, w, padding=0, groups=1):
            return jax.lax.conv_general_dilated(x, w, window_strides=(1, 1), padding=[(padding, padding), (padding, padding)], feature_group_count=groups, dimension_numbers=('NCHW', 'OIHW', 'NCHW'))

        def relu_linear_att(qkv):
            B, C, H, W = qkv.shape
            N = H * W
            G = C // (3 * DIM)
            qkv = qkv.astype(jnp.float32).reshape(B, G, 3 * DIM, N)
            q = jax.nn.relu(qkv[:, :, :DIM])
            k = jax.nn.relu(qkv[:, :, DIM:2 * DIM])
            v = qkv[:, :, 2 * DIM:]
            ones = jnp.ones((B, G, 1, N), qkv.dtype)
            v = jnp.concatenate([v, ones], axis=2)
            vk = jnp.einsum('bgdn,bgen->bgde', v, k)
            out = jnp.einsum('bgde,bgen->bgdn', vk, q)
            out = out[:, :, :DIM] / (out[:, :, DIM:] + EPS)
            return out.reshape(B, G * DIM, H, W)
        qkv = conv2d(x, w_qkv)
        agg = conv2d(qkv, w_dw, padding=SCALE // 2, groups=3 * TOTAL)
        agg = conv2d(agg, w_pw, groups=3 * HEADS)
        qkv_ms = jnp.concatenate([qkv, agg], axis=1)
        out = relu_linear_att(qkv_ms)
        out = conv2d(out, w_proj)
        inv = bn_gamma / jnp.sqrt(bn_var + BN_EPS)
        out = out * inv[None, :, None, None] + (bn_beta - bn_mean * inv)[None, :, None, None]
        return out

    def _L1_conv_ref(x, weight):
        import jax, jax.numpy as jnp
        import numpy as np
        bw = jnp.sign(weight)
        out = jax.lax.conv_general_dilated(x, bw, window_strides=(1, 1), padding=((1, 1), (1, 1)), dimension_numbers=('NCHW', 'OIHW', 'NCHW'))
        return out

    def _L2_attn_ref(x, Wcq, q_norm_w, Wq_nope, Wq_rope, Wckv, kv_norm_w, Wk_nope, Wv, Wk_rope, W_imp, Wsel_k, Wsel_v, Wwin_k, Wwin_v, Wgate, Wproj):
        import jax, jax.numpy as jnp
        import numpy as np
        N_HEAD = 16
        NOPE = 32
        ROPE = 16
        VDIM = 32
        HD = NOPE + ROPE
        WINDOW = 32
        KEEP = 128
        EPS = 1e-06

        def _freqs(T, dim=ROPE, theta=10000.0):
            f = 1.0 / theta ** (np.arange(0, dim, 2, dtype=np.float32) / dim)
            ang = np.outer(np.arange(T, dtype=np.float32), f)
            return (jnp.asarray(np.cos(ang)), jnp.asarray(np.sin(ang)))

        def _rms(x, w):
            return x * jax.lax.rsqrt(jnp.mean(x * x, -1, keepdims=True) + EPS) * w

        def _rope(x, cos, sin):
            T = x.shape[-2]
            c = cos[:T][None, None]
            s = sin[:T][None, None]
            xr, xi = jnp.split(x, 2, -1)
            return jnp.concatenate([xr * c - xi * s, xr * s + xi * c], -1)

        def _attn(q, k, v, mask=None):
            s = jnp.einsum('bhqd,bhkd->bhqk', q, k) / np.float32(np.sqrt(HD))
            if mask is not None:
                s = jnp.where(mask, s, jnp.float32(-1000000000.0))
            return jnp.einsum('bhqk,bhkd->bhqd', jax.nn.softmax(s, -1), v)
        B, T, C = x.shape
        cos, sin = _freqs(T)
        cq = _rms(x @ Wcq, q_norm_w)
        qn = (cq @ Wq_nope).reshape(B, T, N_HEAD, NOPE).transpose(0, 2, 1, 3)
        qr = _rope((cq @ Wq_rope).reshape(B, T, N_HEAD, ROPE).transpose(0, 2, 1, 3), cos, sin)
        q = jnp.concatenate([qn, qr], -1)
        gate = jax.nn.softmax((x @ Wgate).mean(1), -1)
        ckv = _rms(x @ Wckv, kv_norm_w)
        kn = (ckv @ Wk_nope).reshape(B, T, N_HEAD, NOPE).transpose(0, 2, 1, 3)
        v1 = (ckv @ Wv).reshape(B, T, N_HEAD, VDIM).transpose(0, 2, 1, 3)
        kr = (x @ Wk_rope / N_HEAD).reshape(B, T, 1, ROPE).transpose(0, 2, 1, 3)
        kr = _rope(kr, cos, sin)
        k1 = jnp.concatenate([kn, jnp.broadcast_to(kr, (B, N_HEAD, T, ROPE))], -1)
        ii = jnp.arange(T)
        causal = ii[:, None] >= ii[None, :]
        o1 = _attn(q, k1, v1, causal[None, None])
        scores = (x @ W_imp)[..., 0]
        _, idx = jax.lax.top_k(scores, KEEP)
        idx = jnp.sort(idx, 1)
        sel = jnp.take_along_axis(x, idx[..., None], 1)
        ks = (sel @ Wsel_k).reshape(B, KEEP, N_HEAD, HD).transpose(0, 2, 1, 3)
        vs = (sel @ Wsel_v).reshape(B, KEEP, N_HEAD, VDIM).transpose(0, 2, 1, 3)
        ks = jnp.concatenate([ks[..., :NOPE], _rope(ks[..., NOPE:], cos, sin)], -1)
        o2 = _attn(q, ks, vs)
        kw = (x @ Wwin_k).reshape(B, T, N_HEAD, HD).transpose(0, 2, 1, 3)
        vw = (x @ Wwin_v).reshape(B, T, N_HEAD, VDIM).transpose(0, 2, 1, 3)
        kw = jnp.concatenate([kw[..., :NOPE], _rope(kw[..., NOPE:], cos, sin)], -1)
        winmask = causal & (ii[:, None] - ii[None, :] < WINDOW)
        o3 = _attn(q, kw, vw, winmask[None, None])
        g = gate[:, :, None, None, None]
        o = g[:, 0] * o1 + g[:, 1] * o2 + g[:, 2] * o3
        o = o.transpose(0, 2, 1, 3).reshape(B, T, N_HEAD * VDIM)
        return o @ Wproj

    def _L2_ffn_ref(input_embeddings, router_w, w1, b1, w2, b2):
        import jax, jax.numpy as jnp
        import numpy as np
        NUM_EXPERTS = 8
        TOP_K = 2
        B, S, D = (8, 2048, 64)

        def _moe(tokens, router_w, w1, b1, w2, b2):
            N = tokens.shape[0]
            E = router_w.shape[0]
            logits = tokens.astype(jnp.float32) @ router_w.astype(jnp.float32).T
            probs = jax.nn.softmax(logits, axis=-1)
            rw, re = jax.lax.top_k(probs, TOP_K)
            if TOP_K > 1:
                rw = rw / jnp.maximum(rw.sum(-1, keepdims=True), 1e-12)
            rw = rw.astype(tokens.dtype)
            combine = jnp.zeros((N, E), tokens.dtype).at[jnp.arange(N)[:, None], re].set(rw)
            out = tokens
            for e in range(E):
                h = jax.nn.gelu(tokens @ w1[e] + b1[e], approximate=False)
                y = h @ w2[e] + b2[e]
                out = out + combine[:, e:e + 1] * y
            return out
        b, s, d = input_embeddings.shape
        tokens = input_embeddings.reshape(b * s, d)
        return _moe(tokens, router_w, w1, b1, w2, b2).reshape(b, s, d)

    def _L3_attn_ref(x, w_qkv, w_out, b_out):
        import jax, jax.numpy as jnp
        import numpy as np
        HEADS = 8
        DIM_HEAD = 16
        EPS = 1e-05

        def _inst_norm(t):
            mu = jnp.mean(t, axis=-1, keepdims=True)
            var = jnp.var(t, axis=-1, keepdims=True)
            return (t - mu) / jnp.sqrt(var + EPS)
        b, n, dim = x.shape
        qkv = x @ w_qkv
        q, k, v = jnp.split(qkv, 3, axis=-1)
        to_heads = lambda t: t.reshape(b, n, HEADS, DIM_HEAD).transpose(0, 2, 1, 3)
        q, k, v = (to_heads(q), to_heads(k), to_heads(v))
        k = _inst_norm(k)
        v = _inst_norm(v)
        dots = jnp.einsum('bhnd,bhne->bhde', k, v)
        out = jnp.einsum('bhnd,bhde->bhne', q, dots) * (1.0 / n)
        out = out.transpose(0, 2, 1, 3).reshape(b, n, HEADS * DIM_HEAD)
        return out @ w_out + b_out

    def _L3_ffn_ref(x, Wr, br, W1, b1, W2, b2, gamma, beta):
        import math
        import jax, jax.numpy as jnp
        import numpy as np
        CAPACITY_FACTOR = 1.25
        TOP_K = 2
        LN_EPS = 1e-05

        def _layer_norm(x, gamma, beta):
            mu = jnp.mean(x, axis=-1, keepdims=True)
            var = jnp.var(x, axis=-1, keepdims=True)
            return (x - mu) * jax.lax.rsqrt(var + LN_EPS) * gamma + beta
        B, S, D = x.shape
        E = Wr.shape[1]
        N = B * S
        K = TOP_K
        logits = jnp.mean(x, axis=1) @ Wr + br
        routing_weights = jax.nn.softmax(logits, axis=-1)
        capacity = float(math.ceil(N * CAPACITY_FACTOR / E))
        expected_loads = routing_weights.sum(axis=0) * (N / B)
        scale = jnp.where(expected_loads > capacity, capacity / expected_loads, 1.0)
        routing_weights = jax.nn.softmax(routing_weights * scale, axis=-1)
        rw_tok = jnp.broadcast_to(routing_weights[:, None, :], (B, S, E)).reshape(N, E)
        top_w, top_i = jax.lax.top_k(rw_tok, K)
        top_w = jax.nn.softmax(top_w, axis=-1)
        xf = x.reshape(N, D)
        h = jax.nn.gelu(jnp.einsum('nd,edf->enf', xf, W1) + b1[:, None, :], approximate=False)
        y = jnp.einsum('enf,efd->end', h, W2) + b2[:, None, :]
        w_dense = jnp.zeros((N, E), x.dtype).at[jnp.arange(N)[:, None], top_i].add(top_w)
        out = jnp.einsum('ne,end->nd', w_dense, y).reshape(B, S, D)
        out = _layer_norm(out + x, gamma, beta)
        return out

    def _gn(v, G=32, eps=1e-05):
        B_, C_, H_, W_ = v.shape
        g = v.reshape(B_, G, C_ // G, H_, W_)
        m = jnp.mean(g, axis=(2, 3, 4), keepdims=True)
        s = jnp.var(g, axis=(2, 3, 4), keepdims=True)
        return ((g - m) / jnp.sqrt(s + eps)).reshape(v.shape)

    def _ln_c(v, eps=1e-06):
        m = jnp.mean(v, axis=1, keepdims=True)
        s = jnp.var(v, axis=1, keepdims=True)
        return (v - m) / jnp.sqrt(s + eps)

    def _ln_t(v, eps=1e-05):
        m = jnp.mean(v, axis=-1, keepdims=True)
        s = jnp.var(v, axis=-1, keepdims=True)
        return (v - m) / jnp.sqrt(s + eps)

    def _to_tokens(v):
        B_, C_, H_, W_ = v.shape
        return v.reshape(B_, C_, H_ * W_).transpose(0, 2, 1)

    def _from_tokens(t, like):
        B_, C_, H_, W_ = like.shape
        return t.transpose(0, 2, 1).reshape(B_, C_, H_, W_)
    x = x + _L0_conv_ref(_gn(x), L0_conv_w_qkv, L0_conv_w_dw, L0_conv_w_pw, L0_conv_w_proj, L0_conv_bn_gamma, L0_conv_bn_beta, L0_conv_bn_mean, L0_conv_bn_var)
    x = x + _L1_conv_ref(_gn(x), L1_conv_weight)
    t = _to_tokens(x)
    t = t + _L2_attn_ref(_ln_t(t), L2_attn_Wcq, L2_attn_q_norm_w, L2_attn_Wq_nope, L2_attn_Wq_rope, L2_attn_Wckv, L2_attn_kv_norm_w, L2_attn_Wk_nope, L2_attn_Wv, L2_attn_Wk_rope, L2_attn_W_imp, L2_attn_Wsel_k, L2_attn_Wsel_v, L2_attn_Wwin_k, L2_attn_Wwin_v, L2_attn_Wgate, L2_attn_Wproj)
    t = t + _L2_ffn_ref(_ln_t(t), L2_ffn_router_w, L2_ffn_w1, L2_ffn_b1, L2_ffn_w2, L2_ffn_b2)
    t = t + _L3_attn_ref(_ln_t(t), L3_attn_w_qkv, L3_attn_w_out, L3_attn_b_out)
    t = t + _L3_ffn_ref(_ln_t(t), L3_ffn_Wr, L3_ffn_br, L3_ffn_W1, L3_ffn_b1, L3_ffn_W2, L3_ffn_b2, L3_ffn_gamma, L3_ffn_beta)
    x = _from_tokens(t, x)
    return x

_drawn_inputs = setup_inputs


def setup_inputs(seed=0):
    import zlib

    import numpy as np

    out = dict(_drawn_inputs(seed))
    spreads = {'L0_conv_bn_gamma': (1.0, 0.6),
     'L0_conv_bn_beta': (0.0, 0.1),
     'L2_attn_q_norm_w': (1.0, 0.6),
     'L2_attn_kv_norm_w': (1.0, 0.6),
     'L2_ffn_b1': (0.0, 0.8),
     'L2_ffn_b2': (0.0, 0.8),
     'L3_ffn_br': (0.0, 0.645),
     'L3_ffn_b1': (0.0, 2.0),
     'L3_ffn_b2': (0.0, 2.0),
     'L3_ffn_gamma': (1.0, 0.6),
     'L3_ffn_beta': (0.0, 0.8)}
    factors = {'L0_conv_w_qkv': 2.87,
     'L0_conv_w_dw': 8.0,
     'L0_conv_w_pw': 8.0,
     'L0_conv_w_proj': 2.749,
     'L0_conv_bn_var': 3.745,
     'L2_attn_Wcq': 8.0,
     'L2_attn_Wq_nope': 8.0,
     'L2_attn_Wq_rope': 8.0,
     'L2_attn_Wckv': 27.885,
     'L2_attn_Wk_nope': 24.214,
     'L2_attn_Wv': 23.238,
     'L2_attn_Wk_rope': 200.0,
     'L2_attn_W_imp': 8.0,
     'L2_attn_Wsel_k': 8.0,
     'L2_attn_Wsel_v': 8.0,
     'L2_attn_Wwin_k': 8.0,
     'L2_attn_Wwin_v': 8.0,
     'L2_attn_Wgate': 63.725,
     'L2_attn_Wproj': 8.0,
     'L2_ffn_router_w': 3.104,
     'L2_ffn_w1': 3.092,
     'L2_ffn_w2': 2.81,
     'L3_attn_w_qkv': 3.488,
     'L3_attn_w_out': 3.465,
     'L3_attn_b_out': 29.305,
     'L3_ffn_Wr': 4.463,
     'L3_ffn_W1': 3.528,
     'L3_ffn_W2': 3.175}
    for name, (base, spread) in spreads.items():
        noise = np.random.default_rng([zlib.crc32(name.encode()), seed]).standard_normal(out[name].shape)
        drawn = base * np.exp(spread * noise) if base else spread * noise
        out[name] = jnp.asarray(drawn.astype(out[name].dtype))
    for name, factor in factors.items():
        out[name] = (out[name] * factor).astype(out[name].dtype)
    return out
```

```python
from contextlib import ExitStack

import numpy as np

import concourse.bass as bass
from concourse import mybir

ALU = mybir.AluOpType
ACT = mybir.ActivationFunctionType
AX = mybir.AxisListType
F32 = mybir.dt.float32
BF16 = mybir.dt.bfloat16

P = 128
B, C, H, W = 8, 64, 16, 16
T = H * W
NT = T // P
PITCH = 20
HEADS, NOPE, ROPE, VDIM = 16, 32, 16, 32
CQ, CKV = 24, 32
HD = NOPE + ROPE
KEEP, WINDOW = 128, 32
NEG = -1.0e9
E, DE = 8, 64
FF = 128
BR = 3
HB = HEADS * BR
BAND = P + WINDOW
SCALE = 1.0 / float(np.sqrt(np.float32(HD)))

PAIRS5 = [(0, dy, dx) for dy in range(5) for dx in (0, 2)] + [(1, 0, 4), (1, 2, 4), (0, 4, 4)]
PAIRS3 = [(0, dy, 0) for dy in range(3)] + [(1, 0, 2), (0, 2, 2)]


def second_tap(pair, size):
    copy, dy, dx = pair
    dy, dx = (dy, dx + 1) if copy == 0 else (dy + 1, dx)
    return (dy, dx) if dy < size and dx < size else None


PREP = dict(dw_kv=26, dw_q=26, wi_kv=64, wi_q=64, pw_kv=128, pw_q=64, conv1=5 * 64, wqn_t=HEADS * CQ,
            wkn_t=HEADS * CKV)
EARLY = dict(pairmean=128, w_q0=64, w_kv0=128, proj0=128, bn=4, blk8=128, ident=128)
LATE = dict(w_small=68, w_kr=128, nw=1, w_q=HEADS * 128, w_v1=512, w_v=512, w_p=4 * 64, w_k=HEADS * 128,
            qtab=T, ktab=T, before=128, iota=128, ties=2 * T, first8=64,
            r2=E, w1=4 * 128, b1=4, w2=4 * 128, b2=E * C,
            q3=128, kv3=256, out3=64, bout=64, blk16=128, r3=E, br3=E)
FINAL = dict(f1=E * FF, fb1=E, f2=E * C, fb2=C, gamma=C, beta=C)
MASKS = dict(identb=128, causal_s=128, causal_t=128, band_s=128, band_t=128, band_s1=BAND, band_t0=BAND,
             pick=HB)


def offsets(table):
    at, out = 0, {}
    for name, n in table.items():
        out[name] = (at, n)
        at += n
    return out, at


def build(nc, x_in, prep_in, early_in, late_in, masks_in, final_in, y_out):
    ctx = ExitStack()
    with ctx:
        def sb(name, shape, dt=F32):
            return ctx.enter_context(nc.sbuf_tensor(name, shape, dt))

        sems = {}

        def S(name):
            if name not in sems:
                sems[name] = ctx.enter_context(nc.semaphore("s_" + name))
            return sems[name]

        eo, en = offsets(EARLY)
        lo, ln = offsets(LATE)
        mo, mn = offsets(MASKS)
        early = sb("early", [P, en])
        late = sb("late", [P, ln])
        masks = sb("masks", [P, mn], BF16)

        po, pn = offsets(PREP)
        fo, fn = offsets(FINAL)
        pr = sb("pr", [P, 2, 2, 1856])
        kwT = sb("kwT", [P, HEADS, T])
        prep = pr[:, 1, :, :].rearrange("p a n -> p (a n)")[:, 0:pn]
        masks32 = kwT[:, :, :].rearrange("p h t -> p (h t)")[:, 0:mn]
        final = kwT[:, :, :].rearrange("p h t -> p (h t)")[:, 0:fn]

        def cst(name):
            for table, tile in ((eo, early), (lo, late), (mo, masks), (po, prep), (fo, final)):
                if name in table:
                    a, n = table[name]
                    return tile[:, a:a + n]

        ident, identb = cst("ident"), cst("identb")
        w_q = cst("w_q").rearrange("p (h m) -> p h m", h=HEADS)
        w_k = cst("w_k").rearrange("p (h m) -> p h m", h=HEADS)
        w_p = cst("w_p").rearrange("p (g m) -> p g m", g=4)
        w1 = cst("w1").rearrange("p (g m) -> p g m", g=4)
        w2 = cst("w2").rearrange("p (g m) -> p g m", g=4)
        f1 = cst("f1").rearrange("p (e m) -> p e m", e=E)
        f2 = cst("f2").rearrange("p (e m) -> p e m", e=E)
        ties = cst("ties").rearrange("p (t m) -> p t m", t=NT)
        first8 = cst("first8").rearrange("p (e j) -> p e j", e=E)
        conv1 = cst("conv1").rearrange("p (n m) -> p n m", n=len(PAIRS3))
        dw_kv, dw_q = cst("dw_kv"), cst("dw_q")
        pick = cst("pick")
        wqn_t = cst("wqn_t").rearrange("p (h m) -> p h m", h=HEADS)
        wkn_t = cst("wkn_t").rearrange("p (h m) -> p h m", h=HEADS)

        wc_kv = sb("wc_kv", [P, 13, P])
        wc_q = sb("wc_q", [P, 13, C])
        bin1 = sb("bin1", [P, 5, C])
        binn = sb("binn", [P, 5, C])
        bnc = sb("bnc", [P, 4])
        half = sb("half", [P, 1])
        onesk = sb("onesk", [P, 32])
        meank = sb("meank", [P, P])

        xin = sb("xin", [P, T])
        xs = sb("xs", [P, T])
        xg = sb("xg", [P, T])
        img = [sb(f"img{i}", [P, PITCH, PITCH]) for i in range(2)]
        st = sb("st", [P, 2, 6])
        mv = sb("mv", [P, 2, 2])
        gm = sb("gm", [P, 2])
        gv = sb("gv", [P, 2])
        gt = sb("gt", [P, 2])
        kv1 = sb("kv1", [P, T])
        q0 = sb("q0", [P, T])
        ktok = sb("ktok", [P, NT, P])
        vtok = sb("vtok", [P, NT, P + 1])
        kvm = sb("kvm", [P, P])
        ksm = sb("ksm", [P, P])
        den0 = sb("den0", [P, T])
        rec0 = sb("rec0", [P, T])
        o0 = sb("o0", [P, T])
        x1 = sb("x1", [P, T])
        t1 = sb("t1", [P, NT, C])
        xn = sb("xn", [P, NT, C])
        xnT = sb("xnT", [P, T])
        sm = sb("sm", [P, NT, 68])
        sq = sb("sq", [P, NT, 64])
        ms = sb("ms", [P, 2, NT])
        rs = sb("rs", [P, 2, NT])
        cn = sb("cn", [P, NT, 64])
        cnT = sb("cnT", [P, T])
        gl = sb("gl", [P, BR])
        gs = sb("gs", [P, 8])
        gate = sb("gate", [P, BR])
        sbc = sb("sbc", [P, NT, P])
        srow = sb("srow", [P, T])
        cmp_ = sb("cmp_", [P, T])
        rank = sb("rank", [P, 4])
        ranks = sb("ranks", [P, NT])
        sel = sb("sel", [P, NT])
        pos = sb("pos", [P, NT])
        pickm = sb("pickm", [P, NT, KEEP])
        selT = sb("selT", [P, KEEP])
        k1T = sb("k1T", [P, T])
        qT = sb("qT", [P, HEADS, T])
        ksT = sb("ksT", [P, HEADS, KEEP])
        k1b = sb("k1b", [P, T], BF16)
        qb = sb("qb", [P, 2, 2, T], BF16)
        kwb = sb("kwb", [P, 2, 2, T], BF16)
        ksb = sb("ksb", [P, 2, 2, KEEP], BF16)
        v1 = sb("v1", [P, NT, HEADS * VDIM])
        vw = sb("vw", [P, NT, HEADS * VDIM])
        vs = sb("vs", [P, HEADS * VDIM])
        mx = sb("mx", [P, NT, HB])
        mh = sb("mh", [P, NT, P], BF16)
        mT = sb("mT", [P, T], BF16)
        scaled = pr[:, 0, 0, 0:26 * C].rearrange("p (n c) -> p n c", n=26)
        scaled_q = pr[0:C, 0, 1, 0:26 * C].rearrange("p (n c) -> p n c", n=26)
        rden = sb("rden", [P, 2, T])
        ob = sb("ob", [P, 2, BR, T])
        oT = sb("oT", [P, 4, T])
        t2 = sb("t2", [P, NT, C])
        lg = sb("lg", [P, NT, E])
        pe8 = sb("pe8", [P, NT, E])
        c8 = sb("c8", [P, NT, 8])
        cg = sb("cg", [P, NT, E, E])
        ce = sb("ce", [P, NT, E, E])
        comb = sb("comb", [P, NT, E])
        hm = sb("hm", [P, 4, T])
        yb = sb("yb", [P, NT, E, C])
        ysum = sb("ysum", [P, NT, C])
        t3 = sb("t3", [P, NT, C])
        q3 = sb("q3", [P, T])
        kv3 = sb("kv3s", [P, NT, 16, 16])
        kvq = sb("kvq", [P, NT, 16, 16])
        n3 = sb("n3", [P, 4, NT * 16])
        dT = sb("dT", [P, P])
        m3 = sb("m3", [P, C])
        t4 = sb("t4", [P, NT, C])
        x4 = sb("x4", [P, NT, C])
        x4T = sb("x4T", [P, T])
        all_t4 = sb("all_t4", [P, B, NT, C])
        all_x4 = sb("all_x4", [P, B, NT, C])
        xbar = sb("xbar", [P, B])
        lr = sb("lr", [P, E])
        rw = sb("rw", [P, E])
        rt = sb("rt", [P, 12])
        load = sb("load", [P, E])
        r8 = sb("r8", [P, E, E])
        r8b = sb("r8b", [P, E, E])
        wd = sb("wd", [P, B, E])
        wdiag = sb("wdiag", [P, B, E])
        ksf = ksT[:, :, :].rearrange("p h t -> p (h t)")
        x4c = ksf[:, 0:T]
        w2s = ksf[:, T:T + E * C].rearrange("p (e c) -> p e c", e=E)
        fb2s = sb("fb2s", [P, C])
        hf = qT[:, 0:E, :]
        yf = sb("yf", [P, NT, C])
        yo = sb("yo", [P, NT, C])
        tf = sb("tf", [P, NT, C])
        yc = sb("yc", [C, T])

        SA = ctx.enter_context(nc.psum_tensor("SA", [P, 512], F32))
        SB_ = ctx.enter_context(nc.psum_tensor("SB", [P, 512], F32))
        side = [SA, SB_]
        ring = [ctx.enter_context(nc.psum_tensor(f"ring{i}", [P, 512], F32)) for i in range(4)]
        pv = [ctx.enter_context(nc.psum_tensor(f"pv{i}", [P, 512], F32)) for i in range(2)]

        def chain(eng, name, per_round=0, rnd=0):
            count = [0]

            def link(ins):
                count[0] += 1
                ins.then_inc(S(name), 1)
                eng.wait_ge(S(name), rnd * per_round + count[0])
                return ins

            return link, count

        def window(i, dy, dx):
            return img[i][:, dy:dy + H, dx:dx + W]

        DVE_LINKS = 169
        DVE2_LINKS = 11
        PAIRS = HEADS // 2
        PAIR_UNITS = 7
        VALUES = [("v1", 0), ("v1", 1), ("vw", 0), ("vw", 1), ("vs", 0)]
        UNITS = PAIR_UNITS * PAIRS + len(VALUES) + 1

        MAX_PARTS = {"max0": [(0, 0, 0, 0, P), (0, 1, 2 * P, 0, P)], "max1": [(1, 0, 0, 0, T)],
                     "max2": [(0, 2, 0, 0, P), (1, 1, 2 * P, 0, P)], "max3": [(1, 2, 0, T - BAND, BAND)]}

        def unit_order():
            u = 0
            for s in range(PAIRS + 1):
                for kind in ("q", "kw", "ks") if s < PAIRS else ():
                    yield u, kind, s
                    u += 1
                for kind in ("max0", "max1", "max2", "max3") if s else ():
                    yield u, kind, s - 1
                    u += 1
            for kind, t in VALUES:
                yield u, kind, t
                u += 1

        block = ctx.enter_context(nc.Block())

        @block.sync
        def _(sp):
            sp.dma_start(prep, prep_in).then_inc(S("prep"), 16)
            sp.dma_start(early[:, :], early_in).then_inc(S("early"), 16)
            sp.dma_start(late[:, :], late_in).then_inc(S("late"), 16)
            sp.dma_start(masks32, masks_in).then_inc(S("masks"), 16)
            with sp.Fori(0, B) as b:
                sp.wait_ge(S("image_done"), b + 1)
                for half_ in range(2):
                    sp.dma_start(xin[half_ * C:(half_ + 1) * C, :], x_in[b]).then_inc(S("x_loaded"), 16)
            sp.wait_ge(S("image_done"), B + 1)
            sp.dma_start(final, final_in).then_inc(S("final"), 16)
            with sp.Fori(0, B) as b:
                sp.wait_ge(S("y_copied"), b + 1)
                sp.dma_start(y_out[b], yc[:, :]).then_inc(S("y_stored"), 16)
            sp.wait_ge(S("y_stored"), 16 * (B + 1))

        @block.gpsimd
        def _(pool):
            nc.gpsimd.memset(half[:, :], -0.5).then_inc(S("half"), 1)
            pool.wait_ge(S("half"), 1)
            pool.wait_ge(S("bn_var"), 1)
            nc.gpsimd.tensor_tensor(bnc[:, 1:2], bnc[:, 0:1], half[:, :], ALU.pow).then_inc(S("bn_rstd"), 1)
            with pool.Fori(0, B) as b:
                n = pool.snap(b + 1)
                pool.wait_ge(S("image_done"), n)

                def rsqrt(out, in_, ready, done):
                    pool.wait_ge(S(ready), n)
                    shape = in_.shape
                    h = half[:, 0:1]
                    if len(shape) == 3:
                        h = h.unsqueeze(2)
                    nc.gpsimd.tensor_tensor(out, in_, h.broadcast_to(tuple(shape)), ALU.pow)\
                        .then_inc(S(done), 1)

                rsqrt(gt[:, 1:2], gt[:, 0:1], "gn1_var", "gn1_rstd")
                rsqrt(gt[:, 1:2], gt[:, 0:1], "gn2_var", "gn2_rstd")
                rsqrt(gv[:, :], mv[:, :, 1], "ln1_var", "ln1_rstd")
                rsqrt(rs[:, :, :], ms[:, :, :], "rms_var", "rms_rstd")
                for hp in range(PAIRS):
                    for i, (src, dst) in enumerate(((qT, qb), (kwT, kwb), (ksT, ksb))):
                        if hp >= 2:
                            pool.wait_ge(S("max_scores"), b * PAIRS + hp - 1)
                        pool.wait_ge(S("heads_ready"), b * 3 * PAIRS + 3 * hp + i + 1)
                        pool.sem_inc(S("pool_gap"), 1)
                        nc.gpsimd.tensor_copy(dst[:, hp % 2, :, :], src[:, 2 * hp:2 * hp + 2, :])\
                            .then_inc(S("heads_bf16"), 1)
                for g in range(4):
                    pool.wait_ge(S("branch_out"), b * 12 + 3 * g + 3)
                    nc.gpsimd.tensor_tensor(oT[:, g, :], ob[:, g % 2, 0, :], ob[:, g % 2, 1, :], ALU.add)\
                        .then_inc(S("pool_add"), 1)
                    pool.wait_ge(S("pool_add"), b * 4 + g + 1)
                    nc.gpsimd.tensor_tensor(oT[:, g, :], oT[:, g, :], ob[:, g % 2, 2, :], ALU.add)\
                        .then_inc(S("o_summed"), 1)
                rsqrt(gv[:, :], mv[:, :, 1], "ln2_var", "ln2_rstd")
                for t in range(NT):
                    pool.wait_ge(S("y_biased"), b * NT + t + 1)
                    nc.gpsimd.tensor_tensor(yb[:, t, :, :], yb[:, t, :, :],
                                            comb[:, t, :].unsqueeze(2).broadcast_to((P, E, C)), ALU.mult)\
                        .then_inc(S("y_weighted"), 1)
                rsqrt(gv[:, :], mv[:, :, 1], "ln3_var", "ln3_rstd")
                rsqrt(gv[:, :], mv[:, :, 1], "ln4_var", "ln4_rstd")
            with pool.Fori(0, B) as b:
                pool.wait_ge(S("ln5_var"), b + 1)
                nc.gpsimd.tensor_tensor(gv[:, :], mv[:, :, 1], half[:, 0:1].broadcast_to((P, 2)), ALU.pow)\
                    .then_inc(S("ln5_rstd"), 1)

        @block.tensor
        def _(pe):
            pe.wait_ge(S("prep"), 16)
            pe.wait_ge(S("early"), 16)
            pe.wait_ge(S("scaled"), 2)
            for i in range(13):
                bank = ring[i // 4]
                m = pe.matmul(bank[:, (i % 4) * P:(i % 4 + 1) * P],
                              scaled[:, 2 * i:2 * i + 2, :].rearrange("p a c -> p (a c)"), cst("pw_kv"),
                              start=True, stop=True)
            for i in range(13):
                bank = side[i // 8]
                m = pe.matmul(bank[:, (i % 8) * C:(i % 8 + 1) * C],
                              scaled_q[:, 2 * i:2 * i + 2, :].rearrange("p a c -> p (a c)"),
                              cst("pw_q")[0:C, :], start=True, stop=True)
            m.then_inc(S("composed"), 1)
            pe.wait_ge(S("late"), 16)
            for h in range(HEADS):
                m = pe.matmul(pv[0][0:CQ, h * CKV:(h + 1) * CKV], wqn_t[0:NOPE, h, :], wkn_t[0:NOPE, h, :],
                              start=True, stop=True)
            m.then_inc(S("absorbed"), 1)

            with pe.Fori(0, B) as b:
                n = pe.snap(b + 1)

                def after(*names):
                    for name in names:
                        pe.wait_ge(S(name), n)

                def transpose_tok(src, bank, col, done):
                    pe.sem_inc(S("pe_gap"), 1)
                    for t in range(NT):
                        m = pe.transpose(bank[0:C, col + t * P:col + (t + 1) * P], src[:, t, :], ident)
                    m.then_inc(S(done), 1)

                after("image_done")
                after("gn1_stats")
                pe.matmul(SB_[:, 0:2], cst("pairmean"), mv[:, 0, :], start=True, stop=True)\
                    .then_inc(S("gn1_mean"), 1)
                after("gn1_done")
                for i, (copy, dy, dx) in enumerate(PAIRS5):
                    pe.matmul(SA[:, 0:T], wc_kv[:, i, :], window(copy, dy, dx), start=(i == 0), stop=(i == 12))
                pe.matmul(SA[0:C, T:2 * T], cst("w_q0"), window(0, 2, 2), start=True, stop=True)
                for i, (copy, dy, dx) in enumerate(PAIRS5):
                    pe.matmul(SA[C:P, T:2 * T], wc_q[:, i, :], window(copy, dy, dx), start=(i == 0),
                              stop=(i == 12))
                for t in range(NT):
                    m = pe.matmul(SB_[:, t * P:(t + 1) * P], xg[:, t * P:(t + 1) * P], cst("w_kv0"),
                                  start=True, stop=True)
                m.then_inc(S("conv5"), 1)
                after("kv1_copied")
                for t in range(NT):
                    m = pe.transpose(SA[:, t * P:(t + 1) * P], kv1[:, t * P:(t + 1) * P], ident)
                m.then_inc(S("kv1_turned"), 1)
                after("kv_ready")
                for t in range(NT):
                    m = pe.matmul(SB_[:, 0:P + 1], ktok[:, t, :], vtok[:, t, :], start=(t == 0), stop=(t == NT - 1))
                m.then_inc(S("kv_sum"), 1)
                after("kv_masked")
                pe.matmul(SA[:, 0:T], kvm[:, :], q0[:, :], start=True, stop=True)
                pe.matmul(SA[:, T:2 * T], ksm[:, :], q0[:, :], start=True, stop=True).then_inc(S("lin_out"), 1)
                after("o0_ready")
                pe.matmul(SB_[:, 0:T], cst("proj0"), o0[:, :], start=True, stop=True).then_inc(S("proj0"), 1)
                after("gn2_stats")
                pe.matmul(SA[:, 0:2], cst("pairmean"), mv[:, 0, :], start=True, stop=True)\
                    .then_inc(S("gn2_mean"), 1)
                after("gn2_done")
                for i, (copy, dy, dx) in enumerate(PAIRS3):
                    m = pe.matmul(SB_[0:C, 0:T], bin1[:, i, :], window(copy, dy + 1, dx + 1), start=(i == 0),
                                  stop=(i == 4))
                m.then_inc(S("conv3"), 1)
                after("x2")
                pe.sem_inc(S("pe_gap"), 1)
                for t in range(NT):
                    m = pe.transpose(SA[:, t * C:(t + 1) * C], x1[0:C, t * P:(t + 1) * P], ident[0:C, 0:C])
                m.then_inc(S("x2_turned"), 1)
                after("xn1")
                transpose_tok(xn, SA, 0, "xn1_turned")
                after("xnT1")
                for t in range(NT):
                    m = pe.matmul(SB_[:, t * 68:(t + 1) * 68], xnT[:, t * P:(t + 1) * P], cst("w_small"),
                                  start=True, stop=True)
                m.then_inc(S("small"), 1)
                pe.matmul(SA[:, 0:T], cst("w_kr"), xnT[:, :], start=True, stop=True).then_inc(S("k_rope"), 1)
                after("small_copied")
                for t in range(NT):
                    m = pe.matmul(SB_[:, 140:140 + BR], meank[:, :], sm[:, t, 64:64 + BR], start=(t == 0),
                                  stop=(t == NT - 1))
                m.then_inc(S("gate_mean"), 1)
                after("score_bc", "k_rotated")
                for t in range(NT):
                    m = pe.transpose(SA[:, t * P:(t + 1) * P], sbc[:, t, :], ident)
                m.then_inc(S("score_row"), 1)
                after("cn_ready", "gate_read")
                transpose_tok(cn, SB_, T, "cn_turned")
                after("selected")
                pe.matmul(SA[:, 0:1], cst("before"), sel[:, 0:1], start=True, stop=True)
                pe.matmul(SA[:, 1:2], cst("before"), sel[:, 1:2], start=True, stop=False)
                pe.matmul(SA[:, 1:2], meank[:, :], gs[:, 7:8], start=False, stop=True)\
                    .then_inc(S("positions"), 1)
                after("pick_ready")
                for t in range(NT):
                    m = pe.matmul(SA[C:P, 0:P], xn[:, t, :], pickm[:, t, :], start=(t == 0), stop=(t == NT - 1))
                m.then_inc(S("sel_x"), 1)
                after("selT", "cnT", "k1T", "k1b")
                for u, kind, k in unit_order():
                    bank = side[u % 2]
                    if u >= 2:
                        pe.wait_ge(S("unit_free"), b * UNITS + u - 1)
                    if kind in ("q", "kw"):
                        w_, rhs = (w_q, cnT) if kind == "q" else (w_k, xnT)
                        for i in range(2):
                            m = pe.matmul(bank[:, i * T:(i + 1) * T], w_[:, 2 * k + i, :], rhs[:, :],
                                          start=True, stop=True)
                    elif kind == "ks":
                        for i in range(2):
                            m = pe.matmul(bank[:, i * P:(i + 1) * P], w_k[:, 2 * k + i, :], selT[:, :],
                                          start=True, stop=True)
                    elif kind[0] == "v":
                        src = {"v1": cnT, "vw": xnT, "vs": selT}[kind]
                        m = pe.matmul(bank[:, :], src[:, k * P:(k + 1) * P], cst("w_v1" if kind == "v1" else "w_v"), start=True, stop=True)
                    else:
                        if kind == "max0":
                            pe.wait_ge(S("heads_bf16"), b * 3 * PAIRS + 3 * k + 3)
                        for qt, br, at, key0, keys in MAX_PARTS[kind]:
                            for i in range(2):
                                out = bank[:, at + i * keys:at + (i + 1) * keys]
                                rhs = (k1b[:, key0:key0 + keys], ksb[:, k % 2, i, :],
                                       kwb[:, k % 2, i, key0:key0 + keys])[br]
                                m = pe.matmul(out, qb[:, k % 2, i, qt * P:(qt + 1) * P], rhs,
                                              start=True, stop=(br == 1))
                                if br == 0:
                                    m = pe.matmul(out[:, keys - P:keys], identb, cst("causal_s"),
                                                  start=False, stop=True)
                                elif br == 2:
                                    m = pe.matmul(out, identb, cst("band_s" if qt == 0 else "band_s1"),
                                                  start=False, stop=True)
                        if kind == "max3":
                            m.then_inc(S("max_scores"), 1)
                            pe.wait_ge(S("max_scores"), b * PAIRS + k + 1)
                            pe.sem_inc(S("unit_full"), 1)
                            continue
                    m.then_inc(S("unit_full"), 1)
                after("mh_ready")
                assert (UNITS - 1) % 2
                mTp = SB_[:, 0:P].bitcast(BF16)
                pe.wait_ge(S("unit_free"), b * UNITS + UNITS - 2)
                for t in range(NT):
                    m = pe.transpose(mTp[:, t * P:(t + 1) * P], mh[:, t, :], identb)
                m.then_inc(S("unit_full"), 1)
                after("mT")

                def fold(out, br, h, q0_, nq, stop):
                    r = br * HEADS + h
                    return pe.matmul(out, pick[:, r:r + 1].broadcast_to((P, P)), mT[:, q0_:q0_ + nq],
                                     start=False, stop=stop)

                def scores(hp):
                    h0 = 2 * hp
                    for i in range(4):
                        bank = ring[i]
                        if hp:
                            pe.wait_ge(S("exp_done"), b * 32 + 4 * (hp - 1) + i + 1)
                        if i == 0:
                            pe.matmul(bank[:, :], k1T[:, 0:P], qT[:, h0:h0 + 2, :], start=True, stop=False)
                            for j in range(2):
                                fold(bank[:, j * T:(j + 1) * T], 0, h0 + j, 0, T, False)
                                m = pe.matmul(bank[:, j * T:j * T + P], identb, cst("causal_t"), start=False,
                                              stop=(j == 1))
                        elif i == 1:
                            for j in range(2):
                                pe.matmul(bank[:, j * T:(j + 1) * T], ksT[:, h0 + j, :], qT[:, h0 + j, :],
                                          start=True, stop=False)
                                m = fold(bank[:, j * T:(j + 1) * T], 1, h0 + j, 0, T, True)
                        elif i == 2:
                            pe.matmul(bank[:, 0:T], k1T[:, P:T], qT[:, h0:h0 + 2, P:T], start=True, stop=False)
                            for j in range(2):
                                out = bank[:, j * P:(j + 1) * P]
                                fold(out, 0, h0 + j, P, P, False)
                                pe.matmul(out, identb, cst("causal_t"), start=False, stop=(j == 1))
                            for j in range(2):
                                out = bank[:, T + j * P:T + (j + 1) * P]
                                pe.matmul(out, kwT[:, h0 + j, P:T], qT[:, h0 + j, P:T], start=True, stop=False)
                                fold(out, 2, h0 + j, P, P, False)
                                m = pe.matmul(out, identb, cst("band_t"), start=False, stop=True)
                        else:
                            for j in range(2):
                                out = bank[:, j * BAND:(j + 1) * BAND]
                                pe.matmul(out, kwT[:, h0 + j, 0:P], qT[:, h0 + j, 0:BAND], start=True, stop=False)
                                fold(out, 2, h0 + j, 0, BAND, False)
                                m = pe.matmul(out, identb, cst("band_t0"), start=False, stop=True)
                        m.then_inc(S("scores"), 1)

                def weigh(g):
                    pe.wait_ge(S("exp_done"), b * 32 + 8 * (g + 1))
                    for br in range(BR):
                        u = 3 * g + br
                        bank = pv[u % 2]
                        if u >= 2:
                            pe.wait_ge(S("branch_out"), b * 12 + u - 1)
                        for den in range(2):
                            c = T * den

                            def mm(j, cols, vals, probs, start, stop):
                                lhs = onesk[:, :] if den else vals[:, (4 * g + j) * VDIM:(4 * g + j + 1) * VDIM]
                                return pe.matmul(bank[32 * j:32 * j + 32, c + cols[0]:c + cols[1]], lhs, probs,
                                                 start=start, stop=stop)

                            def p_of(j, a, nn):
                                return pr[:, g % 2, j // 2, a:a + nn]

                            if br == 0:
                                for j in range(4):
                                    mm(j, (0, T), v1[:, 0, :], p_of(j, (j % 2) * T, T), True, False)
                                for j in range(4):
                                    m = mm(j, (P, T), v1[:, 1, :], p_of(j, 1024 + (j % 2) * P, P), False, True)
                            elif br == 1:
                                for j in range(4):
                                    m = mm(j, (0, T), vs[:, :], p_of(j, 512 + (j % 2) * T, T), True, True)
                            else:
                                for j in range(4):
                                    mm(j, (P, T), vw[:, 1, :], p_of(j, 1280 + (j % 2) * P, P), True, False)
                                for j in range(4):
                                    mm(j, (P, BAND), vw[:, 0, :], p_of(j, 1536 + (j % 2) * BAND + P, WINDOW),
                                       False, True)
                                for j in range(4):
                                    m = mm(j, (0, P), vw[:, 0, :], p_of(j, 1536 + (j % 2) * BAND, P), True, True)
                        m.then_inc(S("weighed"), 1)

                for g in range(4):
                    scores(2 * g)
                    if g:
                        weigh(g - 1)
                    scores(2 * g + 1)
                weigh(3)
                pe.wait_ge(S("o_summed"), b * 4 + 4)
                for t in range(NT):
                    for g in range(4):
                        m = pe.matmul(SA[:, t * C:(t + 1) * C], oT[:, g, t * P:(t + 1) * P], w_p[:, g, :],
                                      start=(g == 0), stop=(g == 3))
                m.then_inc(S("attn_out"), 1)
                after("xn2")
                transpose_tok(xn, SB_, 0, "xn2_turned")
                after("xnT2")
                for t in range(NT):
                    m = pe.matmul(SA[:, t * E:(t + 1) * E], xnT[:, t * P:(t + 1) * P], cst("r2"),
                                  start=True, stop=True)
                m.then_inc(S("logits"), 1)
                for u in range(2):
                    for i in range(2):
                        m = pe.matmul(ring[u][:, i * T:(i + 1) * T], w1[:, 2 * u + i, :], xnT[:, :],
                                      start=True, stop=True)
                    m.then_inc(S("hidden"), 1)
                after("gelu1")
                for t in range(NT):
                    for i in range(4):
                        m = pe.matmul(ring[2 + t][:, i * P:(i + 1) * P], hm[:, i, t * P:(t + 1) * P], w2[:, i, :],
                                      start=True, stop=True)
                    m.then_inc(S("expert_out"), 1)
                after("xn3")
                transpose_tok(xn, SB_, 0, "xn3_turned")
                after("xnT3")
                pe.matmul(SA[:, 0:T], cst("q3"), xnT[:, :], start=True, stop=True)
                for t in range(NT):
                    m = pe.matmul(SB_[:, t * T:(t + 1) * T], xnT[:, t * P:(t + 1) * P], cst("kv3"),
                                  start=True, stop=True)
                m.then_inc(S("qkv3"), 1)
                after("kv3_normed", "q3_copied")
                kvf = kvq[:, :, :, :].rearrange("p t g d -> p t (g d)")
                for t in range(NT):
                    m = pe.matmul(SA[:, 0:P], kvf[:, t, P:2 * P], kvf[:, t, 0:P], start=(t == 0),
                                  stop=(t == NT - 1))
                m.then_inc(S("dots"), 1)
                after("dots_masked")
                pe.matmul(SA[:, P:P + C], dT[:, :], cst("out3"), start=True, stop=True).then_inc(S("dots_out"), 1)
                after("m3")
                for t in range(NT):
                    m = pe.matmul(SB_[:, t * C:(t + 1) * C], q3[:, t * P:(t + 1) * P], m3[:, :],
                                  start=True, stop=True)
                m.then_inc(S("attn3"), 1)
                after("xn4")
                for t in range(NT):
                    m = pe.matmul(SA[0:C, 200:201], x4[:, t, :], meank[:, 0:1], start=(t == 0), stop=(t == NT - 1))
                m.then_inc(S("token_mean"), 1)

            pe.wait_ge(S("final"), 16)
            pe.wait_ge(S("image_done"), B + 1)
            pe.matmul(SB_[0:B, 0:E], xbar[:, :], cst("r3"), start=True, stop=True).then_inc(S("route_logits"), 1)
            pe.wait_ge(S("route1"), 1)
            pe.matmul(SB_[0:B, 16:16 + E], meank[0:B, 0:B], rw[0:B, :], start=True, stop=True)\
                .then_inc(S("route_load"), 1)
            pe.wait_ge(S("route2"), 1)
            pe.matmul(SA[:, 0:B * E], meank[:, :], wdiag[:, :, :].rearrange("p b e -> p (b e)"),
                      start=True, stop=True).then_inc(S("route_bc"), 1)

            with pe.Fori(0, B) as b:
                n = pe.snap(b + 1)
                pe.wait_ge(S("x4_fetched"), n)
                pe.sem_inc(S("pe_gap"), 1)
                for t in range(NT):
                    m = pe.transpose(SA[0:C, T + t * P:T + (t + 1) * P], x4[:, t, :], ident)
                m.then_inc(S("x4_turned"), 1)
                pe.wait_ge(S("x4c"), n)
                pe.wait_ge(S("f_in"), n)
                for e in range(E):
                    bank = ring[e // 2]
                    m = pe.matmul(bank[:, (e % 2) * T:(e % 2 + 1) * T], f1[:, e, :], x4c[:, :],
                                  start=True, stop=True)
                    if e % 2:
                        m.then_inc(S("f_hidden"), 1)
                pe.wait_ge(S("f_gelu"), b * E + E)
                for t in range(NT):
                    for e in range(E):
                        m = pe.matmul(SB_[:, t * C:(t + 1) * C], hf[:, e, t * P:(t + 1) * P], w2s[:, e, :],
                                      start=(e == 0), stop=False)
                    m = pe.matmul(SB_[:, t * C:(t + 1) * C], meank[:, :], fb2s[:, :], start=False, stop=True)
                m.then_inc(S("f_out"), 1)
                pe.wait_ge(S("tf_ready"), n)
                pe.sem_inc(S("pe_gap"), 1)
                for t in range(NT):
                    m = pe.transpose(SA[0:C, t * P:(t + 1) * P], tf[:, t, :], ident)
                m.then_inc(S("f_turned"), 1)

        @block.scalar
        def _(act):
            with act.Fori(0, B) as b:
                n = act.snap(b + 1)

                def after(*names):
                    for name in names:
                        act.wait_ge(S(name), n)

                after("image_done")
                after("conv5")
                kv_tok = lambda bank, c: bank[:, 0:T].rearrange("p (t c) -> p t c", t=NT)[:, :, c:c + C]
                act.activation(ktok[:, :, 0:C], kv_tok(SB_, 0), ACT.Relu)
                act.activation(vtok[:, :, 0:C], kv_tok(SB_, C), ACT.Copy)
                after("kv1_turned")
                act.activation(ktok[:, :, C:P], kv_tok(SA, 0), ACT.Relu)
                act.activation(vtok[:, :, C:P], kv_tok(SA, C), ACT.Copy).then_inc(S("kv_ready"), 1)
                after("xn1_turned")
                act.activation(xnT[0:C, :], SA[0:C, 0:T], ACT.Copy).then_inc(S("xnT1"), 1)
                after("cn_turned")
                act.activation(cnT[0:C, :], SB_[0:C, T:2 * T], ACT.Copy, scale=cst("nw")[0:C, :])\
                    .then_inc(S("cnT"), 1)
                after("gate_max")
                act.activation(gs[:, 0:BR], gl[:, :], ACT.Exp, bias=gs[:, 4:5]).then_inc(S("gate_exp"), 1)
                after("sel_x")
                act.activation(selT[C:P, :], SA[C:P, 0:P], ACT.Copy).then_inc(S("selT"), 1)
                for u, kind, k in unit_order():
                    if kind[0] != "v":
                        continue
                    act.wait_ge(S("unit_full"), b * UNITS + u + 1)
                    act.wait_ge(S("unit_free"), b * UNITS + u)
                    dst = {"v1": v1[:, k, :], "vw": vw[:, k, :], "vs": vs[:, :]}[kind]
                    act.activation(dst, side[u % 2][:, :], ACT.Copy).then_inc(S("unit_free"), 1)
                act.wait_ge(S("unit_full"), b * UNITS + UNITS)
                act.activation(mT[:, :], SB_[:, 0:P].bitcast(BF16), ACT.Copy).then_inc(S("mT"), 1)
                act.wait_ge(S("mT"), n)
                act.sem_inc(S("unit_free"), 1)
                for hp in range(8):
                    g = hp // 2
                    if hp % 2 == 0 and g >= 2:
                        act.wait_ge(S("weighed"), b * 12 + 3 * (g - 1))
                    for i in range(4):
                        w = 2 * BAND if i == 3 else 512
                        act.wait_ge(S("scores"), b * 32 + 4 * hp + i + 1)
                        act.activation(pr[:, g % 2, hp % 2, 512 * i:512 * i + w], ring[i][:, 0:w], ACT.Exp,
                                       scale=SCALE).then_inc(S("exp_done"), 1)
                after("xn2_turned")
                act.activation(xnT[0:C, :], SB_[0:C, 0:T], ACT.Copy).then_inc(S("xnT2"), 1)
                after("logit_max")
                for t in range(NT):
                    a = act.activation(pe8[:, t, :], SA[:, t * E:(t + 1) * E], ACT.Exp, bias=c8[:, t, 1:2],
                                       accum_out=c8[:, t, 2:3])
                    a.then_inc(S("logit_exp"), 1)
                for u in range(2):
                    act.wait_ge(S("hidden"), b * 2 + u + 1)
                    for i in range(2):
                        a = act.activation(hm[:, 2 * u + i, :], ring[u][:, i * T:(i + 1) * T], ACT.Gelu,
                                           bias=cst("b1")[:, 2 * u + i:2 * u + i + 1])
                a.then_inc(S("gelu1"), 1)
                after("xn3_turned")
                act.activation(xnT[0:C, :], SB_[0:C, 0:T], ACT.Copy).then_inc(S("xnT3"), 1)
                after("qkv3")
                act.activation(q3[:, :], SA[:, 0:T], ACT.Copy).then_inc(S("q3_copied"), 1)
                after("n3_var")
                act.activation(n3[:, 2, :], n3[:, 1, :], ACT.Sqrt).then_inc(S("n3_std"), 1)
                after("token_mean")
                act.activation(xbar[0:C, bass.ds(b, 1)], SA[0:C, 200:201], ACT.Copy).then_inc(S("xbar_kept"), 1)

            act.wait_ge(S("final"), 16)
            act.wait_ge(S("route_max"), 1)
            act.activation(rw[0:B, :], lr[0:B, :], ACT.Exp, bias=rt[0:B, 1:2], accum_out=rt[0:B, 2:3])\
                .then_inc(S("route_exp"), 1)
            act.wait_ge(S("route_max"), 2)
            act.activation(lr[0:B, :], rw[0:B, :], ACT.Exp, bias=rt[0:B, 5:6], accum_out=rt[0:B, 6:7])\
                .then_inc(S("route_exp"), 1)
            act.wait_ge(S("route_max"), 3)
            act.activation(rw[0:B, :], lr[0:B, :], ACT.Exp, bias=rt[0:B, 9:10]).then_inc(S("route_exp"), 1)

            act.sem_inc(S("y_stored"), 16)
            with act.Fori(0, B) as b:
                n = act.snap(b + 1)
                act.wait_ge(S("x4_turned"), n)
                act.activation(x4c[0:C, :], SA[0:C, T:2 * T], ACT.Copy).then_inc(S("x4c"), 1)
                for e in range(E):
                    if e % 2 == 0:
                        act.wait_ge(S("f_hidden"), b * 4 + e // 2 + 1)
                    act.activation(hf[:, e, :], ring[e // 2][:, (e % 2) * T:(e % 2 + 1) * T], ACT.Gelu,
                                   bias=cst("fb1")[:, e:e + 1]).then_inc(S("f_gelu"), 1)
                act.wait_ge(S("f_turned"), n)
                act.wait_ge(S("y_stored"), b * 16 + 16)
                act.activation(yc[:, :], SA[0:C, 0:T], ACT.Copy).then_inc(S("y_copied"), 1)

        @block.vector
        def _(dve):
            V = nc.vector
            link, count = chain(dve, "dve_prep")
            for tile in (img[0], img[1], xnT, cnT, selT, cn, k1T, xbar, mh, wdiag, fb2s, gs, q0, den0):
                ap = tile[:] if len(tile.shape) == 2 else tile[:]
                V.memset(ap, 0.0)
            V.memset(onesk[:, :], 1.0)
            V.memset(meank[:, :], 1.0 / T)
            link(V.memset(vtok[:, :, P:P + 1], 1.0))
            dve.wait_ge(S("prep"), 16)
            dve.wait_ge(S("early"), 16)
            V.tensor_tensor(scaled[:, :, :], cst("wi_kv").unsqueeze(1).broadcast_to((P, 26, C)),
                            dw_kv.unsqueeze(2).broadcast_to((P, 26, C)), ALU.mult).then_inc(S("scaled"), 1)
            V.tensor_tensor(scaled_q[:, :, :], cst("wi_q")[0:C, :].unsqueeze(1).broadcast_to((C, 26, C)),
                            dw_q[0:C, :].unsqueeze(2).broadcast_to((C, 26, C)), ALU.mult)\
                .then_inc(S("scaled"), 1)
            link(V.tensor_scalar(bin1[:, :, :], conv1, 0.0, None, ALU.is_gt))
            link(V.tensor_scalar(binn[:, :, :], conv1, 0.0, None, ALU.is_lt))
            link(V.tensor_tensor(bin1[:, :, :], bin1[:, :, :], binn[:, :, :], ALU.subtract))
            bn = cst("bn")
            V.tensor_scalar(bnc[:, 0:1], bn[:, 3:4], 1e-5, None, ALU.add).then_inc(S("bn_var"), 1)
            dve.wait_ge(S("bn_rstd"), 1)
            link(V.tensor_tensor(bnc[:, 2:3], bn[:, 0:1], bnc[:, 1:2], ALU.mult))
            link(V.tensor_tensor(bnc[:, 3:4], bn[:, 2:3], bnc[:, 2:3], ALU.mult))
            link(V.tensor_tensor(bnc[:, 3:4], bn[:, 1:2], bnc[:, 3:4], ALU.subtract))
            dve.wait_ge(S("composed"), 1)
            for i in range(4):
                k = min(4, 13 - 4 * i)
                V.tensor_copy(wc_kv[:, 4 * i:4 * i + k, :],
                              ring[i][:, 0:k * P].rearrange("p (n m) -> p n m", n=k))
            V.tensor_copy(wc_q[:, 0:8, :], SA[:, :].rearrange("p (n m) -> p n m", n=8))
            link(V.tensor_copy(wc_q[:, 8:13, :], SB_[:, 0:5 * C].rearrange("p (n m) -> p n m", n=5)))
            dve.wait_ge(S("absorbed"), 1)
            link(V.tensor_copy(w_q[0:CQ, :, NOPE:2 * NOPE],
                               pv[0][0:CQ, :].rearrange("p (h m) -> p h m", h=HEADS)))
            link(V.tensor_scalar(cst("w_kr"), cst("w_kr"), 1.0 / HEADS, None, ALU.mult))
            dve.wait_ge(S("masks"), 16)
            link(V.tensor_copy(masks[:, :], masks32))
            dve.sem_inc(S("image_done"), 1)

            with dve.Fori(0, B) as b:
                n = dve.snap(b + 1)
                link, count = chain(dve, "dve_chain", DVE_LINKS, b)

                def after(*names):
                    for name in names:
                        dve.wait_ge(S(name), n)

                def group_norm(x, which):
                    link(V.bn_stats(st[:, 0, :], x[:, :]))
                    dve.sem_inc(S("dve_gap"), 1)
                    link(V.bn_aggr(mv[:, 0, :], st[:, 0, :]))
                    V.scalar_tensor_tensor(out=mv[:, 0, 1:2], in0=mv[:, 0, 0:1], scalar=mv[:, 0, 0:1],
                                           in1=mv[:, 0, 1:2], op0=ALU.mult, op1=ALU.add)\
                        .then_inc(S(f"gn{which}_stats"), 1)
                    after(f"gn{which}_mean")
                    link(V.tensor_copy(gm[:, :], (SB_ if which == 1 else SA)[:, 0:2]))
                    link(V.scalar_tensor_tensor(out=gt[:, 0:1], in0=gm[:, 0:1], scalar=gm[:, 0:1],
                                                in1=gm[:, 1:2], op0=ALU.mult, op1=ALU.subtract))
                    V.tensor_scalar(gt[:, 0:1], gt[:, 0:1], -1.0, 1e-5, ALU.mult, ALU.add)\
                        .then_inc(S(f"gn{which}_var"), 1)
                    after(f"gn{which}_rstd")
                    xv = x[:, :].rearrange("p (h w) -> p h w", h=H)
                    for i in range(2):
                        for up in range(2):
                            dy, dx = (2, 2) if not up else (2, 1) if i == 0 else (1, 2)
                            r = slice(C * up, C * up + C)
                            last = V.tensor_scalar(img[i][r, dy:dy + H, dx:dx + W], xv[r], gm[r, 0:1], gt[r, 1:2],
                                                   ALU.subtract, ALU.mult)
                    link(last)
                    if which == 1:
                        link(V.tensor_scalar(xg[:, :], x[:, :], gm[:, 0:1], gt[:, 1:2], ALU.subtract, ALU.mult))

                def layer_norm(t, out, which, done):
                    for i in range(NT):
                        link(V.bn_stats(st[:, i, :], t[:, i, :]))
                    dve.sem_inc(S("dve_gap"), 1)
                    for i in range(NT):
                        a = (V.bn_aggr(mv[:, i, :], st[:, i, :]))
                    link(a)
                    V.tensor_scalar(mv[:, :, 1], mv[:, :, 1], 1e-5, None, ALU.add)\
                        .then_inc(S(f"ln{which}_var"), 1)
                    after(f"ln{which}_rstd")
                    for i in range(NT):
                        a = V.tensor_scalar(out[:, i, :], t[:, i, :], mv[:, i, 0:1], gv[:, i:i + 1],
                                            ALU.subtract, ALU.mult)
                    link(a)
                    dve.sem_inc(S(done), 1)

                after("image_done")
                dve.wait_ge(S("x_loaded"), b * 32 + 32)
                group_norm(xin, 1)
                dve.sem_inc(S("gn1_done"), 1)
                link(V.tensor_scalar(xs[:, :], xin[:, :], bnc[:, 3:4], None, ALU.add))
                after("conv5")
                link(V.tensor_scalar(q0[:, :], SA[:, T:2 * T], 0.0, None, ALU.max))
                V.tensor_copy(kv1[:, :], SA[:, 0:T]).then_inc(S("kv1_copied"), 1)
                after("kv_sum")
                V.tensor_tensor(kvm[:, :], SB_[:, 0:P], cst("blk8"), ALU.mult)
                V.tensor_scalar(ksm[:, :], cst("blk8"), SB_[:, P:P + 1], None, ALU.mult)\
                    .then_inc(S("kv_masked"), 1)
                after("lin_out")
                link(V.tensor_scalar(den0[:, :], SA[:, T:2 * T], 1e-15, None, ALU.add))
                link(V.reciprocal(rec0[:, :], den0[:, :]))
                V.tensor_tensor(o0[:, :], SA[:, 0:T], rec0[:, :], ALU.mult).then_inc(S("o0_ready"), 1)
                after("proj0")
                link(V.scalar_tensor_tensor(out=x1[:, :], in0=SB_[:, 0:T], scalar=bnc[:, 2:3], in1=xs[:, :],
                                            op0=ALU.mult, op1=ALU.add))
                group_norm(x1, 2)
                dve.sem_inc(S("gn2_done"), 1)
                after("conv3")
                V.tensor_tensor(x1[0:C, :], SB_[0:C, 0:T], x1[0:C, :], ALU.add).then_inc(S("x2"), 1)
                after("x2_turned")
                link(V.tensor_copy(t1[:, :, :], SA[:, 0:NT * C].rearrange("p (t c) -> p t c", t=NT)))
                layer_norm(t1, xn, 1, "xn1")
                after("small")
                link(V.tensor_copy(sm[:, :, :], SB_[:, 0:NT * 68].rearrange("p (t c) -> p t c", t=NT)))
                dve.sem_inc(S("small_copied"), 1)
                after("k_rope")
                V.tensor_tensor(k1T[C:P, :], SA[C:P, 0:T], cst("ktab")[C:P, :], ALU.mult)\
                    .then_inc(S("k_rotated"), 1)
                for t in range(NT):
                    a = V.tensor_copy(sbc[:, t, :], sm[:, t, 67:68].broadcast_to((P, P)))
                a.then_inc(S("score_bc"), 1)
                link(V.tensor_tensor(sq[:, :, :], sm[:, :, 0:64], sm[:, :, 0:64], ALU.mult))
                V.tensor_reduce(ms[:, 0, :], sq[:, :, 0:CQ], AX.X, ALU.add)
                link(V.tensor_reduce(ms[:, 1, :], sq[:, :, 32:32 + CKV], AX.X, ALU.add))
                V.tensor_scalar(ms[:, 0, :], ms[:, 0, :], 1.0 / CQ, 1e-6, ALU.mult, ALU.add)
                V.tensor_scalar(ms[:, 1, :], ms[:, 1, :], 1.0 / CKV, 1e-6, ALU.mult, ALU.add)\
                    .then_inc(S("rms_var"), 1)
                after("rms_rstd")
                V.tensor_tensor(cn[:, :, 0:CQ], sm[:, :, 0:CQ], rs[:, 0, :].unsqueeze(2).broadcast_to((P, NT, CQ)),
                                ALU.mult)
                V.tensor_tensor(cn[:, :, 32:64], sm[:, :, 32:64],
                                rs[:, 1, :].unsqueeze(2).broadcast_to((P, NT, CKV)), ALU.mult)\
                    .then_inc(S("cn_ready"), 1)
                after("gate_mean")
                link(V.tensor_copy(gl[:, :], SB_[:, 140:140 + BR]))
                dve.sem_inc(S("gate_read"), 1)
                link(V.tensor_reduce(gs[:, 3:4], gl[:, :], AX.X, ALU.max))
                V.tensor_scalar(gs[:, 4:5], gs[:, 3:4], -1.0, None, ALU.mult).then_inc(S("gate_max"), 1)
                after("gate_exp")
                link(V.tensor_reduce(gs[:, 5:6], gs[:, 0:BR], AX.X, ALU.add))
                link(V.reciprocal(gs[:, 6:7], gs[:, 5:6]))
                link(V.tensor_scalar(gate[:, :], gs[:, 0:BR], gs[:, 6:7], None, ALU.mult))
                after("score_row")
                link(V.tensor_copy(srow[:, :], SA[:, 0:T]))
                for t in range(NT):
                    link(V.tensor_scalar(cmp_[:, :], srow[:, :], sm[:, t, 67:68], None, ALU.is_gt))
                    link(V.tensor_reduce(rank[:, 0:1], cmp_[:, :], AX.X, ALU.add))
                    link(V.scalar_tensor_tensor(out=cmp_[:, :], in0=srow[:, :], scalar=sm[:, t, 67:68],
                                                in1=ties[:, t, :], op0=ALU.is_equal, op1=ALU.mult))
                    link(V.tensor_reduce(rank[:, 1:2], cmp_[:, :], AX.X, ALU.add))
                    link(V.tensor_tensor(ranks[:, t:t + 1], rank[:, 0:1], rank[:, 1:2], ALU.add))
                link(V.tensor_scalar(sel[:, :], ranks[:, :], float(KEEP), None, ALU.is_lt))
                V.tensor_scalar(gs[:, 7:8], sel[:, 0:1], float(T), None, ALU.mult).then_inc(S("selected"), 1)
                after("positions")
                link(V.tensor_copy(pos[:, :], SA[:, 0:2]))
                for t in range(NT):
                    a = V.tensor_scalar(pickm[:, t, :], cst("iota"), pos[:, t:t + 1], sel[:, t:t + 1],
                                        ALU.is_equal, ALU.mult)
                a.then_inc(S("pick_ready"), 1)
                after("cnT", "k_rotated")
                link(V.tensor_copy(k1T[32:64, :], cnT[32:64, :]))
                dve.sem_inc(S("k1T"), 1)
                link(V.tensor_copy(k1b[:, :], k1T[:, :]))
                dve.sem_inc(S("k1b"), 1)
                mxb = mx[:, :, :].rearrange("p t (r h) -> p t r h", r=BR)
                for u, kind, k in unit_order():
                    if kind[0] == "v":
                        continue
                    dve.wait_ge(S("unit_full"), b * UNITS + u + 1)
                    bank = side[u % 2]
                    if kind in ("q", "kw", "ks"):
                        dst, tab, w_ = {"q": (qT, "qtab", T), "kw": (kwT, "ktab", T), "ks": (ksT, "ktab", P)}[kind]
                        link(V.tensor_tensor(dst[:, 2 * k:2 * k + 2, :],
                                             bank[:, 0:2 * w_].rearrange("p (h t) -> p h t", h=2),
                                             cst(tab)[:, 0:w_].unsqueeze(1).broadcast_to((P, 2, w_)), ALU.mult))
                        dve.sem_inc(S("heads_ready"), 1)
                    else:
                        for qt, br, at, key0, keys in MAX_PARTS[kind]:
                            link(V.tensor_reduce(mxb[:, qt, br, 2 * k:2 * k + 2],
                                                 bank[:, at:at + 2 * keys].rearrange("p (h t) -> p h t", h=2),
                                                 AX.X, ALU.max))
                    dve.sem_inc(S("unit_free"), 1)
                link(V.tensor_scalar(mh[:, :, 0:HB], mx[:, :, :], -1.0, None, ALU.mult))
                V.scalar_tensor_tensor(out=mh[:, :, HB:2 * HB], in0=mx[:, :, :], scalar=-1.0, in1=mh[:, :, 0:HB],
                                       op0=ALU.mult, op1=ALU.subtract).then_inc(S("mh_ready"), 1)
                for u in range(12):
                    g, br = u // 3, u % 3
                    dve.wait_ge(S("weighed"), b * 12 + u + 1)
                    if g >= 2 and br == 0:
                        dve.wait_ge(S("o_summed"), b * 4 + g - 1)
                    link(V.reciprocal(rden[:, u % 2, :], pv[u % 2][:, T:2 * T]))
                    V.scalar_tensor_tensor(out=ob[:, g % 2, br, :], in0=pv[u % 2][:, 0:T],
                                           scalar=gate[:, br:br + 1], in1=rden[:, u % 2, :],
                                           op0=ALU.mult, op1=ALU.mult).then_inc(S("branch_out"), 1)
                after("attn_out")
                link(V.tensor_tensor(t2[:, :, :], SA[:, 0:NT * C].rearrange("p (t c) -> p t c", t=NT),
                                     t1[:, :, :], ALU.add))
                layer_norm(t2, xn, 2, "xn2")
                after("logits")
                link(V.tensor_reduce(c8[:, :, 0], SA[:, 0:NT * E].rearrange("p (t e) -> p t e", t=NT),
                                     AX.X, ALU.max))
                V.tensor_scalar(c8[:, :, 1], c8[:, :, 0], -1.0, None, ALU.mult).then_inc(S("logit_max"), 1)
                dve.wait_ge(S("logit_exp"), b * 2 + 2)
                link(V.reciprocal(c8[:, :, 3], c8[:, :, 2]))
                link(V.tensor_tensor(pe8[:, :, :], pe8[:, :, :], c8[:, :, 3:4].broadcast_to((P, NT, E)), ALU.mult))
                for t in range(NT):
                    p_e = pe8[:, t, :].unsqueeze(2).broadcast_to((P, E, E))
                    p_j = pe8[:, t, :].unsqueeze(1).broadcast_to((P, E, E))
                    V.tensor_tensor(cg[:, t, :, :], p_j, p_e, ALU.is_gt)
                    link(V.tensor_tensor(ce[:, t, :, :], p_j, p_e, ALU.is_equal))
                    link(V.tensor_tensor(ce[:, t, :, :], ce[:, t, :, :], first8, ALU.mult))
                    link(V.tensor_tensor(cg[:, t, :, :], cg[:, t, :, :], ce[:, t, :, :], ALU.add))
                link(V.tensor_reduce(comb[:, :, :], cg[:, :, :, :], AX.X, ALU.add))
                link(V.scalar_tensor_tensor(out=comb[:, :, :], in0=comb[:, :, :], scalar=2.0, in1=pe8[:, :, :],
                                            op0=ALU.is_lt, op1=ALU.mult))
                link(V.tensor_reduce(c8[:, :, 4], comb[:, :, :], AX.X, ALU.add))
                link(V.tensor_scalar(c8[:, :, 5], c8[:, :, 4], 1e-12, None, ALU.max))
                link(V.reciprocal(c8[:, :, 6], c8[:, :, 5]))
                link(V.tensor_tensor(comb[:, :, :], comb[:, :, :], c8[:, :, 6:7].broadcast_to((P, NT, E)), ALU.mult))
                for t in range(NT):
                    dve.wait_ge(S("expert_out"), b * 2 + t + 1)
                    V.tensor_tensor(yb[:, t, :, :].rearrange("p e c -> p (e c)"), ring[2 + t][:, :], cst("b2"),
                                    ALU.add).then_inc(S("y_biased"), 1)
                link(V.tensor_tensor(t2[:, :, :], t2[:, :, :], xn[:, :, :], ALU.add))
                dve.wait_ge(S("y_weighted"), b * 2 + 2)
                for t in range(NT):
                    a = V.tensor_reduce(ysum[:, t, :], yb[:, t, :, :].rearrange("p e c -> p c e"), AX.X, ALU.add)
                link(a)
                link(V.tensor_tensor(t3[:, :, :], t2[:, :, :], ysum[:, :, :], ALU.add))
                layer_norm(t3, xn, 3, "xn3")
                after("qkv3")
                kvp = SB_[:, :].rearrange("p (g d) -> p g d", d=16)
                k3 = kv3[:, :, :, :].rearrange("p t g d -> p (t g) d")
                kq = kvq[:, :, :, :].rearrange("p t g d -> p (t g) d")
                bc = lambda i: n3[:, i, :].unsqueeze(2).broadcast_to((P, NT * 16, 16))
                link(V.tensor_reduce(n3[:, 0, :], kvp, AX.X, ALU.add))
                link(V.tensor_scalar(n3[:, 0, :], n3[:, 0, :], 1.0 / 16, None, ALU.mult))
                link(V.tensor_tensor(k3, kvp, bc(0), ALU.subtract))
                link(V.tensor_tensor(kq, k3, k3, ALU.mult))
                link(V.tensor_reduce(n3[:, 1, :], kq, AX.X, ALU.add))
                V.tensor_scalar(n3[:, 1, :], n3[:, 1, :], 1.0 / 16, 1e-5, ALU.mult, ALU.add)\
                    .then_inc(S("n3_var"), 1)
                after("n3_std")
                link(V.reciprocal(n3[:, 3, :], n3[:, 2, :]))
                V.tensor_tensor(kq, k3, bc(3), ALU.mult).then_inc(S("kv3_normed"), 1)
                after("dots")
                V.tensor_tensor(dT[:, :], SA[:, 0:P], cst("blk16"), ALU.mult).then_inc(S("dots_masked"), 1)
                after("dots_out")
                V.tensor_copy(m3[:, :], SA[:, P:P + C]).then_inc(S("m3"), 1)
                link(V.tensor_tensor(t3[:, :, :], t3[:, :, :], cst("bout").unsqueeze(1).broadcast_to((P, NT, C)),
                                     ALU.add))
                after("attn3")
                link(V.tensor_tensor(t4[:, :, :], SB_[:, 0:NT * C].rearrange("p (t c) -> p t c", t=NT),
                                     t3[:, :, :], ALU.add))
                layer_norm(t4, x4, 4, "xn4")
                V.tensor_copy(all_t4[:, b, :, :], t4[:, :, :])
                link(V.tensor_copy(all_x4[:, b, :, :], x4[:, :, :]))
                after("xbar_kept")
                dve.sem_inc(S("image_done"), 1)
                assert count[0] == DVE_LINKS, count[0]

            dve.wait_ge(S("final"), 16)
            V.memset(x4c, 0.0)
            link, count = chain(dve, "dve_route")
            R = slice(0, B)
            dve.wait_ge(S("route_logits"), 1)
            link(V.tensor_tensor(lr[R, :], SB_[R, 0:E], cst("br3")[R, :], ALU.add))
            link(V.tensor_reduce(rt[R, 0:1], lr[R, :], AX.X, ALU.max))
            V.tensor_scalar(rt[R, 1:2], rt[R, 0:1], -1.0, None, ALU.mult).then_inc(S("route_max"), 1)
            dve.wait_ge(S("route_exp"), 1)
            link(V.reciprocal(rt[R, 3:4], rt[R, 2:3]))
            V.tensor_scalar(rw[R, :], rw[R, :], rt[R, 3:4], None, ALU.mult).then_inc(S("route1"), 1)
            dve.wait_ge(S("route_load"), 1)
            capacity = float(-(-B * T * 5 // (4 * E)))
            link(V.tensor_scalar(load[R, :], SB_[R, 16:16 + E], float(T) * T, None, ALU.mult))
            link(V.tensor_scalar(r8[R, 0, :], load[R, :], capacity, None, ALU.max))
            link(V.reciprocal(r8[R, 1, :], r8[R, 0, :]))
            link(V.scalar_tensor_tensor(out=rw[R, :], in0=rw[R, :], scalar=capacity, in1=r8[R, 1, :],
                                        op0=ALU.mult, op1=ALU.mult))
            link(V.tensor_reduce(rt[R, 4:5], rw[R, :], AX.X, ALU.max))
            V.tensor_scalar(rt[R, 5:6], rt[R, 4:5], -1.0, None, ALU.mult).then_inc(S("route_max"), 1)
            dve.wait_ge(S("route_exp"), 2)
            link(V.reciprocal(rt[R, 7:8], rt[R, 6:7]))
            link(V.tensor_scalar(lr[R, :], lr[R, :], rt[R, 7:8], None, ALU.mult))
            p_e = lr[R, :].unsqueeze(2).broadcast_to((B, E, E))
            p_j = lr[R, :].unsqueeze(1).broadcast_to((B, E, E))
            V.tensor_tensor(r8[R], p_j, p_e, ALU.is_gt)
            link(V.tensor_tensor(r8b[R], p_j, p_e, ALU.is_equal))
            link(V.tensor_tensor(r8b[R], r8b[R], first8[R], ALU.mult))
            link(V.tensor_tensor(r8[R], r8[R], r8b[R], ALU.add))
            link(V.tensor_reduce(load[R, :], r8[R], AX.X, ALU.add))
            link(V.tensor_scalar(load[R, :], load[R, :], 2.0, None, ALU.is_lt))
            link(V.tensor_reduce(rt[R, 8:9], lr[R, :], AX.X, ALU.max))
            V.tensor_scalar(rt[R, 9:10], rt[R, 8:9], -1.0, None, ALU.mult).then_inc(S("route_max"), 1)
            dve.wait_ge(S("route_exp"), 3)
            link(V.tensor_tensor(rw[R, :], rw[R, :], load[R, :], ALU.mult))
            link(V.tensor_reduce(rt[R, 10:11], rw[R, :], AX.X, ALU.add))
            link(V.reciprocal(rt[R, 11:12], rt[R, 10:11]))
            link(V.tensor_scalar(rw[R, :], rw[R, :], rt[R, 11:12], float(T), ALU.mult, ALU.mult))
            V.tensor_tensor(wdiag[R], rw[R, :].unsqueeze(1).broadcast_to((B, B, E)),
                            ident[R, 0:B].unsqueeze(2).broadcast_to((B, B, E)), ALU.mult).then_inc(S("route2"), 1)
            dve.wait_ge(S("route_bc"), 1)
            link(V.tensor_copy(wd[:, :, :], SA[:, 0:B * E].rearrange("p (b e) -> p b e", b=B)))

            with dve.Fori(0, B) as b:
                n = dve.snap(b + 1)
                link, count = chain(dve, "dve_chain2", DVE2_LINKS, b)
                V.tensor_copy(x4[:, :, :], all_x4[:, b, :, :]).then_inc(S("x4_fetched"), 1)
                link(V.tensor_copy(c8[:, 0, :], wd[:, b, :]))
                V.tensor_tensor(w2s[:, :, :], f2, c8[:, 0, :].unsqueeze(2).broadcast_to((P, E, C)), ALU.mult)
                link(V.tensor_tensor(c8[0:E, 1, :], c8[0:E, 0, :], ident[0:E, 0:E], ALU.mult))
                link(V.tensor_reduce(rt[0:E, 0:1], c8[0:E, 1, :], AX.X, ALU.add))
                link(V.tensor_scalar(fb2s[0:E, :], cst("fb2")[0:E, :], rt[0:E, 0:1], float(T), ALU.mult, ALU.mult))
                dve.sem_inc(S("f_in"), 1)
                dve.wait_ge(S("f_out"), n)
                link(V.tensor_tensor(yf[:, :, :], SB_[:, 0:NT * C].rearrange("p (t c) -> p t c", t=NT),
                                     all_x4[:, b, :, :], ALU.add))
                for i in range(NT):
                    link(V.bn_stats(st[:, i, :], yf[:, i, :]))
                dve.sem_inc(S("dve_gap"), 1)
                for i in range(NT):
                    a = V.bn_aggr(mv[:, i, :], st[:, i, :])
                link(a)
                V.tensor_scalar(mv[:, :, 1], mv[:, :, 1], 1e-5, None, ALU.add).then_inc(S("ln5_var"), 1)
                dve.wait_ge(S("ln5_rstd"), n)
                for i in range(NT):
                    a = V.tensor_scalar(yo[:, i, :], yf[:, i, :], mv[:, i, 0:1], gv[:, i:i + 1],
                                        ALU.subtract, ALU.mult)
                link(a)
                link(V.tensor_tensor(yo[:, :, :], yo[:, :, :], cst("gamma").unsqueeze(1).broadcast_to((P, NT, C)),
                                     ALU.mult))
                link(V.tensor_tensor(yo[:, :, :], yo[:, :, :], cst("beta").unsqueeze(1).broadcast_to((P, NT, C)),
                                     ALU.add))
                V.tensor_tensor(tf[:, :, :], yo[:, :, :], all_t4[:, b, :, :], ALU.add).then_inc(S("tf_ready"), 1)
                dve.wait_ge(S("y_copied"), n)
                assert count[0] == DVE2_LINKS, count[0]


def _shape_constants():
    f = np.float32
    i, j = np.arange(P)[:, None], np.arange(P)[None, :]
    k = {}
    k["ident"] = (i == j).astype(f)
    k["pairmean"] = 0.5 * (i // 2 == j // 2).astype(f)
    k["blk8"] = (i // 8 == j // 8).astype(f)
    k["blk16"] = (i // 16 == j // 16).astype(f) / T
    k["before"] = (i < j).astype(f)
    k["iota"] = np.broadcast_to(j, (P, P)).astype(f)
    key = np.arange(T)[None, :]
    k["ties"] = np.concatenate([(key < i + P * t).astype(f) for t in range(NT)], 1)
    e = np.arange(E)
    k["first8"] = np.broadcast_to((e[None, :] < e[:, None]).astype(f).reshape(1, E * E), (P, E * E))
    freq = 1.0 / 10000.0 ** (np.arange(0, ROPE, 2, dtype=f) / ROPE)
    ang = np.outer(np.arange(T, dtype=f), freq)
    cos, sin = np.cos(ang).T.astype(f), np.sin(ang).T.astype(f)
    c16, s16 = np.concatenate([cos, cos]), np.concatenate([-sin, sin])
    ones = np.ones((64, T), f)
    k["qtab"] = np.concatenate([ones, c16, c16, s16, s16])
    k["ktab"] = np.concatenate([ones, c16, s16, c16, s16])
    m = {"identb": (i == j).astype(f)}
    neg = lambda ok: np.where(ok, 0.0, NEG).astype(f)
    m["causal_s"] = neg(i >= j)
    m["causal_t"] = neg(j >= i)
    m["band_s"] = neg((i >= j) & (i - j < WINDOW))
    m["band_t"] = neg((j >= i) & (j - i < WINDOW))
    w = np.arange(BAND)[None, :]
    m["band_s1"] = neg((i + WINDOW >= w) & (i + WINDOW - w < WINDOW))
    m["band_t0"] = neg((w >= i) & (w - i < WINDOW))
    r = np.arange(HB)[None, :]
    m["pick"] = ((i == r) | (i == r + HB)).astype(f)
    return k, m


def _pack(table, parts):
    out = np.zeros((P, sum(table.values())), np.float32)
    at = 0
    for name, n in table.items():
        a = np.asarray(parts[name])
        out[:a.shape[0], at:at + n] = a.reshape(a.shape[0], n)
        at += n
    return out


def _swap(a):
    n = a.shape[-1] // 2
    return np.concatenate([a[..., n:], a[..., :n]], -1)


def _lay_out(x):
    z = lambda *s: np.zeros(s, np.float32)
    p, m = _shape_constants()
    order = np.arange(192).reshape(8, 3, 8).transpose(1, 0, 2).reshape(192)
    wi = x["L0_conv_w_qkv"].reshape(192, C)[order]
    dw = x["L0_conv_w_dw"].reshape(192, 5, 5)[order]
    pw = x["L0_conv_w_pw"].reshape(192, 8)[order]
    dwp = z(192, 26)
    for i, pair in enumerate(PAIRS5):
        dwp[:, 2 * i] = dw[:, pair[1], pair[2]]
        two = second_tap(pair, 5)
        if two:
            dwp[:, 2 * i + 1] = dw[:, two[0], two[1]]
    blocks = z(192, 192)
    for g in range(24):
        blocks[8 * g:8 * g + 8, 8 * g:8 * g + 8] = pw[8 * g:8 * g + 8].T
    p["w_q0"], p["w_kv0"] = wi[:64].T, wi[64:].T
    p["dw_q"], p["dw_kv"] = dwp[:64], dwp[64:]
    p["wi_q"], p["wi_kv"] = wi[:64], wi[64:]
    p["pw_q"], p["pw_kv"] = blocks[:64, :64], blocks[64:, 64:]
    wp = x["L0_conv_w_proj"].reshape(C, P).T
    p["proj0"] = np.concatenate([wp, wp], 1)
    bn = np.stack([x["L0_conv_bn_" + s] for s in ("gamma", "beta", "mean", "var")], 1)
    p["bn"] = np.concatenate([bn, bn], 0)
    w9 = x["L1_conv_weight"]
    conv1 = z(P, 5, C)
    for i, pair in enumerate(PAIRS3):
        conv1[:C, i] = w9[:, :, pair[1], pair[2]].T
        two = second_tap(pair, 3)
        if two:
            conv1[C:, i] = w9[:, :, two[0], two[1]].T
    p["conv1"] = conv1
    small = z(C, 68)
    small[:, 0:CQ], small[:, 32:64] = x["L2_attn_Wcq"], x["L2_attn_Wckv"]
    small[:, 64:67], small[:, 67:68] = x["L2_attn_Wgate"], x["L2_attn_W_imp"]
    p["w_small"] = small
    kr = x["L2_attn_Wk_rope"]
    p["w_kr"] = np.concatenate([z(C, 64), kr, _swap(kr), kr, _swap(kr)], 1)
    nw = z(P, 1)
    nw[0:CQ, 0], nw[32:64, 0] = x["L2_attn_q_norm_w"], x["L2_attn_kv_norm_w"]
    p["nw"] = nw
    qn = x["L2_attn_Wq_nope"].reshape(CQ, HEADS, NOPE)
    kn = x["L2_attn_Wk_nope"].reshape(CKV, HEADS, NOPE)
    p["wqn_t"], p["wkn_t"] = qn.transpose(2, 1, 0), kn.transpose(2, 1, 0)
    qr = x["L2_attn_Wq_rope"].reshape(CQ, HEADS, ROPE)
    p["w_q"] = np.concatenate([qn, z(CQ, HEADS, 32), qr, qr, _swap(qr), _swap(qr)], 2)
    wv1 = z(64, 512)
    wv1[32:64] = x["L2_attn_Wv"]
    p["w_v1"], p["w_v"] = wv1, np.concatenate([x["L2_attn_Wwin_v"], x["L2_attn_Wsel_v"]])
    k = np.concatenate([x["L2_attn_Wwin_k"], x["L2_attn_Wsel_k"]]).reshape(P, HEADS, HD)
    r = k[:, :, NOPE:]
    p["w_k"] = np.concatenate([k[:, :, :NOPE], z(P, HEADS, 32), r, _swap(r), r, _swap(r)], 2)
    p["w_p"] = x["L2_attn_Wproj"].reshape(4, P, C).transpose(1, 0, 2)
    p["r2"] = x["L2_ffn_router_w"].T
    p["w1"] = x["L2_ffn_w1"].transpose(1, 0, 2)
    p["b1"] = x["L2_ffn_b1"].reshape(4, P).T
    w2 = z(P, 4, 2, C)
    for e in range(E):
        w2[(e % 2) * C:(e % 2 + 1) * C, e // 2, e % 2] = x["L2_ffn_w2"][e]
    p["w2"] = w2
    p["b2"] = np.broadcast_to(x["L2_ffn_b2"].reshape(1, E * C), (P, E * C))
    wq = x["L3_attn_w_qkv"]
    p["q3"], p["kv3"], p["out3"] = wq[:, :P], wq[:, P:], x["L3_attn_w_out"]
    p["bout"] = np.broadcast_to(x["L3_attn_b_out"][None], (P, C))
    p["r3"] = x["L3_ffn_Wr"]
    p["br3"] = np.broadcast_to(x["L3_ffn_br"][None], (P, E))
    p["f1"] = x["L3_ffn_W1"].transpose(1, 0, 2)
    p["fb1"] = x["L3_ffn_b1"].T
    p["f2"] = x["L3_ffn_W2"].transpose(1, 0, 2)
    p["fb2"] = x["L3_ffn_b2"]
    p["gamma"] = np.broadcast_to(x["L3_ffn_gamma"][None], (P, C))
    p["beta"] = np.broadcast_to(x["L3_ffn_beta"][None], (P, C))
    return {
        "x": x["x"].reshape(B, C, T),
        "prep": _pack(PREP, p),
        "early": _pack(EARLY, p),
        "late": _pack(LATE, p),
        "masks": _pack(MASKS, m),
        "final": _pack(FINAL, p),
    }


def kernel(**inputs):
    import concourse.bacc as _bacc
    from concourse.bass_utils import run_bass_kernel_spmd as _run

    arrays = _lay_out({k: np.asarray(v) for k, v in inputs.items()})
    arrays = {k: np.ascontiguousarray(v) for k, v in arrays.items()}
    nc = _bacc.Bacc("TRN2", target_bir_lowering=False, num_devices=1)
    args = [nc.dram_tensor("in_" + k, v.shape, mybir.dt.from_np(v.dtype), kind="ExternalInput").ap()
            for k, v in arrays.items()]
    args.append(nc.dram_tensor("y", (B, C, T), F32, kind="ExternalOutput").ap())
    build(nc, *args)
    r = _run(nc, [{"in_" + k: v for k, v in arrays.items()}], core_ids=[0])
    return r.results[0]["y"].reshape(B, C, H, W)
```

```python
from contextlib import ExitStack

import numpy as np

import concourse.bass as bass
from concourse import mybir

ALU = mybir.AluOpType
ACT = mybir.ActivationFunctionType
AX = mybir.AxisListType
F32 = mybir.dt.float32
BF16 = mybir.dt.bfloat16

P = 128
B, C, H, W = 8, 64, 16, 16
T = H * W
NT = T // P
PITCH = 20
HEADS, NOPE, ROPE, VDIM = 16, 32, 16, 32
CQ, CKV = 24, 32
HD = NOPE + ROPE
KEEP, WINDOW = 128, 32
NEG = -1.0e9
E, DE = 8, 64
FF = 128
BR = 3
HB = HEADS * BR
BAND = P + WINDOW
SCALE = 1.0 / float(np.sqrt(np.float32(HD)))

PAIRS5 = [(0, dy, dx) for dy in range(5) for dx in (0, 2)] + [(1, 0, 4), (1, 2, 4), (0, 4, 4)]
PAIRS3 = [(0, dy, 0) for dy in range(3)] + [(1, 0, 2), (0, 2, 2)]


def second_tap(pair, size):
    copy, dy, dx = pair
    dy, dx = (dy, dx + 1) if copy == 0 else (dy + 1, dx)
    return (dy, dx) if dy < size and dx < size else None


PREP = dict(dw_kv=26, dw_q=26, wi_kv=64, wi_q=64, pw_kv=128, pw_q=64, conv1=5 * 64, wqn_t=HEADS * CQ,
            wkn_t=HEADS * CKV)
EARLY = dict(pairmean=128, w_q0=64, w_kv0=128, proj0=128, bn=4, blk8=128, ident=128)
LATE = dict(w_small=68, w_kr=128, nw=1, w_q=HEADS * 128, w_v1=512, w_v=512, w_p=4 * 64, w_k=HEADS * 128,
            qtab=T, ktab=T, before=128, iota=128, ties=2 * T, first8=64,
            r2=E, w1=4 * 128, b1=4, w2=4 * 128, b2=E * C,
            q3=128, kv3=256, out3=64, bout=64, blk16=128, r3=E, br3=E)
FINAL = dict(f1=E * FF, fb1=E, f2=E * C, fb2=C, gamma=C, beta=C)
MASKS = dict(identb=128, causal_s=128, causal_t=128, band_s=128, band_t=128, band_s1=BAND, band_t0=BAND,
             pick=HB)


def offsets(table):
    at, out = 0, {}
    for name, n in table.items():
        out[name] = (at, n)
        at += n
    return out, at


def build(nc, x_in, prep_in, early_in, late_in, masks_in, final_in, y_out):
    ctx = ExitStack()
    with ctx:
        def sb(name, shape, dt=F32):
            return ctx.enter_context(nc.sbuf_tensor(name, shape, dt))

        sems = {}

        def S(name):
            if name not in sems:
                sems[name] = ctx.enter_context(nc.semaphore("s_" + name))
            return sems[name]

        eo, en = offsets(EARLY)
        lo, ln = offsets(LATE)
        mo, mn = offsets(MASKS)
        early = sb("early", [P, en])
        late = sb("late", [P, ln])
        masks = sb("masks", [P, mn], BF16)

        po, pn = offsets(PREP)
        fo, fn = offsets(FINAL)
        pr = sb("pr", [P, 2, 2, 1856])
        kwT = sb("kwT", [P, HEADS, T])
        prep = pr[:, 1, :, :].rearrange("p a n -> p (a n)")[:, 0:pn]
        masks32 = kwT[:, :, :].rearrange("p h t -> p (h t)")[:, 0:mn]
        final = kwT[:, :, :].rearrange("p h t -> p (h t)")[:, 0:fn]

        def cst(name):
            for table, tile in ((eo, early), (lo, late), (mo, masks), (po, prep), (fo, final)):
                if name in table:
                    a, n = table[name]
                    return tile[:, a:a + n]

        ident, identb = cst("ident"), cst("identb")
        w_q = cst("w_q").rearrange("p (h m) -> p h m", h=HEADS)
        w_k = cst("w_k").rearrange("p (h m) -> p h m", h=HEADS)
        w_p = cst("w_p").rearrange("p (g m) -> p g m", g=4)
        w1 = cst("w1").rearrange("p (g m) -> p g m", g=4)
        w2 = cst("w2").rearrange("p (g m) -> p g m", g=4)
        f1 = cst("f1").rearrange("p (e m) -> p e m", e=E)
        f2 = cst("f2").rearrange("p (e m) -> p e m", e=E)
        ties = cst("ties").rearrange("p (t m) -> p t m", t=NT)
        first8 = cst("first8").rearrange("p (e j) -> p e j", e=E)
        conv1 = cst("conv1").rearrange("p (n m) -> p n m", n=len(PAIRS3))
        dw_kv, dw_q = cst("dw_kv"), cst("dw_q")
        pick = cst("pick")
        wqn_t = cst("wqn_t").rearrange("p (h m) -> p h m", h=HEADS)
        wkn_t = cst("wkn_t").rearrange("p (h m) -> p h m", h=HEADS)

        wc_kv = sb("wc_kv", [P, 13, P])
        wc_q = sb("wc_q", [P, 13, C])
        bin1 = sb("bin1", [P, 5, C])
        binn = sb("binn", [P, 5, C])
        bnc = sb("bnc", [P, 4])
        half = sb("half", [P, 1])
        onesk = sb("onesk", [P, 32])
        meank = sb("meank", [P, P])

        xin = sb("xin", [P, T])
        xs = sb("xs", [P, T])
        xg = sb("xg", [P, T])
        img = [sb(f"img{i}", [P, PITCH, PITCH]) for i in range(2)]
        st = sb("st", [P, 2, 6])
        st2 = sb("st2", [P, 2, 6])
        mv2 = sb("mv2", [P, 2, 2])
        gv2 = sb("gv2", [P, 2])
        mv = sb("mv", [P, 2, 2])
        gm = sb("gm", [P, 2])
        gv = sb("gv", [P, 2])
        gt = sb("gt", [P, 2])
        kv1 = sb("kv1", [P, T])
        q0 = sb("q0", [P, T])
        ktok = sb("ktok", [P, NT, P])
        vtok = sb("vtok", [P, NT, P + 1])
        kvm = sb("kvm", [P, P])
        ksm = sb("ksm", [P, P])
        den0 = sb("den0", [P, T])
        rec0 = sb("rec0", [P, T])
        o0 = sb("o0", [P, T])
        x1 = sb("x1", [P, T])
        t1 = sb("t1", [P, NT, C])
        xn = sb("xn", [P, NT, C])
        xnT = sb("xnT", [P, T])
        sm = sb("sm", [P, NT, 68])
        sq = sb("sq", [P, NT, 64])
        ms = sb("ms", [P, 2, NT])
        rs = sb("rs", [P, 2, NT])
        cn = sb("cn", [P, NT, 64])
        cnT = sb("cnT", [P, T])
        gl = sb("gl", [P, BR])
        gs = sb("gs", [P, 8])
        gate = sb("gate", [P, BR])
        gate_next = sb("gate_next", [P, BR])
        k1n = sb("k1n", [P, T])
        t1n = sb("t1n", [P, NT, C])
        xp = sb("xp", [P, NT, C])
        xpT = sb("xpT", [P, T])
        sbc = sb("sbc", [P, NT, P])
        srow = sb("srow", [P, T])
        ranks = sb("ranks", [P, NT])
        sel = sb("sel", [P, NT])
        pos = sb("pos", [P, NT])
        pickm = sb("pickm", [P, NT, KEEP])
        selT = sb("selT", [P, KEEP])
        k1T = sb("k1T", [P, T])
        qT = sb("qT", [P, HEADS, T])
        ksT = sb("ksT", [P, HEADS, KEEP])
        k1b = sb("k1b", [P, T], BF16)
        qb = sb("qb", [P, 2, 2, T], BF16)
        kwb = sb("kwb", [P, 2, 2, T], BF16)
        ksb = sb("ksb", [P, 2, 2, KEEP], BF16)
        v1 = sb("v1", [P, NT, HEADS * VDIM])
        vw = sb("vw", [P, NT, HEADS * VDIM])
        vs = sb("vs", [P, HEADS * VDIM])
        mx = sb("mx", [P, NT, HB])
        mh = sb("mh", [P, NT, P], BF16)
        mT = sb("mT", [P, T], BF16)
        scaled = pr[:, 0, 0, 0:26 * C].rearrange("p (n c) -> p n c", n=26)
        scaled_q = pr[0:C, 0, 1, 0:26 * C].rearrange("p (n c) -> p n c", n=26)
        rden = sb("rden", [P, T])
        ob = sb("ob", [P, 2, BR, T])
        oT = sb("oT", [P, 4, T])
        t2 = sb("t2", [P, NT, C])
        lg = sb("lg", [P, NT, E])
        pe8 = sb("pe8", [P, NT, E])
        c8 = sb("c8", [P, NT, 8])
        cg = sb("cg", [P, NT, E, E])
        ce = sb("ce", [P, NT, E, E])
        comb = sb("comb", [P, NT, E])
        hm = sb("hm", [P, 4, T])
        cmp_, cmq_ = hm[:, 0:NT, :], hm[:, NT:2 * NT, :]
        yb = sb("yb", [P, NT, E, C])
        ysum = sb("ysum", [P, NT, C])
        t3 = sb("t3", [P, NT, C])
        q3 = sb("q3", [P, T])
        kv3 = sb("kv3s", [P, NT, 16, 16])
        kvq = sb("kvq", [P, NT, 16, 16])
        n3 = sb("n3", [P, 4, NT * 16])
        dT = sb("dT", [P, P])
        m3 = sb("m3", [P, C])
        t4 = sb("t4", [P, NT, C])
        x4 = sb("x4", [P, NT, C])
        x4T = sb("x4T", [P, T])
        all_t4 = sb("all_t4", [P, B, NT, C])
        all_x4 = sb("all_x4", [P, B, NT, C])
        xbar = sb("xbar", [P, B])
        lr = sb("lr", [P, E])
        rw = sb("rw", [P, E])
        rt = sb("rt", [P, 12])
        load = sb("load", [P, E])
        r8 = sb("r8", [P, E, E])
        r8b = sb("r8b", [P, E, E])
        wd = sb("wd", [P, B, E])
        wdiag = sb("wdiag", [P, B, E])
        ksf = ksT[:, :, :].rearrange("p h t -> p (h t)")
        x4c = ksf[:, 0:T]
        w2s = ksf[:, T:T + E * C].rearrange("p (e c) -> p e c", e=E)
        fb2s = sb("fb2s", [P, C])
        hf = qT[:, 0:E, :]
        obf = ob[:, :, :, :].rearrange("p g r t -> p (g r t)")
        yf, yo, tf = [obf[:, i * NT * C:(i + 1) * NT * C].rearrange("p (t c) -> p t c", t=NT) for i in range(3)]
        yc = obf[0:C, 3 * NT * C:3 * NT * C + T]

        def bank(name):
            return ctx.enter_context(nc.psum_tensor(name, [P, 512], F32))

        ring = [bank("ring0"), bank("ring1")]
        PV = bank("pv")
        heads = [bank("heads0"), bank("heads1")]
        SA, SB_, SC = bank("side_a"), bank("side_b"), bank("side_c")

        def window(i, dy, dx):
            return img[i][:, dy:dy + H, dx:dx + W]

        PAIRS = HEADS // 2
        PAIR_UNITS = 7
        VALUES = [("v1", 0), ("v1", 1), ("vw", 0), ("vw", 1), ("vs", 0)]
        UNITS = PAIR_UNITS * PAIRS + len(VALUES) + 1

        MAX_PARTS = {"max0": [(0, 0, 0, 0, P), (0, 1, 2 * P, 0, P)], "max1": [(1, 0, 0, 0, T)],
                     "max2": [(0, 2, 0, 0, P), (1, 1, 2 * P, 0, P)], "max3": [(1, 2, 0, T - BAND, BAND)]}

        SCORE_UNITS = 4 * PAIRS
        WEIGH_ROUNDS = [8 * g + 8 + d for g in range(3) for d in (1, 3, 6)] + [32, 33, 34]
        PROJECT_ROUNDS = [20, 21, 23, 24, 26, 27, 29, 32]
        MAX_ROUNDS = [21, 23, 24, 26, 27, 29, 31, 33]
        ROUNDS = 37
        unit_plan, unit_at = [], 0
        for r_ in range(ROUNDS):
            kinds = [(kind, k) for k, at in enumerate(PROJECT_ROUNDS) if at == r_ for kind in ("q", "kw", "ks")]
            kinds += [(kind, k) for k, at in enumerate(MAX_ROUNDS) if at == r_ for kind in MAX_PARTS]
            kinds += {34: [("turn", 0)], 35: VALUES[:3], 36: VALUES[3:]}.get(r_, [])
            unit_plan.append([(unit_at + i, kind, k) for i, (kind, k) in enumerate(kinds)])
            unit_at += len(kinds)
        assert unit_at == UNITS

        def starts(image, n):
            return n >= 0 or type(image) is not int or image > 0

        block = ctx.enter_context(nc.Block())

        def run(eng, step):
            step(None, 0, None)
            step(0, 1, None)
            with eng.Fori(1, B - 1) as j:
                step(j, eng.snap(j + 1), eng.snap(j - 1))
            step(B - 1, None, B - 2)
            step(None, None, B - 1)

        def rounds(main, heads_, side):
            for r in range(ROUNDS):
                if main:
                    main(r)
                if heads_:
                    for unit in unit_plan[r]:
                        heads_(*unit)
                next(side, None)
            for _ in side:
                pass

        @block.sync
        def _(sp):
            sp.dma_start(prep, prep_in).then_inc(S("prep"), 16)
            sp.dma_start(early[:, :], early_in).then_inc(S("early"), 16)
            sp.dma_start(late[:, :], late_in).then_inc(S("late"), 16)
            sp.dma_start(masks32, masks_in).then_inc(S("masks"), 16)
            with sp.Fori(0, B) as b:
                sp.wait_ge(S("x_free"), b + 1)
                for half_ in range(2):
                    sp.dma_start(xin[half_ * C:(half_ + 1) * C, :], x_in[b]).then_inc(S("x_loaded"), 16)
            sp.wait_ge(S("attention_done"), 1)
            sp.dma_start(final, final_in).then_inc(S("final"), 16)
            with sp.Fori(0, B) as b:
                sp.wait_ge(S("y_copied"), b + 1)
                sp.dma_start(y_out[b], yc[:, :]).then_inc(S("y_stored"), 16)
            sp.wait_ge(S("y_stored"), 16 * (B + 1))

        @block.gpsimd
        def _(pool):
            nc.gpsimd.memset(half[:, :], -0.5).then_inc(S("half"), 1)
            pool.wait_ge(S("half"), 1)
            pool.wait_ge(S("bn_var"), 1)
            nc.gpsimd.tensor_tensor(bnc[:, 1:2], bnc[:, 0:1], half[:, :], ALU.pow).then_inc(S("bn_rstd"), 1)

            def rsqrt(n, out, in_, ready, done):
                pool.wait_ge(S(ready), n)
                h = half[:, 0:1]
                if len(in_.shape) == 3:
                    h = h.unsqueeze(2)
                nc.gpsimd.tensor_tensor(out, in_, h.broadcast_to(tuple(in_.shape)), ALU.pow)\
                    .then_inc(S(done), 1)

            def front(n):
                yield
                rsqrt(n, gt[:, 1:2], gt[:, 0:1], "gn1_var", "gn1_rstd")
                for _ in range(8):
                    yield
                rsqrt(n, gt[:, 1:2], gt[:, 0:1], "gn2_var", "gn2_rstd")
                for _ in range(3):
                    yield
                rsqrt(n, gv[:, :], mv[:, :, 1], "ln1_var", "ln1_rstd")
                for _ in range(3):
                    yield
                rsqrt(n, rs[:, :, :], ms[:, :, :], "rms_var", "rms_rstd")
                for _ in range(5):
                    yield

            def back_first(n):
                rsqrt(n, gv2[:, :], mv2[:, :, 1], "ln2_var", "ln2_rstd")

            def back(n, image):
                for _ in range(4):
                    yield
                for t in range(NT):
                    pool.wait_ge(S("y_biased"), image * NT + t + 1)
                    nc.gpsimd.tensor_tensor(yb[:, t, :, :], yb[:, t, :, :],
                                            comb[:, t, :].unsqueeze(2).broadcast_to((P, E, C)), ALU.mult)\
                        .then_inc(S("y_weighted"), 1)
                yield
                rsqrt(n, gv2[:, :], mv2[:, :, 1], "ln3_var", "ln3_rstd")
                for _ in range(3):
                    yield
                rsqrt(n, n3[:, 2, :], n3[:, 1, :], "n3_var", "n3_rstd")
                for _ in range(4):
                    yield
                rsqrt(n, gv2[:, :], mv2[:, :, 1], "ln4_var", "ln4_rstd")
                yield

            def step(image, nxt, prev):
                def side():
                    if prev is not None:
                        back_first(prev + 1)
                    if nxt is not None:
                        yield from front(nxt + 1)
                    if prev is not None:
                        yield from back(prev + 1, prev)

                def main(r):
                    if r in WEIGH_ROUNDS[2::3]:
                        g = WEIGH_ROUNDS.index(r) // 3
                        pool.wait_ge(S("branch_out"), image * 12 + 3 * g + 3)
                        if g == 0 and starts(image, -1):
                            pool.wait_ge(S("attn_out"), image)
                        nc.gpsimd.tensor_tensor(oT[:, g, :], ob[:, g % 2, 0, :], ob[:, g % 2, 1, :], ALU.add)\
                            .then_inc(S("pool_add"), 1)
                        pool.wait_ge(S("pool_add"), image * 4 + g + 1)
                        nc.gpsimd.tensor_tensor(oT[:, g, :], oT[:, g, :], ob[:, g % 2, 2, :], ALU.add)\
                            .then_inc(S("o_summed"), 1)

                rounds(main if image is not None else None, None, side())

            run(pool, step)
            with pool.Fori(0, B) as b:
                rsqrt(b + 1, gv[:, :], mv[:, :, 1], "ln5_var", "ln5_rstd")

        @block.tensor
        def _(pe):
            wide = [ring[0], ring[1], heads[0], heads[1]]
            pe.wait_ge(S("prep"), 16)
            pe.wait_ge(S("early"), 16)
            pe.wait_ge(S("scaled"), 2)
            for i in range(13):
                m = pe.matmul(wide[i // 4][:, (i % 4) * P:(i % 4 + 1) * P],
                              scaled[:, 2 * i:2 * i + 2, :].rearrange("p a c -> p (a c)"), cst("pw_kv"),
                              start=True, stop=True)
            for i in range(13):
                m = pe.matmul((SA, SB_)[i // 8][:, (i % 8) * C:(i % 8 + 1) * C],
                              scaled_q[:, 2 * i:2 * i + 2, :].rearrange("p a c -> p (a c)"),
                              cst("pw_q")[0:C, :], start=True, stop=True)
            m.then_inc(S("composed"), 1)
            pe.wait_ge(S("late"), 16)
            for h in range(HEADS):
                m = pe.matmul(PV[0:CQ, h * CKV:(h + 1) * CKV], wqn_t[0:NOPE, h, :], wkn_t[0:NOPE, h, :],
                              start=True, stop=True)
            m.then_inc(S("absorbed"), 1)
            pe.wait_ge(S("prepared"), 1)

            def after(n, *names):
                for name in names:
                    pe.wait_ge(S(name), n)

            def transpose_tok(src, dst, col, done):
                pe.sem_inc(S("pe_gap"), 1)
                for t in range(NT):
                    m = pe.transpose(dst[0:C, col + t * P:col + (t + 1) * P], src[:, t, :], ident)
                m.then_inc(S(done), 1)

            def front(n):
                yield
                after(n, "gn1_stats")
                pe.matmul(SB_[:, 0:2], cst("pairmean"), mv[:, 0, :], start=True, stop=True)\
                    .then_inc(S("gn1_mean"), 1)
                yield
                yield
                after(n, "gn1_done")
                for i, (copy, dy, dx) in enumerate(PAIRS5):
                    pe.matmul(SA[:, 0:T], wc_kv[:, i, :], window(copy, dy, dx), start=(i == 0), stop=(i == 12))
                yield
                pe.matmul(SA[0:C, T:2 * T], cst("w_q0"), window(0, 2, 2), start=True, stop=True)
                for i, (copy, dy, dx) in enumerate(PAIRS5):
                    pe.matmul(SA[C:P, T:2 * T], wc_q[:, i, :], window(copy, dy, dx), start=(i == 0),
                              stop=(i == 12))
                for t in range(NT):
                    m = pe.matmul(SB_[:, t * P:(t + 1) * P], xg[:, t * P:(t + 1) * P], cst("w_kv0"),
                                  start=True, stop=True)
                m.then_inc(S("conv5"), 1)
                yield
                after(n, "kv1_copied")
                for t in range(NT):
                    m = pe.transpose(SA[:, t * P:(t + 1) * P], kv1[:, t * P:(t + 1) * P], ident)
                m.then_inc(S("kv1_turned"), 1)
                yield
                after(n, "kv_ready")
                for t in range(NT):
                    m = pe.matmul(SB_[:, 0:P + 1], ktok[:, t, :], vtok[:, t, :], start=(t == 0), stop=(t == NT - 1))
                m.then_inc(S("kv_sum"), 1)
                yield
                after(n, "kv_masked")
                pe.matmul(SA[:, 0:T], kvm[:, :], q0[:, :], start=True, stop=True)
                pe.matmul(SA[:, T:2 * T], ksm[:, :], q0[:, :], start=True, stop=True).then_inc(S("lin_out"), 1)
                yield
                after(n, "o0_ready")
                pe.matmul(SB_[:, 0:T], cst("proj0"), o0[:, :], start=True, stop=True).then_inc(S("proj0"), 1)
                yield
                after(n, "gn2_stats")
                pe.matmul(SA[:, 0:2], cst("pairmean"), mv[:, 0, :], start=True, stop=True)\
                    .then_inc(S("gn2_mean"), 1)
                yield
                yield
                after(n, "gn2_done")
                for i, (copy, dy, dx) in enumerate(PAIRS3):
                    m = pe.matmul(SB_[0:C, 0:T], bin1[:, i, :], window(copy, dy + 1, dx + 1), start=(i == 0),
                                  stop=(i == 4))
                m.then_inc(S("conv3"), 1)
                yield
                after(n, "x2")
                pe.sem_inc(S("pe_gap"), 1)
                for t in range(NT):
                    m = pe.transpose(SA[:, t * C:(t + 1) * C], x1[0:C, t * P:(t + 1) * P], ident[0:C, 0:C])
                m.then_inc(S("x2_turned"), 1)
                yield
                yield
                after(n, "xn1")
                transpose_tok(xn, SA, 0, "xn1_turned")
                yield
                after(n, "xnT1")
                for t in range(NT):
                    m = pe.matmul(SB_[:, t * 68:(t + 1) * 68], xnT[:, t * P:(t + 1) * P], cst("w_small"),
                                  start=True, stop=True)
                m.then_inc(S("small"), 1)
                pe.matmul(SA[:, 0:T], cst("w_kr"), xnT[:, :], start=True, stop=True).then_inc(S("k_rope"), 1)
                yield
                after(n, "small_copied")
                for t in range(NT):
                    m = pe.matmul(SB_[:, 140:140 + BR], meank[:, :], sm[:, t, 64:64 + BR], start=(t == 0),
                                  stop=(t == NT - 1))
                m.then_inc(S("gate_mean"), 1)
                after(n, "score_bc", "k_rotated")
                for t in range(NT):
                    m = pe.transpose(SA[:, t * P:(t + 1) * P], sbc[:, t, :], ident)
                m.then_inc(S("score_row"), 1)
                yield
                after(n, "cn_ready", "gate_read")
                transpose_tok(cn, SB_, T, "cn_turned")
                yield
                after(n, "selected")
                pe.matmul(SA[:, 0:1], cst("before"), sel[:, 0:1], start=True, stop=True)
                pe.matmul(SA[:, 1:2], cst("before"), sel[:, 1:2], start=True, stop=False)
                pe.matmul(SA[:, 1:2], meank[:, :], gs[:, 7:8], start=False, stop=True)\
                    .then_inc(S("positions"), 1)
                yield
                after(n, "pick_ready")
                for t in range(NT):
                    m = pe.matmul(SA[C:P, 0:P], xn[:, t, :], pickm[:, t, :], start=(t == 0), stop=(t == NT - 1))
                m.then_inc(S("sel_x"), 1)
                after(n, "cnT")
                yield

            def back_first(n, image):
                pe.wait_ge(S("o_summed"), image * 4 + 4)
                for t in range(NT):
                    for g in range(4):
                        m = pe.matmul(SA[:, t * C:(t + 1) * C], oT[:, g, t * P:(t + 1) * P], w_p[:, g, :],
                                      start=(g == 0), stop=(g == 3))
                m.then_inc(S("attn_out"), 1)

            def back(n, image):
                yield
                after(n, "xn2")
                transpose_tok(xp, SB_, 0, "xn2_turned")
                yield
                after(n, "xnT2")
                for t in range(NT):
                    m = pe.matmul(SA[:, t * E:(t + 1) * E], xpT[:, t * P:(t + 1) * P], cst("r2"),
                                  start=True, stop=True)
                m.then_inc(S("logits"), 1)
                after(n, "sc_free")
                for u in range(2):
                    for i in range(2):
                        m = pe.matmul((SC, SB_)[u][:, i * T:(i + 1) * T], w1[:, 2 * u + i, :], xpT[:, :],
                                      start=True, stop=True)
                    m.then_inc(S("hidden"), 1)
                yield
                yield
                after(n, "gelu1")
                for t in range(NT):
                    for i in range(4):
                        m = pe.matmul((SA, SC)[t][:, i * P:(i + 1) * P], hm[:, i, t * P:(t + 1) * P], w2[:, i, :],
                                      start=True, stop=True)
                    m.then_inc(S("expert_out"), 1)
                yield
                yield
                yield
                after(n, "xn3")
                transpose_tok(xp, SB_, 0, "xn3_turned")
                yield
                after(n, "xnT3")
                pe.matmul(SA[:, 0:T], cst("q3"), xpT[:, :], start=True, stop=True)
                for t in range(NT):
                    m = pe.matmul(SB_[:, t * T:(t + 1) * T], xpT[:, t * P:(t + 1) * P], cst("kv3"),
                                  start=True, stop=True)
                m.then_inc(S("qkv3"), 1)
                yield
                yield
                after(n, "kv3_normed", "q3_copied")
                kvf = kvq[:, :, :, :].rearrange("p t g d -> p t (g d)")
                for t in range(NT):
                    m = pe.matmul(SA[:, 0:P], kvf[:, t, P:2 * P], kvf[:, t, 0:P], start=(t == 0),
                                  stop=(t == NT - 1))
                m.then_inc(S("dots"), 1)
                yield
                after(n, "dots_masked")
                pe.matmul(SA[:, P:P + C], dT[:, :], cst("out3"), start=True, stop=True).then_inc(S("dots_out"), 1)
                yield
                after(n, "m3")
                for t in range(NT):
                    m = pe.matmul(SB_[:, t * C:(t + 1) * C], q3[:, t * P:(t + 1) * P], m3[:, :],
                                  start=True, stop=True)
                m.then_inc(S("attn3"), 1)
                yield
                yield
                after(n, "xn4")
                for t in range(NT):
                    m = pe.matmul(SC[0:C, 0:1], x4[:, t, :], meank[:, 0:1], start=(t == 0), stop=(t == NT - 1))
                m.then_inc(S("token_mean"), 1)
                yield

            def step(image, nxt, prev):
                def side():
                    if prev is not None:
                        back_first(prev + 1, prev)
                    if nxt is not None:
                        yield from front(nxt + 1)
                    if prev is not None:
                        yield from back(prev + 1, prev)

                def heads_(u, kind, k):
                    dst = heads[u % 2]
                    if u >= 2 or starts(nxt, -1):
                        pe.wait_ge(S("unit_free"), nxt * UNITS + u - 1)
                    if kind == "q":
                        if k == 0:
                            after(nxt + 1, "cnT")
                        for i in range(2):
                            m = pe.matmul(dst[:, i * T:(i + 1) * T], w_q[:, 2 * k + i, :], cnT[:, :],
                                          start=True, stop=True)
                    elif kind == "kw":
                        for i in range(2):
                            m = pe.matmul(dst[:, i * T:(i + 1) * T], w_k[:, 2 * k + i, :], xnT[:, :],
                                          start=True, stop=True)
                    elif kind == "ks":
                        if k == 0:
                            after(nxt + 1, "selT")
                        for i in range(2):
                            m = pe.matmul(dst[:, i * P:(i + 1) * P], w_k[:, 2 * k + i, :], selT[:, :],
                                          start=True, stop=True)
                    elif kind == "turn":
                        after(nxt + 1, "mh_ready")
                        pe.sem_inc(S("pe_gap"), 1)
                        mTp = dst[:, 0:P].bitcast(BF16)
                        for t in range(NT):
                            m = pe.transpose(mTp[:, t * P:(t + 1) * P], mh[:, t, :], identb)
                    elif kind[0] == "v":
                        src = {"v1": cnT, "vw": xnT, "vs": selT}[kind]
                        m = pe.matmul(dst[:, :], src[:, k * P:(k + 1) * P], cst("w_v1" if kind == "v1" else "w_v"),
                                      start=True, stop=True)
                    else:
                        if kind == "max0":
                            pe.wait_ge(S("heads_bf16"), nxt * 3 * PAIRS + 3 * k + 3)
                            if k == 0:
                                after(nxt + 1, "k1b")
                        for qt, br, at, key0, keys in MAX_PARTS[kind]:
                            for i in range(2):
                                out = dst[:, at + i * keys:at + (i + 1) * keys]
                                rhs = (k1b[:, key0:key0 + keys], ksb[:, k % 2, i, :],
                                       kwb[:, k % 2, i, key0:key0 + keys])[br]
                                m = pe.matmul(out, qb[:, k % 2, i, qt * P:(qt + 1) * P], rhs,
                                              start=True, stop=(br == 1))
                                if br == 0:
                                    m = pe.matmul(out[:, keys - P:keys], identb, cst("causal_s"),
                                                  start=False, stop=True)
                                elif br == 2:
                                    m = pe.matmul(out, identb, cst("band_s" if qt == 0 else "band_s1"),
                                                  start=False, stop=True)
                    m.then_inc(S("unit_full"), 1)

                def fold(out, br, h, q_, nq, stop):
                    r = br * HEADS + h
                    return pe.matmul(out, pick[:, r:r + 1].broadcast_to((P, P)), mT[:, q_:q_ + nq],
                                     start=False, stop=stop)

                def scores(t):
                    hp, i = t // 4, t % 4
                    h0 = 2 * hp
                    dst = ring[t % 2]
                    if t == 0:
                        after(image + 1, "mT", "k1T_taken")
                    if t >= 2 or starts(image, -1):
                        pe.wait_ge(S("exp_done"), image * SCORE_UNITS + t - 1)
                    if i == 0:
                        pe.matmul(dst[:, :], k1T[:, 0:P], qT[:, h0:h0 + 2, :], start=True, stop=False)
                        for j in range(2):
                            fold(dst[:, j * T:(j + 1) * T], 0, h0 + j, 0, T, False)
                            m = pe.matmul(dst[:, j * T:j * T + P], identb, cst("causal_t"), start=False,
                                          stop=(j == 1))
                    elif i == 1:
                        for j in range(2):
                            pe.matmul(dst[:, j * T:(j + 1) * T], ksT[:, h0 + j, :], qT[:, h0 + j, :],
                                      start=True, stop=False)
                            m = fold(dst[:, j * T:(j + 1) * T], 1, h0 + j, 0, T, True)
                    elif i == 2:
                        pe.matmul(dst[:, 0:T], k1T[:, P:T], qT[:, h0:h0 + 2, P:T], start=True, stop=False)
                        for j in range(2):
                            out = dst[:, j * P:(j + 1) * P]
                            fold(out, 0, h0 + j, P, P, False)
                            pe.matmul(out, identb, cst("causal_t"), start=False, stop=(j == 1))
                        for j in range(2):
                            out = dst[:, T + j * P:T + (j + 1) * P]
                            pe.matmul(out, kwT[:, h0 + j, P:T], qT[:, h0 + j, P:T], start=True, stop=False)
                            fold(out, 2, h0 + j, P, P, False)
                            m = pe.matmul(out, identb, cst("band_t"), start=False, stop=True)
                    else:
                        for j in range(2):
                            out = dst[:, j * BAND:(j + 1) * BAND]
                            pe.matmul(out, kwT[:, h0 + j, 0:P], qT[:, h0 + j, 0:BAND], start=True, stop=False)
                            fold(out, 2, h0 + j, 0, BAND, False)
                            m = pe.matmul(out, identb, cst("band_t0"), start=False, stop=True)
                    m.then_inc(S("scores"), 1)

                def weigh(u):
                    g, br = u // 3, u % 3
                    if br == 0:
                        pe.wait_ge(S("exp_done"), image * SCORE_UNITS + 8 * (g + 1))
                    if u or starts(image, -1):
                        pe.wait_ge(S("branch_out"), image * 12 + u)
                    for den in range(2):
                        c = T * den

                        def mm(j, cols, vals, probs, start, stop):
                            lhs = onesk[:, :] if den else vals[:, (4 * g + j) * VDIM:(4 * g + j + 1) * VDIM]
                            return pe.matmul(PV[32 * j:32 * j + 32, c + cols[0]:c + cols[1]], lhs, probs,
                                             start=start, stop=stop)

                        def p_of(j, a, nn):
                            return pr[:, g % 2, j // 2, a:a + nn]

                        if br == 0:
                            for j in range(4):
                                mm(j, (0, T), v1[:, 0, :], p_of(j, (j % 2) * T, T), True, False)
                            for j in range(4):
                                m = mm(j, (P, T), v1[:, 1, :], p_of(j, 1024 + (j % 2) * P, P), False, True)
                        elif br == 1:
                            for j in range(4):
                                m = mm(j, (0, T), vs[:, :], p_of(j, 512 + (j % 2) * T, T), True, True)
                        else:
                            for j in range(4):
                                mm(j, (P, T), vw[:, 1, :], p_of(j, 1280 + (j % 2) * P, P), True, False)
                            for j in range(4):
                                mm(j, (P, BAND), vw[:, 0, :], p_of(j, 1536 + (j % 2) * BAND + P, WINDOW),
                                   False, True)
                            for j in range(4):
                                m = mm(j, (0, P), vw[:, 0, :], p_of(j, 1536 + (j % 2) * BAND, P), True, True)
                    m.then_inc(S("weighed"), 1)

                def main(r):
                    if r < SCORE_UNITS:
                        scores(r)
                    if r in WEIGH_ROUNDS:
                        weigh(WEIGH_ROUNDS.index(r))

                rounds(main if image is not None else None, heads_ if nxt is not None else None, side())

            run(pe, step)

            pe.wait_ge(S("final"), 16)
            pe.wait_ge(S("xbar_kept"), B)
            pe.matmul(SB_[0:B, 0:E], xbar[:, :], cst("r3"), start=True, stop=True).then_inc(S("route_logits"), 1)
            pe.wait_ge(S("route1"), 1)
            pe.matmul(SB_[0:B, 16:16 + E], meank[0:B, 0:B], rw[0:B, :], start=True, stop=True)\
                .then_inc(S("route_load"), 1)
            pe.wait_ge(S("route2"), 1)
            pe.matmul(SA[:, 0:B * E], meank[:, :], wdiag[:, :, :].rearrange("p b e -> p (b e)"),
                      start=True, stop=True).then_inc(S("route_bc"), 1)

            with pe.Fori(0, B) as b:
                n = pe.snap(b + 1)
                pe.wait_ge(S("x4_fetched"), n)
                pe.sem_inc(S("pe_gap"), 1)
                for t in range(NT):
                    m = pe.transpose(SA[0:C, T + t * P:T + (t + 1) * P], x4[:, t, :], ident)
                m.then_inc(S("x4_turned"), 1)
                pe.wait_ge(S("x4c"), n)
                pe.wait_ge(S("f_in"), n)
                for e in range(E):
                    m = pe.matmul(wide[e // 2][:, (e % 2) * T:(e % 2 + 1) * T], f1[:, e, :], x4c[:, :],
                                  start=True, stop=True)
                    if e % 2:
                        m.then_inc(S("f_hidden"), 1)
                pe.wait_ge(S("f_gelu"), b * E + E)
                for t in range(NT):
                    for e in range(E):
                        m = pe.matmul(SB_[:, t * C:(t + 1) * C], hf[:, e, t * P:(t + 1) * P], w2s[:, e, :],
                                      start=(e == 0), stop=False)
                    m = pe.matmul(SB_[:, t * C:(t + 1) * C], meank[:, :], fb2s[:, :], start=False, stop=True)
                m.then_inc(S("f_out"), 1)
                pe.wait_ge(S("tf_ready"), n)
                pe.sem_inc(S("pe_gap"), 1)
                for t in range(NT):
                    m = pe.transpose(SA[0:C, t * P:(t + 1) * P], tf[:, t, :], ident)
                m.then_inc(S("f_turned"), 1)

        @block.scalar
        def _(act):
            def after(n, *names):
                for name in names:
                    act.wait_ge(S(name), n)

            def front(n):
                for _ in range(4):
                    yield
                after(n, "conv5")
                kv_tok = lambda src, c: src[:, 0:T].rearrange("p (t c) -> p t c", t=NT)[:, :, c:c + C]
                act.activation(ktok[:, :, 0:C], kv_tok(SB_, 0), ACT.Relu)
                act.activation(vtok[:, :, 0:C], kv_tok(SB_, C), ACT.Copy)
                yield
                after(n, "kv1_turned")
                act.activation(ktok[:, :, C:P], kv_tok(SA, 0), ACT.Relu)
                act.activation(vtok[:, :, C:P], kv_tok(SA, C), ACT.Copy).then_inc(S("kv_ready"), 1)
                for _ in range(9):
                    yield
                after(n, "xn1_turned")
                act.activation(xnT[0:C, :], SA[0:C, 0:T], ACT.Copy).then_inc(S("xnT1"), 1)
                yield
                yield
                yield
                after(n, "cn_turned")
                act.activation(cnT[0:C, :], SB_[0:C, T:2 * T], ACT.Copy, scale=cst("nw")[0:C, :])\
                    .then_inc(S("cnT"), 1)
                after(n, "gate_max")
                act.activation(gs[:, 0:BR], gl[:, :], ACT.Exp, bias=gs[:, 4:5]).then_inc(S("gate_exp"), 1)
                yield
                yield
                after(n, "sel_x")
                act.activation(selT[C:P, :], SA[C:P, 0:P], ACT.Copy).then_inc(S("selT"), 1)
                yield

            def back(n, image):
                yield
                after(n, "xn2_turned")
                act.activation(xpT[0:C, :], SB_[0:C, 0:T], ACT.Copy).then_inc(S("xnT2"), 1)
                yield
                after(n, "logit_max")
                for t in range(NT):
                    act.activation(pe8[:, t, :], SA[:, t * E:(t + 1) * E], ACT.Exp, bias=c8[:, t, 1:2],
                                   accum_out=c8[:, t, 2:3]).then_inc(S("logit_exp"), 1)
                yield
                for u in range(2):
                    act.wait_ge(S("hidden"), image * 2 + u + 1)
                    for i in range(2):
                        a = act.activation(hm[:, 2 * u + i, :], (SC, SB_)[u][:, i * T:(i + 1) * T], ACT.Gelu,
                                           bias=cst("b1")[:, 2 * u + i:2 * u + i + 1])
                a.then_inc(S("gelu1"), 1)
                for _ in range(4):
                    yield
                after(n, "xn3_turned")
                act.activation(xpT[0:C, :], SB_[0:C, 0:T], ACT.Copy).then_inc(S("xnT3"), 1)
                yield
                after(n, "qkv3")
                act.activation(q3[:, :], SA[:, 0:T], ACT.Copy).then_inc(S("q3_copied"), 1)
                for _ in range(6):
                    yield
                after(n, "token_mean")
                slot = slice(image, image + 1) if type(image) is int else bass.ds(image, 1)
                act.activation(xbar[0:C, slot], SC[0:C, 0:1], ACT.Copy).then_inc(S("xbar_kept"), 1)
                act.wait_ge(S("xbar_kept"), n)
                act.sem_inc(S("sc_free"), 1)
                yield

            def step(image, nxt, prev):
                def side():
                    if nxt is not None:
                        yield from front(nxt + 1)
                    if prev is not None:
                        yield from back(prev + 1, prev)

                def heads_(u, kind, k):
                    if kind in ("q", "kw", "ks"):
                        i = ("q", "kw", "ks").index(kind)
                        src, dst = ((qT, qb), (kwT, kwb), (ksT, ksb))[i]
                        act.wait_ge(S("heads_ready"), nxt * 3 * PAIRS + 3 * k + i + 1)
                        if k >= 2:
                            act.wait_ge(S("unit_full"), nxt * UNITS + last_max[k - 2] + 1)
                        act.activation(dst[:, k % 2, :, :], src[:, 2 * k:2 * k + 2, :], ACT.Copy)\
                            .then_inc(S("heads_bf16"), 1)
                    elif kind == "turn" or kind[0] == "v":
                        act.wait_ge(S("unit_full"), nxt * UNITS + u + 1)
                        act.wait_ge(S("unit_free"), nxt * UNITS + u)
                        if kind == "turn":
                            if image is not None:
                                act.wait_ge(S("scores"), image * SCORE_UNITS + SCORE_UNITS)
                            act.activation(mT[:, :], heads[u % 2][:, 0:P].bitcast(BF16), ACT.Copy)\
                                .then_inc(S("unit_free"), 1)
                            act.wait_ge(S("unit_free"), nxt * UNITS + u + 1)
                            act.sem_inc(S("mT"), 1)
                        else:
                            if image is not None:
                                act.wait_ge(S("weighed"), image * 12 + 12)
                            dst = {"v1": v1[:, k, :], "vw": vw[:, k, :], "vs": vs[:, :]}[kind]
                            act.activation(dst, heads[u % 2][:, :], ACT.Copy).then_inc(S("unit_free"), 1)

                def main(r):
                    if r < SCORE_UNITS:
                        hp, i = r // 4, r % 4
                        g = hp // 2
                        if hp % 2 == 0 and i == 0 and (g >= 2 or starts(image, -1)):
                            act.wait_ge(S("weighed"), image * 12 + 3 * (g - 1))
                        w = 2 * BAND if i == 3 else 512
                        act.wait_ge(S("scores"), image * SCORE_UNITS + r + 1)
                        act.activation(pr[:, g % 2, hp % 2, 512 * i:512 * i + w], ring[r % 2][:, 0:w], ACT.Exp,
                                       scale=SCALE).then_inc(S("exp_done"), 1)

                rounds(main if image is not None else None, heads_ if nxt is not None else None, side())

            last_max = {k: u for units in unit_plan for u, kind, k in units if kind == "max3"}
            act.sem_inc(S("sc_free"), 1)
            run(act, step)

            act.wait_ge(S("final"), 16)
            act.wait_ge(S("route_max"), 1)
            act.activation(rw[0:B, :], lr[0:B, :], ACT.Exp, bias=rt[0:B, 1:2], accum_out=rt[0:B, 2:3])\
                .then_inc(S("route_exp"), 1)
            act.wait_ge(S("route_max"), 2)
            act.activation(lr[0:B, :], rw[0:B, :], ACT.Exp, bias=rt[0:B, 5:6], accum_out=rt[0:B, 6:7])\
                .then_inc(S("route_exp"), 1)
            act.wait_ge(S("route_max"), 3)
            act.activation(rw[0:B, :], lr[0:B, :], ACT.Exp, bias=rt[0:B, 9:10]).then_inc(S("route_exp"), 1)

            wide = [ring[0], ring[1], heads[0], heads[1]]
            act.sem_inc(S("y_stored"), 16)
            with act.Fori(0, B) as b:
                n = act.snap(b + 1)
                act.wait_ge(S("x4_turned"), n)
                act.activation(x4c[0:C, :], SA[0:C, T:2 * T], ACT.Copy).then_inc(S("x4c"), 1)
                for e in range(E):
                    if e % 2 == 0:
                        act.wait_ge(S("f_hidden"), b * 4 + e // 2 + 1)
                    act.activation(hf[:, e, :], wide[e // 2][:, (e % 2) * T:(e % 2 + 1) * T], ACT.Gelu,
                                   bias=cst("fb1")[:, e:e + 1]).then_inc(S("f_gelu"), 1)
                act.wait_ge(S("f_turned"), n)
                act.wait_ge(S("y_stored"), b * 16 + 16)
                act.activation(yc[:, :], SA[0:C, 0:T], ACT.Copy).then_inc(S("y_copied"), 1)

        @block.vector
        def _(dve):
            V = nc.vector
            count = [0]

            def link(ins):
                count[0] += 1
                ins.then_inc(S("dve_chain"), 1)
                dve.wait_ge(S("dve_chain"), count[0])

            def restart():
                count[0] = 0
                dve.sem_clear(S("dve_chain"))

            for tile in (img[0], img[1], xnT, xpT, cnT, selT, cn, k1n, xbar, mh, wdiag, fb2s, gs):
                V.memset(tile[:], 0.0)
            V.memset(onesk[:, :], 1.0)
            V.memset(meank[:, :], 1.0 / T)
            link(V.memset(vtok[:, :, P:P + 1], 1.0))
            dve.sem_inc(S("x_free"), 1)
            dve.wait_ge(S("prep"), 16)
            dve.wait_ge(S("early"), 16)
            V.tensor_tensor(scaled[:, :, :], cst("wi_kv").unsqueeze(1).broadcast_to((P, 26, C)),
                            dw_kv.unsqueeze(2).broadcast_to((P, 26, C)), ALU.mult).then_inc(S("scaled"), 1)
            V.tensor_tensor(scaled_q[:, :, :], cst("wi_q")[0:C, :].unsqueeze(1).broadcast_to((C, 26, C)),
                            dw_q[0:C, :].unsqueeze(2).broadcast_to((C, 26, C)), ALU.mult)\
                .then_inc(S("scaled"), 1)
            link(V.tensor_scalar(bin1[:, :, :], conv1, 0.0, None, ALU.is_gt))
            link(V.tensor_scalar(binn[:, :, :], conv1, 0.0, None, ALU.is_lt))
            link(V.tensor_tensor(bin1[:, :, :], bin1[:, :, :], binn[:, :, :], ALU.subtract))
            bn = cst("bn")
            V.tensor_scalar(bnc[:, 0:1], bn[:, 3:4], 1e-5, None, ALU.add).then_inc(S("bn_var"), 1)
            dve.wait_ge(S("bn_rstd"), 1)
            link(V.tensor_tensor(bnc[:, 2:3], bn[:, 0:1], bnc[:, 1:2], ALU.mult))
            link(V.tensor_tensor(bnc[:, 3:4], bn[:, 2:3], bnc[:, 2:3], ALU.mult))
            link(V.tensor_tensor(bnc[:, 3:4], bn[:, 1:2], bnc[:, 3:4], ALU.subtract))
            dve.wait_ge(S("composed"), 1)
            for i, src in enumerate((ring[0], ring[1], heads[0], heads[1])):
                k = min(4, 13 - 4 * i)
                V.tensor_copy(wc_kv[:, 4 * i:4 * i + k, :], src[:, 0:k * P].rearrange("p (n m) -> p n m", n=k))
            V.tensor_copy(wc_q[:, 0:8, :], SA[:, :].rearrange("p (n m) -> p n m", n=8))
            link(V.tensor_copy(wc_q[:, 8:13, :], SB_[:, 0:5 * C].rearrange("p (n m) -> p n m", n=5)))
            dve.wait_ge(S("absorbed"), 1)
            link(V.tensor_copy(w_q[0:CQ, :, NOPE:2 * NOPE],
                               PV[0:CQ, :].rearrange("p (h m) -> p h m", h=HEADS)))
            link(V.tensor_scalar(cst("w_kr"), cst("w_kr"), 1.0 / HEADS, None, ALU.mult))
            dve.wait_ge(S("masks"), 16)
            link(V.tensor_copy(masks[:, :], masks32))
            dve.sem_inc(S("prepared"), 1)

            def after(n, *names):
                for name in names:
                    dve.wait_ge(S(name), n)

            def tok(src):
                return src[:, 0:NT * C].rearrange("p (t c) -> p t c", t=NT)

            def group_stats(x, which):
                link(V.bn_stats(st[:, 0, :], x[:, :]))
                link(V.bn_aggr(mv[:, 0, :], st[:, 0, :]))
                V.scalar_tensor_tensor(out=mv[:, 0, 1:2], in0=mv[:, 0, 0:1], scalar=mv[:, 0, 0:1],
                                       in1=mv[:, 0, 1:2], op0=ALU.mult, op1=ALU.add)\
                    .then_inc(S(f"gn{which}_stats"), 1)

            def group_var(n, src, which):
                after(n, f"gn{which}_mean")
                link(V.tensor_copy(gm[:, :], src[:, 0:2]))
                link(V.scalar_tensor_tensor(out=gt[:, 0:1], in0=gm[:, 0:1], scalar=gm[:, 0:1],
                                            in1=gm[:, 1:2], op0=ALU.mult, op1=ALU.subtract))
                V.tensor_scalar(gt[:, 0:1], gt[:, 0:1], -1.0, 1e-5, ALU.mult, ALU.add)\
                    .then_inc(S(f"gn{which}_var"), 1)

            def group_apply(n, x, which):
                after(n, f"gn{which}_rstd")
                xv = x[:, :].rearrange("p (h w) -> p h w", h=H)
                for i in range(2):
                    for up in range(2):
                        dy, dx = (2, 2) if not up else (2, 1) if i == 0 else (1, 2)
                        r = slice(C * up, C * up + C)
                        a = V.tensor_scalar(img[i][r, dy:dy + H, dx:dx + W], xv[r], gm[r, 0:1], gt[r, 1:2],
                                            ALU.subtract, ALU.mult)
                if which == 1:
                    a = V.tensor_scalar(xg[:, :], x[:, :], gm[:, 0:1], gt[:, 1:2], ALU.subtract, ALU.mult)
                a.then_inc(S(f"gn{which}_done"), 1)

            def layer_stats(t, st_, mv_, which):
                for i in range(NT):
                    a = V.bn_stats(st_[:, i, :], t[:, i, :])
                link(a)
                for i in range(NT):
                    a = V.bn_aggr(mv_[:, i, :], st_[:, i, :])
                link(a)
                V.tensor_scalar(mv_[:, :, 1], mv_[:, :, 1], 1e-5, None, ALU.add).then_inc(S(f"ln{which}_var"), 1)

            def layer_apply(n, t, mv_, gv_, out, which):
                after(n, f"ln{which}_rstd")
                for i in range(NT):
                    a = V.tensor_scalar(out[:, i, :], t[:, i, :], mv_[:, i, 0:1], gv_[:, i:i + 1],
                                        ALU.subtract, ALU.mult)
                if which < 5:
                    a.then_inc(S(f"xn{which}"), 1)
                else:
                    link(a)

            def front(n, image):
                dve.wait_ge(S("x_loaded"), image * 32 + 32)
                group_stats(xin, 1)
                yield
                group_var(n, SB_, 1)
                yield
                group_apply(n, xin, 1)
                V.tensor_scalar(xs[:, :], xin[:, :], bnc[:, 3:4], None, ALU.add).then_inc(S("x_free"), 1)
                yield
                yield
                after(n, "conv5")
                link(V.tensor_scalar(q0[:, :], SA[:, T:2 * T], 0.0, None, ALU.max))
                V.tensor_copy(kv1[:, :], SA[:, 0:T]).then_inc(S("kv1_copied"), 1)
                yield
                yield
                after(n, "kv_sum")
                V.tensor_tensor(kvm[:, :], SB_[:, 0:P], cst("blk8"), ALU.mult)
                V.tensor_scalar(ksm[:, :], cst("blk8"), SB_[:, P:P + 1], None, ALU.mult)\
                    .then_inc(S("kv_masked"), 1)
                yield
                after(n, "lin_out")
                link(V.tensor_scalar(den0[:, :], SA[:, T:2 * T], 1e-15, None, ALU.add))
                link(V.reciprocal(rec0[:, :], den0[:, :]))
                V.tensor_tensor(o0[:, :], SA[:, 0:T], rec0[:, :], ALU.mult).then_inc(S("o0_ready"), 1)
                yield
                after(n, "proj0")
                link(V.scalar_tensor_tensor(out=x1[:, :], in0=SB_[:, 0:T], scalar=bnc[:, 2:3], in1=xs[:, :],
                                            op0=ALU.mult, op1=ALU.add))
                group_stats(x1, 2)
                yield
                group_var(n, SA, 2)
                yield
                group_apply(n, x1, 2)
                yield
                after(n, "conv3")
                V.tensor_tensor(x1[0:C, :], SB_[0:C, 0:T], x1[0:C, :], ALU.add).then_inc(S("x2"), 1)
                yield
                after(n, "x2_turned")
                link(V.tensor_copy(t1n[:, :, :], tok(SA)))
                layer_stats(t1n, st, mv, 1)
                yield
                layer_apply(n, t1n, mv, gv, xn, 1)
                yield
                yield
                after(n, "small")
                link(V.tensor_copy(sm[:, :, :], SB_[:, 0:NT * 68].rearrange("p (t c) -> p t c", t=NT)))
                dve.sem_inc(S("small_copied"), 1)
                for t in range(NT):
                    a = V.tensor_copy(sbc[:, t, :], sm[:, t, 67:68].broadcast_to((P, P)))
                a.then_inc(S("score_bc"), 1)
                after(n, "k_rope")
                V.tensor_tensor(k1n[C:P, :], SA[C:P, 0:T], cst("ktab")[C:P, :], ALU.mult)\
                    .then_inc(S("k_rotated"), 1)
                link(V.tensor_tensor(sq[:, :, :], sm[:, :, 0:64], sm[:, :, 0:64], ALU.mult))
                V.tensor_reduce(ms[:, 0, :], sq[:, :, 0:CQ], AX.X, ALU.add)
                link(V.tensor_reduce(ms[:, 1, :], sq[:, :, 32:32 + CKV], AX.X, ALU.add))
                V.tensor_scalar(ms[:, 0, :], ms[:, 0, :], 1.0 / CQ, 1e-6, ALU.mult, ALU.add)
                V.tensor_scalar(ms[:, 1, :], ms[:, 1, :], 1.0 / CKV, 1e-6, ALU.mult, ALU.add)\
                    .then_inc(S("rms_var"), 1)
                yield
                after(n, "gate_mean")
                link(V.tensor_copy(gl[:, :], SB_[:, 140:140 + BR]))
                dve.sem_inc(S("gate_read"), 1)
                link(V.tensor_reduce(gs[:, 3:4], gl[:, :], AX.X, ALU.max))
                V.tensor_scalar(gs[:, 4:5], gs[:, 3:4], -1.0, None, ALU.mult).then_inc(S("gate_max"), 1)
                after(n, "rms_rstd")
                V.tensor_tensor(cn[:, :, 0:CQ], sm[:, :, 0:CQ], rs[:, 0, :].unsqueeze(2).broadcast_to((P, NT, CQ)),
                                ALU.mult)
                V.tensor_tensor(cn[:, :, 32:64], sm[:, :, 32:64],
                                rs[:, 1, :].unsqueeze(2).broadcast_to((P, NT, CKV)), ALU.mult)\
                    .then_inc(S("cn_ready"), 1)
                after(n, "score_row")
                link(V.tensor_copy(srow[:, :], SA[:, 0:T]))
                for t in range(NT):
                    V.tensor_scalar(cmp_[:, t, :], srow[:, :], sm[:, t, 67:68], None, ALU.is_gt)
                    a = V.scalar_tensor_tensor(out=cmq_[:, t, :], in0=srow[:, :], scalar=sm[:, t, 67:68],
                                               in1=ties[:, t, :], op0=ALU.is_equal, op1=ALU.mult)
                link(a)
                link(V.tensor_tensor(cmp_[:, :, :], cmp_[:, :, :], cmq_[:, :, :], ALU.add))
                link(V.tensor_reduce(ranks[:, :], cmp_[:, :, :], AX.X, ALU.add))
                link(V.tensor_scalar(sel[:, :], ranks[:, :], float(KEEP), None, ALU.is_lt))
                V.tensor_scalar(gs[:, 7:8], sel[:, 0:1], float(T), None, ALU.mult).then_inc(S("selected"), 1)
                yield
                after(n, "gate_exp")
                link(V.tensor_reduce(gs[:, 5:6], gs[:, 0:BR], AX.X, ALU.add))
                link(V.reciprocal(gs[:, 6:7], gs[:, 5:6]))
                V.tensor_scalar(gate_next[:, :], gs[:, 0:BR], gs[:, 6:7], None, ALU.mult)
                after(n, "cnT")
                link(V.tensor_copy(k1n[32:64, :], cnT[32:64, :]))
                V.tensor_copy(k1b[:, :], k1n[:, :]).then_inc(S("k1b"), 1)
                yield
                after(n, "positions")
                link(V.tensor_copy(pos[:, :], SA[:, 0:2]))
                for t in range(NT):
                    a = V.tensor_scalar(pickm[:, t, :], cst("iota"), pos[:, t:t + 1], sel[:, t:t + 1],
                                        ALU.is_equal, ALU.mult)
                a.then_inc(S("pick_ready"), 1)
                yield
                yield

            def back_first(n, image):
                after(n, "attn_out")
                link(V.tensor_tensor(t2[:, :, :], tok(SA), t1[:, :, :], ALU.add))
                layer_stats(t2, st2, mv2, 2)

            def back(n, image):
                layer_apply(n, t2, mv2, gv2, xp, 2)
                yield
                yield
                after(n, "logits")
                link(V.tensor_reduce(c8[:, :, 0], SA[:, 0:NT * E].rearrange("p (t e) -> p t e", t=NT),
                                     AX.X, ALU.max))
                V.tensor_scalar(c8[:, :, 1], c8[:, :, 0], -1.0, None, ALU.mult).then_inc(S("logit_max"), 1)
                V.tensor_tensor(t2[:, :, :], t2[:, :, :], xp[:, :, :], ALU.add)
                yield
                dve.wait_ge(S("logit_exp"), image * 2 + 2)
                link(V.reciprocal(c8[:, :, 3], c8[:, :, 2]))
                link(V.tensor_tensor(pe8[:, :, :], pe8[:, :, :], c8[:, :, 3:4].broadcast_to((P, NT, E)), ALU.mult))
                for t in range(NT):
                    p_e = pe8[:, t, :].unsqueeze(2).broadcast_to((P, E, E))
                    p_j = pe8[:, t, :].unsqueeze(1).broadcast_to((P, E, E))
                    V.tensor_tensor(cg[:, t, :, :], p_j, p_e, ALU.is_gt)
                    a = V.tensor_tensor(ce[:, t, :, :], p_j, p_e, ALU.is_equal)
                link(a)
                link(V.tensor_tensor(ce[:, :, :, :], ce[:, :, :, :], first8.unsqueeze(1).broadcast_to((P, NT, E, E)),
                                     ALU.mult))
                link(V.tensor_tensor(cg[:, :, :, :], cg[:, :, :, :], ce[:, :, :, :], ALU.add))
                link(V.tensor_reduce(comb[:, :, :], cg[:, :, :, :], AX.X, ALU.add))
                link(V.scalar_tensor_tensor(out=comb[:, :, :], in0=comb[:, :, :], scalar=2.0, in1=pe8[:, :, :],
                                            op0=ALU.is_lt, op1=ALU.mult))
                link(V.tensor_reduce(c8[:, :, 4], comb[:, :, :], AX.X, ALU.add))
                link(V.tensor_scalar(c8[:, :, 5], c8[:, :, 4], 1e-12, None, ALU.max))
                link(V.reciprocal(c8[:, :, 6], c8[:, :, 5]))
                link(V.tensor_tensor(comb[:, :, :], comb[:, :, :], c8[:, :, 6:7].broadcast_to((P, NT, E)), ALU.mult))
                yield
                for t in range(NT):
                    dve.wait_ge(S("expert_out"), image * 2 + t + 1)
                    V.tensor_tensor(yb[:, t, :, :].rearrange("p e c -> p (e c)"), (SA, SC)[t][:, :], cst("b2"),
                                    ALU.add).then_inc(S("y_biased"), 1)
                yield
                dve.wait_ge(S("y_weighted"), image * 2 + 2)
                for t in range(NT):
                    a = V.tensor_reduce(ysum[:, t, :], yb[:, t, :, :].rearrange("p e c -> p c e"), AX.X, ALU.add)
                link(a)
                link(V.tensor_tensor(t3[:, :, :], t2[:, :, :], ysum[:, :, :], ALU.add))
                layer_stats(t3, st2, mv2, 3)
                yield
                layer_apply(n, t3, mv2, gv2, xp, 3)
                yield
                yield
                after(n, "qkv3")
                kvp = SB_[:, :].rearrange("p (g d) -> p g d", d=16)
                k3 = kv3[:, :, :, :].rearrange("p t g d -> p (t g) d")
                kq = kvq[:, :, :, :].rearrange("p t g d -> p (t g) d")
                bc = lambda i: n3[:, i, :].unsqueeze(2).broadcast_to((P, NT * 16, 16))
                link(V.tensor_reduce(n3[:, 0, :], kvp, AX.X, ALU.add))
                link(V.tensor_scalar(n3[:, 0, :], n3[:, 0, :], 1.0 / 16, None, ALU.mult))
                link(V.tensor_tensor(k3, kvp, bc(0), ALU.subtract))
                link(V.tensor_tensor(kq, k3, k3, ALU.mult))
                link(V.tensor_reduce(n3[:, 1, :], kq, AX.X, ALU.add))
                V.tensor_scalar(n3[:, 1, :], n3[:, 1, :], 1.0 / 16, 1e-5, ALU.mult, ALU.add)\
                    .then_inc(S("n3_var"), 1)
                yield
                link(V.tensor_tensor(t3[:, :, :], t3[:, :, :], cst("bout").unsqueeze(1).broadcast_to((P, NT, C)),
                                     ALU.add))
                after(n, "n3_rstd")
                V.tensor_tensor(kq, k3, bc(2), ALU.mult).then_inc(S("kv3_normed"), 1)
                yield
                after(n, "dots")
                V.tensor_tensor(dT[:, :], SA[:, 0:P], cst("blk16"), ALU.mult).then_inc(S("dots_masked"), 1)
                yield
                after(n, "dots_out")
                V.tensor_copy(m3[:, :], SA[:, P:P + C]).then_inc(S("m3"), 1)
                yield
                after(n, "attn3")
                link(V.tensor_tensor(t4[:, :, :], tok(SB_), t3[:, :, :], ALU.add))
                layer_stats(t4, st2, mv2, 4)
                yield
                layer_apply(n, t4, mv2, gv2, x4, 4)
                V.tensor_copy(all_t4[:, image, :, :], t4[:, :, :])
                dve.wait_ge(S("xn4"), n)
                link(V.tensor_copy(all_x4[:, image, :, :], x4[:, :, :]))
                yield
                yield

            def step(image, nxt, prev):
                restart()

                def side():
                    if prev is not None:
                        back_first(prev + 1, prev)
                    if image is not None:
                        link(V.tensor_copy(t1[:, :, :], t1n[:, :, :]))
                    if nxt is not None:
                        yield from front(nxt + 1, nxt)
                    if prev is not None:
                        yield from back(prev + 1, prev)

                def heads_(u, kind, k):
                    mxb = mx[:, :, :].rearrange("p t (r h) -> p t r h", r=BR)
                    src = heads[u % 2]
                    if kind in ("q", "kw", "ks"):
                        dve.wait_ge(S("unit_full"), nxt * UNITS + u + 1)
                        if kind == "q" and image is not None:
                            dve.wait_ge(S("scores"), image * SCORE_UNITS + 4 * k + 4)
                        dst, tab, w_ = {"q": (qT, "qtab", T), "kw": (kwT, "ktab", T), "ks": (ksT, "ktab", P)}[kind]
                        link(V.tensor_tensor(dst[:, 2 * k:2 * k + 2, :],
                                             src[:, 0:2 * w_].rearrange("p (h t) -> p h t", h=2),
                                             cst(tab)[:, 0:w_].unsqueeze(1).broadcast_to((P, 2, w_)), ALU.mult))
                        dve.sem_inc(S("unit_free"), 1)
                        dve.sem_inc(S("heads_ready"), 1)
                    elif kind in MAX_PARTS:
                        dve.wait_ge(S("unit_full"), nxt * UNITS + u + 1)
                        for qt, br, at, key0, keys in MAX_PARTS[kind]:
                            a = V.tensor_reduce(mxb[:, qt, br, 2 * k:2 * k + 2],
                                                src[:, at:at + 2 * keys].rearrange("p (h t) -> p h t", h=2),
                                                AX.X, ALU.max)
                        a.then_inc(S("unit_free"), 1)
                        if kind == "max3" and k == PAIRS - 1:
                            dve.wait_ge(S("unit_free"), nxt * UNITS + u + 1)
                            link(V.tensor_scalar(mh[:, :, 0:HB], mx[:, :, :], -1.0, None, ALU.mult))
                            V.scalar_tensor_tensor(out=mh[:, :, HB:2 * HB], in0=mx[:, :, :], scalar=-1.0,
                                                   in1=mh[:, :, 0:HB], op0=ALU.mult, op1=ALU.subtract)\
                                .then_inc(S("mh_ready"), 1)

                def main(r):
                    if r == 0:
                        if starts(image, -1):
                            dve.wait_ge(S("scores"), image * SCORE_UNITS)
                        V.tensor_copy(k1T[:, :], k1n[:, :]).then_inc(S("k1T_taken"), 1)
                        if starts(image, -1):
                            dve.wait_ge(S("branch_out"), image * 12)
                        link(V.tensor_copy(gate[:, :], gate_next[:, :]))
                    if r in WEIGH_ROUNDS:
                        u = WEIGH_ROUNDS.index(r)
                        g, br = u // 3, u % 3
                        dve.wait_ge(S("weighed"), image * 12 + u + 1)
                        if br == 0 and (g >= 2 or starts(image, -1)):
                            dve.wait_ge(S("o_summed"), image * 4 + g - 1)
                        link(V.reciprocal(rden[:, :], PV[:, T:2 * T]))
                        V.scalar_tensor_tensor(out=ob[:, g % 2, br, :], in0=PV[:, 0:T],
                                               scalar=gate[:, br:br + 1], in1=rden[:, :],
                                               op0=ALU.mult, op1=ALU.mult).then_inc(S("branch_out"), 1)

                rounds(main if image is not None else None, heads_ if nxt is not None else None, side())
                if image is not None and nxt is None:
                    dve.sem_inc(S("attention_done"), 1)

            run(dve, step)

            dve.wait_ge(S("final"), 16)
            restart()
            V.memset(x4c, 0.0)
            R = slice(0, B)
            dve.wait_ge(S("route_logits"), 1)
            link(V.tensor_tensor(lr[R, :], SB_[R, 0:E], cst("br3")[R, :], ALU.add))
            link(V.tensor_reduce(rt[R, 0:1], lr[R, :], AX.X, ALU.max))
            V.tensor_scalar(rt[R, 1:2], rt[R, 0:1], -1.0, None, ALU.mult).then_inc(S("route_max"), 1)
            dve.wait_ge(S("route_exp"), 1)
            link(V.reciprocal(rt[R, 3:4], rt[R, 2:3]))
            V.tensor_scalar(rw[R, :], rw[R, :], rt[R, 3:4], None, ALU.mult).then_inc(S("route1"), 1)
            dve.wait_ge(S("route_load"), 1)
            capacity = float(-(-B * T * 5 // (4 * E)))
            link(V.tensor_scalar(load[R, :], SB_[R, 16:16 + E], float(T) * T, None, ALU.mult))
            link(V.tensor_scalar(r8[R, 0, :], load[R, :], capacity, None, ALU.max))
            link(V.reciprocal(r8[R, 1, :], r8[R, 0, :]))
            link(V.scalar_tensor_tensor(out=rw[R, :], in0=rw[R, :], scalar=capacity, in1=r8[R, 1, :],
                                        op0=ALU.mult, op1=ALU.mult))
            link(V.tensor_reduce(rt[R, 4:5], rw[R, :], AX.X, ALU.max))
            V.tensor_scalar(rt[R, 5:6], rt[R, 4:5], -1.0, None, ALU.mult).then_inc(S("route_max"), 1)
            dve.wait_ge(S("route_exp"), 2)
            link(V.reciprocal(rt[R, 7:8], rt[R, 6:7]))
            link(V.tensor_scalar(lr[R, :], lr[R, :], rt[R, 7:8], None, ALU.mult))
            p_e = lr[R, :].unsqueeze(2).broadcast_to((B, E, E))
            p_j = lr[R, :].unsqueeze(1).broadcast_to((B, E, E))
            V.tensor_tensor(r8[R], p_j, p_e, ALU.is_gt)
            link(V.tensor_tensor(r8b[R], p_j, p_e, ALU.is_equal))
            link(V.tensor_tensor(r8b[R], r8b[R], first8[R], ALU.mult))
            link(V.tensor_tensor(r8[R], r8[R], r8b[R], ALU.add))
            link(V.tensor_reduce(load[R, :], r8[R], AX.X, ALU.add))
            link(V.tensor_scalar(load[R, :], load[R, :], 2.0, None, ALU.is_lt))
            link(V.tensor_reduce(rt[R, 8:9], lr[R, :], AX.X, ALU.max))
            V.tensor_scalar(rt[R, 9:10], rt[R, 8:9], -1.0, None, ALU.mult).then_inc(S("route_max"), 1)
            dve.wait_ge(S("route_exp"), 3)
            link(V.tensor_tensor(rw[R, :], rw[R, :], load[R, :], ALU.mult))
            link(V.tensor_reduce(rt[R, 10:11], rw[R, :], AX.X, ALU.add))
            link(V.reciprocal(rt[R, 11:12], rt[R, 10:11]))
            link(V.tensor_scalar(rw[R, :], rw[R, :], rt[R, 11:12], float(T), ALU.mult, ALU.mult))
            V.tensor_tensor(wdiag[R], rw[R, :].unsqueeze(1).broadcast_to((B, B, E)),
                            ident[R, 0:B].unsqueeze(2).broadcast_to((B, B, E)), ALU.mult).then_inc(S("route2"), 1)
            dve.wait_ge(S("route_bc"), 1)
            link(V.tensor_copy(wd[:, :, :], SA[:, 0:B * E].rearrange("p (b e) -> p b e", b=B)))

            with dve.Fori(0, B) as b:
                restart()
                n = dve.snap(b + 1)
                V.tensor_copy(x4[:, :, :], all_x4[:, b, :, :]).then_inc(S("x4_fetched"), 1)
                link(V.tensor_copy(c8[:, 0, :], wd[:, b, :]))
                V.tensor_tensor(w2s[:, :, :], f2, c8[:, 0, :].unsqueeze(2).broadcast_to((P, E, C)), ALU.mult)
                link(V.tensor_tensor(c8[0:E, 1, :], c8[0:E, 0, :], ident[0:E, 0:E], ALU.mult))
                link(V.tensor_reduce(rt[0:E, 0:1], c8[0:E, 1, :], AX.X, ALU.add))
                link(V.tensor_scalar(fb2s[0:E, :], cst("fb2")[0:E, :], rt[0:E, 0:1], float(T), ALU.mult, ALU.mult))
                dve.sem_inc(S("f_in"), 1)
                dve.wait_ge(S("f_out"), n)
                link(V.tensor_tensor(yf[:, :, :], tok(SB_), all_x4[:, b, :, :], ALU.add))
                layer_stats(yf, st, mv, 5)
                layer_apply(n, yf, mv, gv, yo, 5)
                link(V.tensor_tensor(yo[:, :, :], yo[:, :, :], cst("gamma").unsqueeze(1).broadcast_to((P, NT, C)),
                                     ALU.mult))
                link(V.tensor_tensor(yo[:, :, :], yo[:, :, :], cst("beta").unsqueeze(1).broadcast_to((P, NT, C)),
                                     ALU.add))
                V.tensor_tensor(tf[:, :, :], yo[:, :, :], all_t4[:, b, :, :], ALU.add).then_inc(S("tf_ready"), 1)
                dve.wait_ge(S("y_copied"), n)


def _shape_constants():
    f = np.float32
    i, j = np.arange(P)[:, None], np.arange(P)[None, :]
    k = {}
    k["ident"] = (i == j).astype(f)
    k["pairmean"] = 0.5 * (i // 2 == j // 2).astype(f)
    k["blk8"] = (i // 8 == j // 8).astype(f)
    k["blk16"] = (i // 16 == j // 16).astype(f) / T
    k["before"] = (i < j).astype(f)
    k["iota"] = np.broadcast_to(j, (P, P)).astype(f)
    key = np.arange(T)[None, :]
    k["ties"] = np.concatenate([(key < i + P * t).astype(f) for t in range(NT)], 1)
    e = np.arange(E)
    k["first8"] = np.broadcast_to((e[None, :] < e[:, None]).astype(f).reshape(1, E * E), (P, E * E))
    freq = 1.0 / 10000.0 ** (np.arange(0, ROPE, 2, dtype=f) / ROPE)
    ang = np.outer(np.arange(T, dtype=f), freq)
    cos, sin = np.cos(ang).T.astype(f), np.sin(ang).T.astype(f)
    c16, s16 = np.concatenate([cos, cos]), np.concatenate([-sin, sin])
    ones = np.ones((64, T), f)
    k["qtab"] = np.concatenate([ones, c16, c16, s16, s16])
    k["ktab"] = np.concatenate([ones, c16, s16, c16, s16])
    m = {"identb": (i == j).astype(f)}
    neg = lambda ok: np.where(ok, 0.0, NEG).astype(f)
    m["causal_s"] = neg(i >= j)
    m["causal_t"] = neg(j >= i)
    m["band_s"] = neg((i >= j) & (i - j < WINDOW))
    m["band_t"] = neg((j >= i) & (j - i < WINDOW))
    w = np.arange(BAND)[None, :]
    m["band_s1"] = neg((i + WINDOW >= w) & (i + WINDOW - w < WINDOW))
    m["band_t0"] = neg((w >= i) & (w - i < WINDOW))
    r = np.arange(HB)[None, :]
    m["pick"] = ((i == r) | (i == r + HB)).astype(f)
    return k, m


def _pack(table, parts):
    out = np.zeros((P, sum(table.values())), np.float32)
    at = 0
    for name, n in table.items():
        a = np.asarray(parts[name])
        out[:a.shape[0], at:at + n] = a.reshape(a.shape[0], n)
        at += n
    return out


def _swap(a):
    n = a.shape[-1] // 2
    return np.concatenate([a[..., n:], a[..., :n]], -1)


def _lay_out(x):
    z = lambda *s: np.zeros(s, np.float32)
    p, m = _shape_constants()
    order = np.arange(192).reshape(8, 3, 8).transpose(1, 0, 2).reshape(192)
    wi = x["L0_conv_w_qkv"].reshape(192, C)[order]
    dw = x["L0_conv_w_dw"].reshape(192, 5, 5)[order]
    pw = x["L0_conv_w_pw"].reshape(192, 8)[order]
    dwp = z(192, 26)
    for i, pair in enumerate(PAIRS5):
        dwp[:, 2 * i] = dw[:, pair[1], pair[2]]
        two = second_tap(pair, 5)
        if two:
            dwp[:, 2 * i + 1] = dw[:, two[0], two[1]]
    blocks = z(192, 192)
    for g in range(24):
        blocks[8 * g:8 * g + 8, 8 * g:8 * g + 8] = pw[8 * g:8 * g + 8].T
    p["w_q0"], p["w_kv0"] = wi[:64].T, wi[64:].T
    p["dw_q"], p["dw_kv"] = dwp[:64], dwp[64:]
    p["wi_q"], p["wi_kv"] = wi[:64], wi[64:]
    p["pw_q"], p["pw_kv"] = blocks[:64, :64], blocks[64:, 64:]
    wp = x["L0_conv_w_proj"].reshape(C, P).T
    p["proj0"] = np.concatenate([wp, wp], 1)
    bn = np.stack([x["L0_conv_bn_" + s] for s in ("gamma", "beta", "mean", "var")], 1)
    p["bn"] = np.concatenate([bn, bn], 0)
    w9 = x["L1_conv_weight"]
    conv1 = z(P, 5, C)
    for i, pair in enumerate(PAIRS3):
        conv1[:C, i] = w9[:, :, pair[1], pair[2]].T
        two = second_tap(pair, 3)
        if two:
            conv1[C:, i] = w9[:, :, two[0], two[1]].T
    p["conv1"] = conv1
    small = z(C, 68)
    small[:, 0:CQ], small[:, 32:64] = x["L2_attn_Wcq"], x["L2_attn_Wckv"]
    small[:, 64:67], small[:, 67:68] = x["L2_attn_Wgate"], x["L2_attn_W_imp"]
    p["w_small"] = small
    kr = x["L2_attn_Wk_rope"]
    p["w_kr"] = np.concatenate([z(C, 64), kr, _swap(kr), kr, _swap(kr)], 1)
    nw = z(P, 1)
    nw[0:CQ, 0], nw[32:64, 0] = x["L2_attn_q_norm_w"], x["L2_attn_kv_norm_w"]
    p["nw"] = nw
    qn = x["L2_attn_Wq_nope"].reshape(CQ, HEADS, NOPE)
    kn = x["L2_attn_Wk_nope"].reshape(CKV, HEADS, NOPE)
    p["wqn_t"], p["wkn_t"] = qn.transpose(2, 1, 0), kn.transpose(2, 1, 0)
    qr = x["L2_attn_Wq_rope"].reshape(CQ, HEADS, ROPE)
    p["w_q"] = np.concatenate([qn, z(CQ, HEADS, 32), qr, qr, _swap(qr), _swap(qr)], 2)
    wv1 = z(64, 512)
    wv1[32:64] = x["L2_attn_Wv"]
    p["w_v1"], p["w_v"] = wv1, np.concatenate([x["L2_attn_Wwin_v"], x["L2_attn_Wsel_v"]])
    k = np.concatenate([x["L2_attn_Wwin_k"], x["L2_attn_Wsel_k"]]).reshape(P, HEADS, HD)
    r = k[:, :, NOPE:]
    p["w_k"] = np.concatenate([k[:, :, :NOPE], z(P, HEADS, 32), r, _swap(r), r, _swap(r)], 2)
    p["w_p"] = x["L2_attn_Wproj"].reshape(4, P, C).transpose(1, 0, 2)
    p["r2"] = x["L2_ffn_router_w"].T
    p["w1"] = x["L2_ffn_w1"].transpose(1, 0, 2)
    p["b1"] = x["L2_ffn_b1"].reshape(4, P).T
    w2 = z(P, 4, 2, C)
    for e in range(E):
        w2[(e % 2) * C:(e % 2 + 1) * C, e // 2, e % 2] = x["L2_ffn_w2"][e]
    p["w2"] = w2
    p["b2"] = np.broadcast_to(x["L2_ffn_b2"].reshape(1, E * C), (P, E * C))
    wq = x["L3_attn_w_qkv"]
    p["q3"], p["kv3"], p["out3"] = wq[:, :P], wq[:, P:], x["L3_attn_w_out"]
    p["bout"] = np.broadcast_to(x["L3_attn_b_out"][None], (P, C))
    p["r3"] = x["L3_ffn_Wr"]
    p["br3"] = np.broadcast_to(x["L3_ffn_br"][None], (P, E))
    p["f1"] = x["L3_ffn_W1"].transpose(1, 0, 2)
    p["fb1"] = x["L3_ffn_b1"].T
    p["f2"] = x["L3_ffn_W2"].transpose(1, 0, 2)
    p["fb2"] = x["L3_ffn_b2"]
    p["gamma"] = np.broadcast_to(x["L3_ffn_gamma"][None], (P, C))
    p["beta"] = np.broadcast_to(x["L3_ffn_beta"][None], (P, C))
    return {
        "x": x["x"].reshape(B, C, T),
        "prep": _pack(PREP, p),
        "early": _pack(EARLY, p),
        "late": _pack(LATE, p),
        "masks": _pack(MASKS, m),
        "final": _pack(FINAL, p),
    }


def kernel(**inputs):
    import concourse.bacc as _bacc
    from concourse.bass_utils import run_bass_kernel_spmd as _run

    arrays = _lay_out({k: np.asarray(v) for k, v in inputs.items()})
    arrays = {k: np.ascontiguousarray(v) for k, v in arrays.items()}
    nc = _bacc.Bacc("TRN2", target_bir_lowering=False, num_devices=1)
    args = [nc.dram_tensor("in_" + k, v.shape, mybir.dt.from_np(v.dtype), kind="ExternalInput").ap()
            for k, v in arrays.items()]
    args.append(nc.dram_tensor("y", (B, C, T), F32, kind="ExternalOutput").ap())
    build(nc, *args)
    r = _run(nc, [{"in_" + k: v for k, v in arrays.items()}], core_ids=[0])
    return r.results[0]["y"].reshape(B, C, H, W)
```

```python
from contextlib import ExitStack

import numpy as np

import concourse.bass as bass
from concourse import mybir

ALU = mybir.AluOpType
ACT = mybir.ActivationFunctionType
AX = mybir.AxisListType
F32 = mybir.dt.float32
BF16 = mybir.dt.bfloat16

P = 128
B, C, H, W = 8, 64, 16, 16
T = H * W
NT = T // P
PITCH = 20
HEADS, NOPE, ROPE, VDIM = 16, 32, 16, 32
CQ, CKV = 24, 32
HD = NOPE + ROPE
KEEP, WINDOW = 128, 32
NEG = -1.0e9
E, DE = 8, 64
FF = 128
BR = 3
HB = HEADS * BR
BAND = P + WINDOW
SCALE = 1.0 / float(np.sqrt(np.float32(HD)))

PAIRS5 = [(0, dy, dx) for dy in range(5) for dx in (0, 2)] + [(1, 0, 4), (1, 2, 4), (0, 4, 4)]
PAIRS3 = [(0, dy, 0) for dy in range(3)] + [(1, 0, 2), (0, 2, 2)]


def second_tap(pair, size):
    copy, dy, dx = pair
    dy, dx = (dy, dx + 1) if copy == 0 else (dy + 1, dx)
    return (dy, dx) if dy < size and dx < size else None


PREP = dict(dw_kv=26, dw_q=26, wi_kv=64, wi_q=64, pw_kv=128, pw_q=64, conv1=5 * 64, wqn_t=HEADS * CQ,
            wkn_t=HEADS * CKV)
EARLY = dict(pairmean=128, w_q0=64, w_kv0=128, proj0=128, bn=4, blk8=128, ident=128)
LATE = dict(w_small=68, w_kr=128, nw=1, w_q=HEADS * 128, w_v1=512, w_v=512, w_p=4 * 64, w_k=HEADS * 128,
            qtab=T, ktab=T, before=128, iota=128, ties=2 * T, first8=64,
            r2=E, w1=4 * 128, b1=4, w2=4 * 128, b2=E * C,
            q3=128, kv3=256, out3=64, bout=64, blk16=128, r3=E, br3=E)
FINAL = dict(f1=E * FF, fb1=E, f2=E * C, fb2=C, gamma=C, beta=C)
MASKS = dict(identb=128, causal_s=128, causal_t=128, band_s=128, band_t=128, band_s1=BAND, band_t0=BAND,
             pick=HB)


def offsets(table):
    at, out = 0, {}
    for name, n in table.items():
        out[name] = (at, n)
        at += n
    return out, at


def build(nc, x_in, prep_in, early_in, late_in, masks_in, final_in, y_out):
    ctx = ExitStack()
    with ctx:
        def sb(name, shape, dt=F32):
            return ctx.enter_context(nc.sbuf_tensor(name, shape, dt))

        sems = {}

        def S(name):
            if name not in sems:
                sems[name] = ctx.enter_context(nc.semaphore("s_" + name))
            return sems[name]

        eo, en = offsets(EARLY)
        lo, ln = offsets(LATE)
        mo, mn = offsets(MASKS)
        early = sb("early", [P, en])
        late = sb("late", [P, ln])
        masks = sb("masks", [P, mn], BF16)

        po, pn = offsets(PREP)
        fo, fn = offsets(FINAL)
        pr = sb("pr", [P, 2, 2, 1856])
        kwT = sb("kwT", [P, HEADS, T])
        prep = pr[:, 1, :, :].rearrange("p a n -> p (a n)")[:, 0:pn]
        masks32 = kwT[:, :, :].rearrange("p h t -> p (h t)")[:, 0:mn]
        final = kwT[:, :, :].rearrange("p h t -> p (h t)")[:, 0:fn]

        def cst(name):
            for table, tile in ((eo, early), (lo, late), (mo, masks), (po, prep), (fo, final)):
                if name in table:
                    a, n = table[name]
                    return tile[:, a:a + n]

        ident, identb = cst("ident"), cst("identb")
        w_q = cst("w_q").rearrange("p (h m) -> p h m", h=HEADS)
        w_k = cst("w_k").rearrange("p (h m) -> p h m", h=HEADS)
        w_p = cst("w_p").rearrange("p (g m) -> p g m", g=4)
        w1 = cst("w1").rearrange("p (g m) -> p g m", g=4)
        w2 = cst("w2").rearrange("p (g m) -> p g m", g=4)
        f1 = cst("f1").rearrange("p (e m) -> p e m", e=E)
        f2 = cst("f2").rearrange("p (e m) -> p e m", e=E)
        ties = cst("ties").rearrange("p (t m) -> p t m", t=NT)
        first8 = cst("first8").rearrange("p (e j) -> p e j", e=E)
        conv1 = cst("conv1").rearrange("p (n m) -> p n m", n=len(PAIRS3))
        dw_kv, dw_q = cst("dw_kv"), cst("dw_q")
        pick = cst("pick")
        wqn_t = cst("wqn_t").rearrange("p (h m) -> p h m", h=HEADS)
        wkn_t = cst("wkn_t").rearrange("p (h m) -> p h m", h=HEADS)

        wc_kv = sb("wc_kv", [P, 13, P])
        wc_q = sb("wc_q", [P, 13, C])
        bin1 = sb("bin1", [P, 5, C])
        binn = sb("binn", [P, 5, C])
        bnc = sb("bnc", [P, 4])
        half = sb("half", [P, 1])
        onesk = sb("onesk", [P, 32])
        meank = sb("meank", [P, P])

        xin = sb("xin", [P, T])
        keep5 = sb("keep5", [P, 5, T])
        xs, xg, kv1, q0, o0 = [keep5[:, i, :] for i in range(5)]
        kept = [keep5[:, 0:2, :], keep5[:, 2:4, :], keep5[:, 4, :].rearrange("p (h t) -> p h t", h=2)]
        img = [sb(f"img{i}", [P, PITCH, PITCH]) for i in range(2)]
        st = sb("st", [P, 2, 6])
        st2 = sb("st2", [P, 2, 6])
        mv2 = sb("mv2", [P, 2, 2])
        gv2 = sb("gv2", [P, 2])
        mv = sb("mv", [P, 2, 2])
        gm = sb("gm", [P, 2])
        gv = sb("gv", [P, 2])
        gt = sb("gt", [P, 2])
        ktok = sb("ktok", [P, NT, P])
        vtok = sb("vtok", [P, NT, P + 1])
        kvm = sb("kvm", [P, P])
        ksm = sb("ksm", [P, P])
        den0, rec0 = xg, kv1
        x1 = sb("x1", [P, T])
        t1n = sb("t1n", [P, NT, C])
        xn = sb("xn", [P, NT, C])
        xnT = sb("xnT", [P, T])
        sm = sb("sm", [P, NT, 68])
        sq = sb("sq", [P, NT, 64])
        ms = sb("ms", [P, 2, NT])
        rs = sb("rs", [P, 2, NT])
        cn = sb("cn", [P, NT, 64])
        cnT = sb("cnT", [P, T])
        gl = sb("gl", [P, BR])
        gs = sb("gs", [P, 8])
        gate = sb("gate", [P, BR])
        all_gates = sb("all_gates", [P, B, BR])
        k1n = sb("k1n", [P, T])
        k1h = sb("k1h", [P, T])
        cnH = sb("cnH", [P, T])
        xnH = sb("xnH", [P, T])
        selH = sb("selH", [P, KEEP])
        xp = sb("xp", [P, NT, C])
        xpT = sb("xpT", [P, T])
        sbc = sb("sbc", [P, NT, P])
        ranks = sb("ranks", [P, NT])
        sel = sb("sel", [P, NT])
        pos = sb("pos", [P, NT])
        pickm = sb("pickm", [P, NT, KEEP])
        selT = sb("selT", [P, KEEP])
        k1T = sb("k1T", [P, T])
        qT = sb("qT", [P, HEADS, T])
        ksT = sb("ksT", [P, HEADS, KEEP])
        k1b = sb("k1b", [P, T], BF16)
        qb = sb("qb", [P, 2, 2, T], BF16)
        kwb = sb("kwb", [P, 2, 2, T], BF16)
        ksb = sb("ksb", [P, 2, 2, KEEP], BF16)
        v1 = sb("v1", [P, NT, HEADS * VDIM])
        vw = sb("vw", [P, NT, HEADS * VDIM])
        vs = sb("vs", [P, HEADS * VDIM])
        mx = sb("mx", [P, NT, HB])
        mh = sb("mh", [P, NT, P], BF16)
        mT = sb("mT", [P, T], BF16)
        scaled = pr[:, 0, 0, 0:26 * C].rearrange("p (n c) -> p n c", n=26)
        scaled_q = pr[0:C, 0, 1, 0:26 * C].rearrange("p (n c) -> p n c", n=26)
        rden = sb("rden", [P, T])
        ob = sb("ob", [P, 2, BR, T])
        oT = sb("oT", [P, 4, T])
        t2 = sb("t2", [P, NT, C])
        pe8 = sb("pe8", [P, NT, E])
        c8 = sb("c8", [P, NT, 8])
        cg = sb("cg", [P, NT, E, E])
        ce = sb("ce", [P, NT, E, E])
        comb = sb("comb", [P, NT, E])
        hm = sb("hm", [P, 4, T])
        cmp_, cmq_ = hm[:, 0:NT, :], hm[:, NT:2 * NT, :]
        yb = sb("yb", [P, NT, E, C])
        ysum = sb("ysum", [P, NT, C])
        t3 = sb("t3", [P, NT, C])
        q3 = sb("q3", [P, T])
        srow = q3
        kv3 = sb("kv3s", [P, NT, 16, 16])
        kvq = sb("kvq", [P, NT, 16, 16])
        n3 = sb("n3", [P, 4, NT * 16])
        dT = sb("dT", [P, P])
        m3 = sb("m3", [P, C])
        t4 = sb("t4", [P, NT, C])
        x4 = sb("x4", [P, NT, C])
        all_t4 = sb("all_t4", [P, B, NT, C])
        all_x4 = sb("all_x4", [P, B, NT, C])
        xbar = sb("xbar", [P, B])
        lr = sb("lr", [P, E])
        rw = sb("rw", [P, E])
        rt = sb("rt", [P, 12])
        load = sb("load", [P, E])
        r8 = sb("r8", [P, E, E])
        r8b = sb("r8b", [P, E, E])
        wd = sb("wd", [P, B, E])
        wdiag = sb("wdiag", [P, B, E])
        ksf = ksT[:, :, :].rearrange("p h t -> p (h t)")
        x4c = [ksf[:, i * T:(i + 1) * T] for i in range(2)]
        w2s = [ksf[:, 2 * T + i * E * C:2 * T + (i + 1) * E * C].rearrange("p (e c) -> p e c", e=E) for i in range(2)]
        fb2s = [sb(f"fb2s{i}", [P, C]) for i in range(2)]
        hf = [qT[:, i * E:(i + 1) * E, :] for i in range(2)]
        x4s = [x4, xp]
        obf = ob[:, :, :, :].rearrange("p g r t -> p (g r t)")
        yf, yo, *tf = [obf[:, i * NT * C:(i + 1) * NT * C].rearrange("p (t c) -> p t c", t=NT) for i in range(4)]
        y_cm = obf[:, 4 * NT * C + 2 * T:4 * NT * C + 3 * T]
        yc = [obf[0:C, 4 * NT * C + i * T:4 * NT * C + (i + 1) * T] for i in range(2)]

        def bank(name):
            return ctx.enter_context(nc.psum_tensor(name, [P, 512], F32))

        ring = [bank("ring0"), bank("ring1")]
        PV = bank("pv")
        heads = [bank("heads0"), bank("heads1")]
        SA, SB_, SC = bank("side_a"), bank("side_b"), bank("side_c")

        def window(i, dy, dx):
            return img[i][:, dy:dy + H, dx:dx + W]

        PAIRS = HEADS // 2
        PAIR_UNITS = 7
        VALUES = [("v1", 0), ("v1", 1), ("vw", 0), ("vw", 1), ("vs", 0)]
        UNITS = PAIR_UNITS * PAIRS + len(VALUES) + 1

        MAX_OUT = {"max0": (0, HEADS, 2, P), "max1": (HB, HEADS, 1, T), "max2": (2 * HEADS, 2 * HEADS, 2, P),
                   "max3": (HB + 2 * HEADS, HEADS, 1, BAND)}
        MAX_OF = {"max0": ("q", "ks"), "max1": ("q",), "max2": ("q", "ks", "kw"), "max3": ("q", "kw")}
        MAX_PARTS = {"max0": [(0, 0, 0, 0, P), (0, 1, 2 * P, 0, P)], "max1": [(1, 0, 0, 0, T)],
                     "max2": [(0, 2, 0, 0, P), (1, 1, 2 * P, 0, P)], "max3": [(1, 2, 0, T - BAND, BAND)]}

        SCORE_UNITS = 4 * PAIRS
        WEIGH_AT = {8 * g + 8 + d: 3 * g + i for g in range(4) for i, d in enumerate((1, 3, 5))}
        OUT_ROUND = 3
        ROUNDS = 35
        SIDE_STAGES = (2, 1, 0, 1, 2, 1, 1, 1, 1, 1, 1, 1, 1, 1, 1, 1, 1, 1, 1, 1, 2, 1, 1, 1,
                       1, 1, 1, 1, 1, 1, 1, 1, 1, 0, 1)
        PE_ORDER, DVE_ORDER, ACT_ORDER, POOL_ORDER = 'auws', 'usw', 'aus', 'ws'
        HEAD_UNITS = UNITS - len(VALUES)
        at_round = {}
        for r_, value in zip((0, 2, 3, 3, 3), VALUES):
            at_round.setdefault(r_, []).append(value)
        HEADS_AT = (4, 8, 12, 16, 20, 24, 28, 26)
        HEADS_AFTER = (dict(q=0, kw=0, ks=0, max1=2, max0=2, max3=3, max2=3),
                       dict(q=0, kw=0, ks=0, max1=1, max0=1, max3=3, max2=3))
        KEPT = PAIRS - 1
        PAIR_ORDER = sorted(range(PAIRS), key=lambda k: HEADS_AT[k])
        slot = {k: i % 2 for i, k in enumerate(PAIR_ORDER)}
        for k in PAIR_ORDER:
            for kind, d in HEADS_AFTER[k % 2].items():
                at_round.setdefault(HEADS_AT[k] + d, []).append((kind, k))
        at_round.setdefault(33, []).append(("turn", 0))
        in_order = [u for r_ in sorted(at_round) for u in at_round[r_] if u[0] in ("q", "kw", "ks")]
        made = {u: i + 1 for i, u in enumerate(in_order)}
        FIRST_UNIT = in_order[0]
        unit_plan, unit_at = [], 0
        for r_ in range(ROUNDS):
            for kind, k in at_round.get(r_, []):
                value = (kind, k) in VALUES
                unit_plan.append((r_, HEAD_UNITS + unit_at if value else unit_at - len(VALUES), kind, k))
                unit_at += 1
        unit_plan = [[u[1:] for u in unit_plan if u[0] == r_] for r_ in range(ROUNDS)]
        assert unit_at == UNITS
        maxima_done = {k: u for units_ in unit_plan for u, kind, k in units_ if kind in MAX_PARTS}
        filling = [u for units_ in unit_plan for u in units_ if u[0] < HEAD_UNITS]
        FILL_ROUNDS = 16
        filling_plan = [[u for i, u in enumerate(filling) if i * FILL_ROUNDS // len(filling) == r_]
                        for r_ in range(ROUNDS)]

        def starts(image, n):
            return n >= 0 or type(image) is not int or image > 0

        block = ctx.enter_context(nc.Block())

        def run(eng, step):
            step(0, None, None, None)
            step(1, 0, None, None)
            step(2, 1, 0, None)
            with eng.Fori(1, B - 2) as j:
                step(eng.snap(j + 2), eng.snap(j + 1), j, eng.snap(j - 1))
            step(None, B - 1, B - 2, B - 3)
            step(None, None, B - 1, B - 2)
            step(None, None, None, B - 1)

        FRONT_STAGES = 20

        def idle(n):
            for _ in range(n):
                yield

        def rounds(order, scored, weighed, units, nxt, image, prev, side):
            for r in range(ROUNDS):
                for part in order:
                    if part == "a" and scored and image is not None:
                        scored(r)
                    if part == "w" and weighed:
                        weighed(r)
                    if part == "u" and units:
                        for u, kind, k in (filling_plan if image is None else unit_plan)[r]:
                            of = image if kind in ("v1", "vw", "vs") else nxt
                            if of is not None:
                                units(of, u, kind, k)
                    if part == "s":
                        for _ in range(SIDE_STAGES[r]):
                            next(side, None)
            for _ in side:
                pass

        def second_loop(eng, turn):
            for b in (-1, 0, 1):
                turn(b, b % 2)
            with eng.Fori(1, B // 2 - 1) as i:
                for parity in range(2):
                    turn(eng.snap(2 * i + parity), parity)
            for b in (B - 2, B - 1, B, B + 1):
                turn(b, b % 2)

        def there(image):
            return type(image) is not int or 0 <= image < B

        @block.sync
        def _(sp):
            sp.dma_start(prep, prep_in).then_inc(S("prep"), 16)
            sp.dma_start(early[:, :], early_in).then_inc(S("early"), 16)
            for half_ in range(2):
                sp.dma_start(xin[half_ * C:(half_ + 1) * C, :], x_in[0]).then_inc(S("x_loaded"), 16)
            sp.dma_start(late[:, :], late_in).then_inc(S("late"), 16)
            sp.dma_start(masks32, masks_in).then_inc(S("masks"), 16)
            with sp.Fori(1, B) as b:
                sp.wait_ge(S("x_free"), b)
                for half_ in range(2):
                    sp.dma_start(xin[half_ * C:(half_ + 1) * C, :], x_in[b]).then_inc(S("x_loaded"), 16)
            sp.wait_ge(S("attention_done"), 1)
            sp.dma_start(final, final_in).then_inc(S("final"), 16)
            with sp.Fori(0, B // 2) as i:
                for parity in range(2):
                    sp.wait_ge(S("y_copied"), 2 * i + parity + 2)
                    sp.dma_start(y_out[2 * i + parity], yc[parity]).then_inc(S(f"y_stored{parity}"), 16)
            for parity in range(2):
                sp.wait_ge(S(f"y_stored{parity}"), 16 + 16 * (B // 2))

        @block.gpsimd
        def _(pool):
            nc.gpsimd.memset(half[:, :], -0.5).then_inc(S("half"), 1)
            pool.wait_ge(S("half"), 1)
            pool.wait_ge(S("bn_var"), 1)
            nc.gpsimd.tensor_tensor(bnc[:, 1:2], bnc[:, 0:1], half[:, :], ALU.pow).then_inc(S("bn_rstd"), 1)

            def rsqrt(n, out, in_, ready, done):
                pool.wait_ge(S(ready), n)
                h = half[:, 0:1]
                if len(in_.shape) == 3:
                    h = h.unsqueeze(2)
                nc.gpsimd.tensor_tensor(out, in_, h.broadcast_to(tuple(in_.shape)), ALU.pow)\
                    .then_inc(S(done), 1)

            def front(n):
                yield
                rsqrt(n, gt[:, 1:2], gt[:, 0:1], "gn1_var", "gn1_rstd")
                yield from idle(8)
                rsqrt(n, gt[:, 1:2], gt[:, 0:1], "gn2_var", "gn2_rstd")
                yield from idle(3)
                rsqrt(n, gv[:, :], mv[:, :, 1], "ln1_var", "ln1_rstd")
                yield from idle(3)
                rsqrt(n, rs[:, :, :], ms[:, :, :], "rms_var", "rms_rstd")
                yield from idle(5)

            def back_first(n):
                rsqrt(n, gv2[:, :], mv2[:, :, 1], "ln2_var", "ln2_rstd")

            def back(n, image):
                yield from idle(4)
                for t in range(NT):
                    pool.wait_ge(S("y_biased"), image * NT + t + 1)
                    nc.gpsimd.tensor_tensor(yb[:, t, :, :], yb[:, t, :, :],
                                            comb[:, t, :].unsqueeze(2).broadcast_to((P, E, C)), ALU.mult)\
                        .then_inc(S("y_weighted"), 1)
                yield
                rsqrt(n, gv2[:, :], mv2[:, :, 1], "ln3_var", "ln3_rstd")
                yield from idle(4)
                rsqrt(n, n3[:, 2, :], n3[:, 1, :], "n3_var", "n3_rstd")
                yield from idle(4)
                rsqrt(n, gv2[:, :], mv2[:, :, 1], "ln4_var", "ln4_rstd")
                yield

            def step(fresh, nxt, image, prev):
                def side():
                    if fresh is not None:
                        yield from front(fresh + 1)
                    elif prev is not None:
                        yield from idle(FRONT_STAGES if image is not None else OUT_ROUND + 1)
                    if prev is not None:
                        yield from back(prev + 1, prev)

                def add_branches(of, g):
                    pool.wait_ge(S("branch_out"), of * 12 + 3 * g + 3)
                    if g == 0 and starts(of, -1):
                        pool.wait_ge(S("attn_out"), of)
                    nc.gpsimd.tensor_tensor(oT[:, g, :], ob[:, g % 2, 0, :], ob[:, g % 2, 1, :], ALU.add)\
                        .then_inc(S("pool_add"), 1)
                    pool.wait_ge(S("pool_add"), of * 4 + g + 1)
                    nc.gpsimd.tensor_tensor(oT[:, g, :], oT[:, g, :], ob[:, g % 2, 2, :], ALU.add)\
                        .then_inc(S("o_summed"), 1)

                def weighed(r):
                    if prev is not None and WEIGH_AT.get(r + ROUNDS) == 11:
                        add_branches(prev, 3)
                    if prev is not None and r == OUT_ROUND:
                        back_first(prev + 1)
                    if image is not None and WEIGH_AT.get(r, 0) % 3 == 2:
                        add_branches(image, WEIGH_AT[r] // 3)

                rounds(POOL_ORDER, None, weighed, None, nxt, image, prev, side())

            run(pool, step)
            with pool.Fori(0, B) as b:
                rsqrt(b + 1, gv[:, :], mv[:, :, 1], "ln5_var", "ln5_rstd")

        @block.tensor
        def _(pe):
            wide = [ring[0], ring[1], heads[0], heads[1]]
            pe.sem_inc(S("f_turned"), 1)
            pe.wait_ge(S("prep"), 16)
            pe.wait_ge(S("early"), 16)
            pe.wait_ge(S("scaled"), 2)
            for i in range(13):
                m = pe.matmul(wide[i // 4][:, (i % 4) * P:(i % 4 + 1) * P],
                              scaled[:, 2 * i:2 * i + 2, :].rearrange("p a c -> p (a c)"), cst("pw_kv"),
                              start=True, stop=True)
            for i in range(13):
                m = pe.matmul((SA, SB_)[i // 8][:, (i % 8) * C:(i % 8 + 1) * C],
                              scaled_q[:, 2 * i:2 * i + 2, :].rearrange("p a c -> p (a c)"),
                              cst("pw_q")[0:C, :], start=True, stop=True)
            m.then_inc(S("composed"), 1)
            def after(n, *names):
                for name in names:
                    pe.wait_ge(S(name), n)

            def transpose_tok(src, dst, col, done):
                pe.sem_inc(S("pe_gap"), 1)
                for t in range(NT):
                    m = pe.transpose(dst[0:C, col + t * P:col + (t + 1) * P], src[:, t, :], ident)
                m.then_inc(S(done), 1)

            def front(n, mean_bank=SB_):
                yield
                after(n, "gn1_stats")
                pe.matmul(mean_bank[:, 0:2], cst("pairmean"), mv[:, 0, :], start=True, stop=True)\
                    .then_inc(S("gn1_mean"), 1)
                yield
                yield
                after(n, "gn1_done")
                for i, (copy, dy, dx) in enumerate(PAIRS5):
                    pe.matmul(SA[:, 0:T], wc_kv[:, i, :], window(copy, dy, dx), start=(i == 0), stop=(i == 12))
                yield
                pe.matmul(SA[0:C, T:2 * T], cst("w_q0"), window(0, 2, 2), start=True, stop=True)
                for i, (copy, dy, dx) in enumerate(PAIRS5):
                    pe.matmul(SA[C:P, T:2 * T], wc_q[:, i, :], window(copy, dy, dx), start=(i == 0),
                              stop=(i == 12))
                for t in range(NT):
                    m = pe.matmul(SB_[:, t * P:(t + 1) * P], xg[:, t * P:(t + 1) * P], cst("w_kv0"),
                                  start=True, stop=True)
                m.then_inc(S("conv5"), 1)
                yield
                after(n, "kv1_copied")
                for t in range(NT):
                    m = pe.transpose(SA[:, t * P:(t + 1) * P], kv1[:, t * P:(t + 1) * P], ident)
                m.then_inc(S("kv1_turned"), 1)
                yield
                after(n, "kv_ready")
                for t in range(NT):
                    m = pe.matmul(SB_[:, 0:P + 1], ktok[:, t, :], vtok[:, t, :], start=(t == 0), stop=(t == NT - 1))
                m.then_inc(S("kv_sum"), 1)
                yield
                after(n, "kv_masked")
                pe.matmul(SA[:, 0:T], kvm[:, :], q0[:, :], start=True, stop=True)
                pe.matmul(SA[:, T:2 * T], ksm[:, :], q0[:, :], start=True, stop=True).then_inc(S("lin_out"), 1)
                yield
                after(n, "o0_ready")
                pe.matmul(SB_[:, 0:T], cst("proj0"), o0[:, :], start=True, stop=True).then_inc(S("proj0"), 1)
                yield
                after(n, "gn2_stats")
                pe.matmul(SA[:, 0:2], cst("pairmean"), mv[:, 0, :], start=True, stop=True)\
                    .then_inc(S("gn2_mean"), 1)
                yield
                yield
                after(n, "gn2_done")
                for i, (copy, dy, dx) in enumerate(PAIRS3):
                    m = pe.matmul(SB_[0:C, 0:T], bin1[:, i, :], window(copy, dy + 1, dx + 1), start=(i == 0),
                                  stop=(i == 4))
                m.then_inc(S("conv3"), 1)
                yield
                after(n, "x2")
                pe.sem_inc(S("pe_gap"), 1)
                for t in range(NT):
                    m = pe.transpose(SA[:, t * C:(t + 1) * C], x1[0:C, t * P:(t + 1) * P], ident[0:C, 0:C])
                m.then_inc(S("x2_turned"), 1)
                yield
                yield
                after(n, "xn1")
                transpose_tok(xn, SA, 0, "xn1_turned")
                yield
                if type(n) is int and n == 1:
                    pe.wait_ge(S("prepared"), 1)
                after(n, "xnT1")
                for t in range(NT):
                    m = pe.matmul(SB_[:, t * 68:(t + 1) * 68], xnT[:, t * P:(t + 1) * P], cst("w_small"),
                                  start=True, stop=True)
                m.then_inc(S("small"), 1)
                pe.matmul(SA[:, 0:T], cst("w_kr"), xnT[:, :], start=True, stop=True).then_inc(S("k_rope"), 1)
                yield
                after(n, "small_copied")
                for t in range(NT):
                    m = pe.matmul(SB_[:, 140:140 + BR], meank[:, :], sm[:, t, 64:64 + BR], start=(t == 0),
                                  stop=(t == NT - 1))
                m.then_inc(S("gate_mean"), 1)
                after(n, "score_bc", "k_rotated")
                for t in range(NT):
                    m = pe.transpose(SA[:, t * P:(t + 1) * P], sbc[:, t, :], ident)
                m.then_inc(S("score_row"), 1)
                yield
                after(n, "cn_ready", "gate_read")
                transpose_tok(cn, SB_, T, "cn_turned")
                yield
                after(n, "selected")
                pe.matmul(SA[:, 0:1], cst("before"), sel[:, 0:1], start=True, stop=True)
                pe.matmul(SA[:, 1:2], cst("before"), sel[:, 1:2], start=True, stop=False)
                pe.matmul(SA[:, 1:2], meank[:, :], gs[:, 7:8], start=False, stop=True)\
                    .then_inc(S("positions"), 1)
                yield
                after(n, "pick_ready")
                for t in range(NT):
                    m = pe.matmul(SA[C:P, 0:P], xn[:, t, :], pickm[:, t, :], start=(t == 0), stop=(t == NT - 1))
                m.then_inc(S("sel_x"), 1)
                yield
                after(n, "cnT", "selT")

            def back_first(n, image):
                pe.wait_ge(S("o_summed"), image * 4 + 4)
                after(n, "sc_free")
                for t in range(NT):
                    for g in range(4):
                        m = pe.matmul(SC[:, t * C:(t + 1) * C], oT[:, g, t * P:(t + 1) * P], w_p[:, g, :],
                                      start=(g == 0), stop=(g == 3))
                m.then_inc(S("attn_out"), 1)

            def back(n, image):
                yield
                after(n, "xn2")
                transpose_tok(xp, SB_, 0, "xn2_turned")
                yield
                after(n, "xnT2")
                for t in range(NT):
                    m = pe.matmul(SA[:, t * E:(t + 1) * E], xpT[:, t * P:(t + 1) * P], cst("r2"),
                                  start=True, stop=True)
                m.then_inc(S("logits"), 1)
                for u in range(2):
                    for i in range(2):
                        m = pe.matmul((SC, SB_)[u][:, i * T:(i + 1) * T], w1[:, 2 * u + i, :], xpT[:, :],
                                      start=True, stop=True)
                    m.then_inc(S("hidden"), 1)
                yield
                yield
                after(n, "gelu1")
                for t in range(NT):
                    for i in range(4):
                        m = pe.matmul((SA, SC)[t][:, i * P:(i + 1) * P], hm[:, i, t * P:(t + 1) * P], w2[:, i, :],
                                      start=True, stop=True)
                    m.then_inc(S("expert_out"), 1)
                yield
                yield
                yield
                after(n, "xn3")
                transpose_tok(xp, SB_, 0, "xn3_turned")
                yield
                after(n, "xnT3")
                pe.matmul(SA[:, 0:T], cst("q3"), xpT[:, :], start=True, stop=True)
                for t in range(NT):
                    m = pe.matmul(SB_[:, t * T:(t + 1) * T], xpT[:, t * P:(t + 1) * P], cst("kv3"),
                                  start=True, stop=True)
                m.then_inc(S("qkv3"), 1)
                yield from idle(3)
                after(n, "kv3_normed", "q3_copied")
                kvf = kvq[:, :, :, :].rearrange("p t g d -> p t (g d)")
                for t in range(NT):
                    m = pe.matmul(SA[:, 0:P], kvf[:, t, P:2 * P], kvf[:, t, 0:P], start=(t == 0),
                                  stop=(t == NT - 1))
                m.then_inc(S("dots"), 1)
                yield
                after(n, "dots_masked")
                pe.matmul(SA[:, P:P + C], dT[:, :], cst("out3"), start=True, stop=True).then_inc(S("dots_out"), 1)
                yield
                after(n, "m3")
                for t in range(NT):
                    m = pe.matmul(SB_[:, t * C:(t + 1) * C], q3[:, t * P:(t + 1) * P], m3[:, :],
                                  start=True, stop=True)
                m.then_inc(S("attn3"), 1)
                yield
                yield
                after(n, "xn4")
                for t in range(NT):
                    m = pe.matmul(SC[0:C, 0:1], x4[:, t, :], meank[:, 0:1], start=(t == 0), stop=(t == NT - 1))
                m.then_inc(S("token_mean"), 1)
                yield

            first_front = front(1, SC)
            for _ in range(3):
                next(first_front)
            pe.wait_ge(S("late"), 16)
            for h in range(HEADS):
                m = pe.matmul(PV[0:CQ, h * CKV:(h + 1) * CKV], wqn_t[0:NOPE, h, :], wkn_t[0:NOPE, h, :],
                              start=True, stop=True)
            m.then_inc(S("absorbed"), 1)
            pe.wait_ge(S("convolution"), 1)

            def step(fresh, nxt, image, prev):
                def side():
                    if fresh is not None:
                        yield from first_front if type(fresh) is int and fresh == 0 else front(fresh + 1)
                    elif prev is not None:
                        yield from idle(FRONT_STAGES if image is not None else OUT_ROUND + 1)
                    if prev is not None:
                        yield from back(prev + 1, prev)

                def units(of, u, kind, k):
                    dst = heads[u % 2]
                    if u >= 2 or starts(of, -1):
                        pe.wait_ge(S("unit_free"), of * UNITS + u - 1)
                    if kind == "q":
                        if (kind, k) == FIRST_UNIT:
                            pe.wait_ge(S("handed"), of * 5 + 5)
                        for i in range(2):
                            m = pe.matmul(dst[:, i * T:(i + 1) * T], w_q[:, 2 * k + i, :], cnH[:, :],
                                          start=True, stop=True)
                    elif kind == "kw":
                        for i in range(2):
                            m = pe.matmul(dst[:, i * T:(i + 1) * T], w_k[:, 2 * k + i, :], xnH[:, :],
                                          start=True, stop=True)
                    elif kind == "ks":
                        for i in range(2):
                            m = pe.matmul(dst[:, i * P:(i + 1) * P], w_k[:, 2 * k + i, :], selH[:, :],
                                          start=True, stop=True)
                    elif kind == "turn":
                        after(of + 1, "mh_ready")
                        pe.sem_inc(S("pe_gap"), 1)
                        mTp = dst[:, 0:P].bitcast(BF16)
                        for t in range(NT):
                            m = pe.transpose(mTp[:, t * P:(t + 1) * P], mh[:, t, :], identb)
                    elif kind[0] == "v":
                        src = {"v1": cnH, "vw": xnH, "vs": selH}[kind]
                        m = pe.matmul(dst[:, :], src[:, k * P:(k + 1) * P], cst("w_v1" if kind == "v1" else "w_v"),
                                      start=True, stop=True)
                    else:
                        pe.wait_ge(S("heads_bf16"), of * 3 * PAIRS + max(made[kind_, k] for kind_ in MAX_OF[kind]))
                        for qt, br, at, key0, keys in MAX_PARTS[kind]:
                            for i in range(2):
                                out = dst[:, at + i * keys:at + (i + 1) * keys]
                                rhs = (k1b[:, key0:key0 + keys], ksb[:, slot[k], i, :],
                                       kwb[:, slot[k], i, key0:key0 + keys])[br]
                                m = pe.matmul(out, qb[:, slot[k], i, qt * P:(qt + 1) * P], rhs,
                                              start=True, stop=(br == 1))
                                if br == 0:
                                    m = pe.matmul(out[:, keys - P:keys], identb, cst("causal_s"),
                                                  start=False, stop=True)
                                elif br == 2:
                                    m = pe.matmul(out, identb, cst("band_s" if qt == 0 else "band_s1"),
                                                  start=False, stop=True)
                    m.then_inc(S("unit_full"), 1)

                def fold(out, br, h, q_, nq, stop):
                    r = br * HEADS + h
                    return pe.matmul(out, pick[:, r:r + 1].broadcast_to((P, P)), mT[:, q_:q_ + nq],
                                     start=False, stop=stop)

                def scores(t):
                    hp, i = t // 4, t % 4
                    h0 = 2 * hp
                    if hp == KEPT and i == 0:
                        pe.wait_ge(S("moved"), image * 3 + 3)
                    dst = ring[t % 2]
                    if t == 0:
                        after(image + 1, "mT", "k1T_taken")
                    if t >= 2 or starts(image, -1):
                        pe.wait_ge(S("exp_done"), image * SCORE_UNITS + t - 1)
                    if i == 0:
                        pe.matmul(dst[:, :], k1T[:, 0:P], qT[:, h0:h0 + 2, :], start=True, stop=False)
                        for j in range(2):
                            fold(dst[:, j * T:(j + 1) * T], 0, h0 + j, 0, T, False)
                            m = pe.matmul(dst[:, j * T:j * T + P], identb, cst("causal_t"), start=False,
                                          stop=(j == 1))
                    elif i == 1:
                        for j in range(2):
                            pe.matmul(dst[:, j * T:(j + 1) * T], ksT[:, h0 + j, :], qT[:, h0 + j, :],
                                      start=True, stop=False)
                            m = fold(dst[:, j * T:(j + 1) * T], 1, h0 + j, 0, T, True)
                    elif i == 2:
                        pe.matmul(dst[:, 0:T], k1T[:, P:T], qT[:, h0:h0 + 2, P:T], start=True, stop=False)
                        for j in range(2):
                            out = dst[:, j * P:(j + 1) * P]
                            fold(out, 0, h0 + j, P, P, False)
                            pe.matmul(out, identb, cst("causal_t"), start=False, stop=(j == 1))
                        for j in range(2):
                            out = dst[:, T + j * P:T + (j + 1) * P]
                            pe.matmul(out, kwT[:, h0 + j, P:T], qT[:, h0 + j, P:T], start=True, stop=False)
                            fold(out, 2, h0 + j, P, P, False)
                            m = pe.matmul(out, identb, cst("band_t"), start=False, stop=True)
                    else:
                        for j in range(2):
                            out = dst[:, j * BAND:(j + 1) * BAND]
                            pe.matmul(out, kwT[:, h0 + j, 0:P], qT[:, h0 + j, 0:BAND], start=True, stop=False)
                            fold(out, 2, h0 + j, 0, BAND, False)
                            m = pe.matmul(out, identb, cst("band_t0"), start=False, stop=True)
                    m.then_inc(S("scores"), 1)

                def weigh(image, u):
                    g, br = u // 3, u % 3
                    if br == 0:
                        pe.wait_ge(S("exp_done"), image * SCORE_UNITS + 8 * (g + 1))
                    if u or starts(image, -1):
                        pe.wait_ge(S("branch_out"), image * 12 + u)
                    for den in range(2):
                        c = T * den

                        def mm(j, cols, vals, probs, start, stop):
                            lhs = onesk[:, :] if den else vals[:, (4 * g + j) * VDIM:(4 * g + j + 1) * VDIM]
                            return pe.matmul(PV[32 * j:32 * j + 32, c + cols[0]:c + cols[1]], lhs, probs,
                                             start=start, stop=stop)

                        def p_of(j, a, nn):
                            return pr[:, g % 2, j // 2, a:a + nn]

                        if br == 0:
                            for j in range(4):
                                mm(j, (0, T), v1[:, 0, :], p_of(j, (j % 2) * T, T), True, False)
                            for j in range(4):
                                m = mm(j, (P, T), v1[:, 1, :], p_of(j, 1024 + (j % 2) * P, P), False, True)
                        elif br == 1:
                            for j in range(4):
                                m = mm(j, (0, T), vs[:, :], p_of(j, 512 + (j % 2) * T, T), True, True)
                        else:
                            for j in range(4):
                                mm(j, (P, T), vw[:, 1, :], p_of(j, 1280 + (j % 2) * P, P), True, False)
                            for j in range(4):
                                mm(j, (P, BAND), vw[:, 0, :], p_of(j, 1536 + (j % 2) * BAND + P, WINDOW),
                                   False, True)
                            for j in range(4):
                                m = mm(j, (0, P), vw[:, 0, :], p_of(j, 1536 + (j % 2) * BAND, P), True, True)
                    m.then_inc(S("weighed"), 1)

                def scored(r):
                    if r < SCORE_UNITS:
                        scores(r)

                def weighed(r):
                    if prev is not None and r + ROUNDS in WEIGH_AT:
                        weigh(prev, WEIGH_AT[r + ROUNDS])
                    if prev is not None and r == OUT_ROUND:
                        back_first(prev + 1, prev)
                    if image is not None and r in WEIGH_AT:
                        weigh(image, WEIGH_AT[r])

                rounds(PE_ORDER, scored, weighed, units, nxt, image, prev, side())

            run(pe, step)

            def turn_in(b, parity):
                pe.wait_ge(S("x4_fetched"), b + 1)
                pe.sem_inc(S("pe_gap"), 1)
                for t in range(NT):
                    m = pe.transpose(SA[0:C, t * P:(t + 1) * P], x4s[parity][:, t, :], ident)
                m.then_inc(S("x4_turned"), 1)

            def hidden(b, parity):
                pe.wait_ge(S("x4c"), b + 1)
                for e in range(E):
                    if e % 2 == 0 and (type(b) is not int or b > 0):
                        pe.wait_ge(S("f_gelu"), b * E - E + e + 2)
                    m = pe.matmul(wide[e // 2][:, (e % 2) * T:(e % 2 + 1) * T], f1[:, e, :], x4c[parity][:, :],
                                  start=True, stop=True)
                    if e % 2:
                        m.then_inc(S("f_hidden"), 1)

            def experts(b, parity):
                pe.wait_ge(S("f_in"), b + 1)
                pe.wait_ge(S("f_gelu"), b * E + E)
                if type(b) is not int or b > 0:
                    pe.wait_ge(S("y_cm"), b)
                for e in range(E):
                    at = e % 2 * C
                    pe.matmul(SB_[at:at + C, 0:T], w2s[parity][:, e, :], hf[parity][:, e, :], start=(e < 2),
                              stop=(e == E - 1))
                m = pe.matmul(SB_[0:C, 0:T], fb2s[parity][:, :], meank[:, 0:1].broadcast_to((P, T)), start=False,
                              stop=True)
                m.then_inc(S("f_out"), 1)

            def turn_y(b):
                pe.wait_ge(S("y_cm"), b + 1)
                for t in range(NT):
                    m = pe.transpose(PV[:, t * P:(t + 1) * P], y_cm[:, t * P:(t + 1) * P], ident)
                m.then_inc(S("y_turned"), 1)

            def turn_out(b, parity):
                pe.wait_ge(S("tf_ready"), b + 1)
                if type(b) is not int or b > 0:
                    pe.wait_ge(S("y_copied"), b + 1)
                pe.sem_inc(S("pe_gap"), 1)
                for t in range(NT):
                    m = pe.transpose(SC[0:C, t * P:(t + 1) * P], tf[parity][:, t, :], ident)
                m.then_inc(S("f_turned"), 1)

            def route():
                pe.wait_ge(S("xbar_kept"), B)
                pe.matmul(SB_[0:B, 0:E], xbar[:, :], cst("r3"), start=True, stop=True).then_inc(S("route_logits"), 1)
                pe.wait_ge(S("route1"), 1)
                pe.matmul(SB_[0:B, 16:16 + E], meank[0:B, 0:B], rw[0:B, :], start=True, stop=True)\
                    .then_inc(S("route_load"), 1)
                pe.wait_ge(S("route2"), 1)
                pe.matmul(PV[:, 0:B * E], meank[:, :], wdiag[:, :, :].rearrange("p b e -> p (b e)"),
                          start=True, stop=True).then_inc(S("route_bc"), 1)

            def turn(b, parity):
                if there(b):
                    hidden(b, parity)
                if type(b) is int and b == 0:
                    route()
                if there(b - 1 if type(b) is int else b):
                    experts(b - 1, 1 - parity)
                if there(b + 1 if type(b) is int else b):
                    turn_in(b + 1, 1 - parity)
                if there(b - 2 if type(b) is int else b):
                    turn_out(b - 2, parity)
                if there(b - 1 if type(b) is int else b):
                    turn_y(b - 1)

            pe.wait_ge(S("final"), 16)
            second_loop(pe, turn)

        @block.scalar
        def _(act):
            act.sem_inc(S("y_copied"), 1)
            act.sem_inc(S("y_stored0"), 16)
            act.sem_inc(S("y_stored1"), 16)
            def after(n, *names):
                for name in names:
                    act.wait_ge(S(name), n)

            def front(n, image):
                yield from idle(4)
                after(n, "conv5")
                kv_tok = lambda src, c: src[:, 0:T].rearrange("p (t c) -> p t c", t=NT)[:, :, c:c + C]
                act.activation(ktok[:, :, 0:C], kv_tok(SB_, 0), ACT.Relu)
                act.activation(vtok[:, :, 0:C], kv_tok(SB_, C), ACT.Copy)
                yield
                after(n, "kv1_turned")
                act.activation(ktok[:, :, C:P], kv_tok(SA, 0), ACT.Relu)
                act.activation(vtok[:, :, C:P], kv_tok(SA, C), ACT.Copy).then_inc(S("kv_ready"), 1)
                yield from idle(9)
                if starts(image, -1):
                    act.wait_ge(S("handed"), image * 5)
                after(n, "xn1_turned")
                act.activation(xnT[0:C, :], SA[0:C, 0:T], ACT.Copy).then_inc(S("xnT1"), 1)
                yield
                yield
                yield
                after(n, "cn_turned")
                act.activation(cnT[0:C, :], SB_[0:C, T:2 * T], ACT.Copy, scale=cst("nw")[0:C, :])\
                    .then_inc(S("cnT"), 1)
                after(n, "gate_max")
                act.activation(gs[:, 0:BR], gl[:, :], ACT.Exp, bias=gs[:, 4:5]).then_inc(S("gate_exp"), 1)
                yield
                yield
                after(n, "sel_x")
                act.activation(selT[C:P, :], SA[C:P, 0:P], ACT.Copy).then_inc(S("selT"), 1)
                yield

            def hand_over(image):
                if starts(image, -1):
                    act.wait_ge(S("k1T_taken"), image)
                after(image + 1, "k1n", "cnT", "xnT1", "selT")
                act.activation(cnH[0:C, :], cnT[0:C, :], ACT.Copy).then_inc(S("handed"), 1)
                act.activation(selH[C:P, :], selT[C:P, :], ACT.Copy).then_inc(S("handed"), 1)
                act.activation(xnH[0:C, :], xnT[0:C, :], ACT.Copy).then_inc(S("handed"), 1)
                act.activation(k1b[:, :], k1n[:, :], ACT.Copy).then_inc(S("handed"), 1)
                act.activation(k1h[:, :], k1n[:, :], ACT.Copy).then_inc(S("handed"), 1)

            def back(n, image):
                yield
                after(n, "xn2_turned")
                act.activation(xpT[0:C, :], SB_[0:C, 0:T], ACT.Copy).then_inc(S("xnT2"), 1)
                yield
                after(n, "logit_max")
                for t in range(NT):
                    act.activation(pe8[:, t, :], SA[:, t * E:(t + 1) * E], ACT.Exp, bias=c8[:, t, 1:2],
                                   accum_out=c8[:, t, 2:3]).then_inc(S("logit_exp"), 1)
                yield
                for u in range(2):
                    act.wait_ge(S("hidden"), image * 2 + u + 1)
                    for i in range(2):
                        a = act.activation(hm[:, 2 * u + i, :], (SC, SB_)[u][:, i * T:(i + 1) * T], ACT.Gelu,
                                           bias=cst("b1")[:, 2 * u + i:2 * u + i + 1])
                a.then_inc(S("gelu1"), 1)
                yield from idle(4)
                after(n, "xn3_turned")
                act.activation(xpT[0:C, :], SB_[0:C, 0:T], ACT.Copy).then_inc(S("xnT3"), 1)
                yield
                after(n, "qkv3")
                act.activation(q3[:, :], SA[:, 0:T], ACT.Copy).then_inc(S("q3_copied"), 1)
                yield from idle(7)
                after(n, "token_mean")
                slot = slice(image, image + 1) if type(image) is int else bass.ds(image, 1)
                act.activation(xbar[0:C, slot], SC[0:C, 0:1], ACT.Copy).then_inc(S("xbar_kept"), 1)
                act.wait_ge(S("xbar_kept"), n)
                act.sem_inc(S("sc_free"), 1)
                yield

            def step(fresh, nxt, image, prev):
                def side():
                    if fresh is not None:
                        yield from front(fresh + 1, fresh)
                    elif prev is not None:
                        yield from idle(FRONT_STAGES if image is not None else OUT_ROUND + 1)
                    if prev is not None:
                        yield from back(prev + 1, prev)

                def units(of, u, kind, k):
                    if kind in ("q", "kw", "ks"):
                        i = ("q", "kw", "ks").index(kind)
                        src, dst = ((qT, qb), (kwT, kwb), (ksT, ksb))[i]
                        if (kind, k) == FIRST_UNIT:
                            hand_over(of)
                        act.wait_ge(S("unit_free"), of * UNITS + u + 1)
                        if k in last_max:
                            act.wait_ge(S("unit_full"), of * UNITS + last_max[k] + 1)
                        act.activation(dst[:, slot[k], :, :], kept[i] if k == KEPT else src[:, 2 * k:2 * k + 2, :],
                                       ACT.Copy)\
                            .then_inc(S("heads_bf16"), 1)
                    elif kind == "turn" or kind[0] == "v":
                        act.wait_ge(S("unit_full"), of * UNITS + u + 1)
                        act.wait_ge(S("unit_free"), of * UNITS + u)
                        if kind == "turn":
                            if image is not None:
                                act.wait_ge(S("scores"), image * SCORE_UNITS + SCORE_UNITS)
                            act.activation(mT[:, :], heads[u % 2][:, 0:P].bitcast(BF16), ACT.Copy)\
                                .then_inc(S("unit_free"), 1)
                            act.wait_ge(S("unit_free"), of * UNITS + u + 1)
                            act.sem_inc(S("mT"), 1)
                            for src_, dst in zip(kept, (qT, kwT, ksT)):
                                act.activation(dst[:, 2 * KEPT:2 * KEPT + 2, :], src_, ACT.Copy)\
                                    .then_inc(S("moved"), 1)
                        else:
                            if starts(of, -1):
                                act.wait_ge(S("weighed"), of * 12 - {"v1": 2, "vs": 1, "vw": 0}[kind])
                            dst = {"v1": v1[:, k, :], "vw": vw[:, k, :], "vs": vs[:, :]}[kind]
                            act.activation(dst, heads[u % 2][:, :], ACT.Copy).then_inc(S("unit_free"), 1)

                def scored(r):
                    if r == 0:
                        act.wait_ge(S("handed"), image * 5 + 5)
                        if starts(image, -1):
                            act.wait_ge(S("scores"), image * SCORE_UNITS)
                        act.activation(k1T[:, :], k1h[:, :], ACT.Copy).then_inc(S("k1T_taken"), 1)
                    if r < SCORE_UNITS:
                        hp, i = r // 4, r % 4
                        g = hp // 2
                        if hp % 2 == 0 and i == 0 and (g >= 2 or starts(image, -1)):
                            act.wait_ge(S("weighed"), image * 12 + 3 * (g - 1))
                        w = 2 * BAND if i == 3 else 512
                        act.wait_ge(S("scores"), image * SCORE_UNITS + r + 1)
                        act.activation(pr[:, g % 2, hp % 2, 512 * i:512 * i + w], ring[r % 2][:, 0:w], ACT.Exp,
                                       scale=SCALE).then_inc(S("exp_done"), 1)

                rounds(ACT_ORDER, scored, None, units, nxt, image, prev, side())

            last_max = {PAIR_ORDER[i]: maxima_done[PAIR_ORDER[i - 2]] for i in range(2, PAIRS)}
            act.sem_inc(S("sc_free"), 1)
            run(act, step)

            wide = [ring[0], ring[1], heads[0], heads[1]]

            def route():
                for k, (src, dst, sums) in enumerate(((lr, rw, rt[0:B, 2:3]), (rw, lr, rt[0:B, 6:7]),
                                                      (lr, rw, None))):
                    act.wait_ge(S("route_max"), k + 1)
                    act.activation(dst[0:B, :], src[0:B, :], ACT.Exp, bias=rt[0:B, 4 * k + 1:4 * k + 2],
                                   **({} if sums is None else {"accum_out": sums})).then_inc(S("route_exp"), 1)

            def turn(b, parity):
                if there(b):
                    if type(b) is not int or b >= 2:
                        act.wait_ge(S("f_out"), b - 1)
                    for e in range(E):
                        if e % 2 == 0:
                            act.wait_ge(S("f_hidden"), b * 4 + e // 2 + 1)
                        act.activation(hf[parity][:, e, :], wide[e // 2][:, (e % 2) * T:(e % 2 + 1) * T], ACT.Gelu,
                                       bias=cst("fb1")[:, e:e + 1]).then_inc(S("f_gelu"), 1)
                if there(b + 1 if type(b) is int else b):
                    act.wait_ge(S("x4_turned"), b + 2)
                    act.activation(x4c[1 - parity][0:C, :], SA[0:C, 0:T], ACT.Copy).then_inc(S("x4c"), 1)
                if type(b) is int and b == -1:
                    route()
                if there(b - 2 if type(b) is int else b):
                    act.wait_ge(S("f_turned"), b)
                    if type(b) is not int or b >= 4:
                        stored = 16 * (b // 2) if type(b) is int else act.snap((b - parity) * 8)
                        act.wait_ge(S(f"y_stored{parity}"), stored)
                    act.activation(yc[parity], SC[0:C, 0:T], ACT.Copy).then_inc(S("y_copied"), 1)

            act.wait_ge(S("final"), 16)
            second_loop(act, turn)

        @block.vector
        def _(dve):
            V = nc.vector
            count = [0]

            def link(ins):
                count[0] += 1
                ins.then_inc(S("dve_chain"), 1)
                dve.wait_ge(S("dve_chain"), count[0])

            def restart():
                count[0] = 0
                dve.sem_clear(S("dve_chain"))

            for tile in (img[0], img[1], xnT, xpT, cnT, selT, cnH, xnH, selH, cn, k1n, xbar, mh, wdiag,
                         fb2s[0], fb2s[1], gs):
                V.memset(tile[:], 0.0)
            V.memset(onesk[:, :], 1.0)
            V.memset(meank[:, :], 1.0 / T)
            link(V.memset(vtok[:, :, P:P + 1], 1.0))
            dve.wait_ge(S("prep"), 16)
            dve.wait_ge(S("early"), 16)
            V.tensor_tensor(scaled[:, :, :], cst("wi_kv").unsqueeze(1).broadcast_to((P, 26, C)),
                            dw_kv.unsqueeze(2).broadcast_to((P, 26, C)), ALU.mult).then_inc(S("scaled"), 1)
            V.tensor_tensor(scaled_q[:, :, :], cst("wi_q")[0:C, :].unsqueeze(1).broadcast_to((C, 26, C)),
                            dw_q[0:C, :].unsqueeze(2).broadcast_to((C, 26, C)), ALU.mult)\
                .then_inc(S("scaled"), 1)
            link(V.tensor_scalar(bin1[:, :, :], conv1, 0.0, None, ALU.is_gt))
            link(V.tensor_scalar(binn[:, :, :], conv1, 0.0, None, ALU.is_lt))
            link(V.tensor_tensor(bin1[:, :, :], bin1[:, :, :], binn[:, :, :], ALU.subtract))
            bn = cst("bn")
            V.tensor_scalar(bnc[:, 0:1], bn[:, 3:4], 1e-5, None, ALU.add).then_inc(S("bn_var"), 1)
            dve.wait_ge(S("bn_rstd"), 1)
            link(V.tensor_tensor(bnc[:, 2:3], bn[:, 0:1], bnc[:, 1:2], ALU.mult))
            link(V.tensor_tensor(bnc[:, 3:4], bn[:, 2:3], bnc[:, 2:3], ALU.mult))
            link(V.tensor_tensor(bnc[:, 3:4], bn[:, 1:2], bnc[:, 3:4], ALU.subtract))
            def after(n, *names):
                for name in names:
                    dve.wait_ge(S(name), n)

            def tok(src):
                return src[:, 0:NT * C].rearrange("p (t c) -> p t c", t=NT)

            def group_stats(x, which):
                link(V.bn_stats(st[:, 0, :], x[:, :]))
                link(V.bn_aggr(mv[:, 0, :], st[:, 0, :]))
                V.scalar_tensor_tensor(out=mv[:, 0, 1:2], in0=mv[:, 0, 0:1], scalar=mv[:, 0, 0:1],
                                       in1=mv[:, 0, 1:2], op0=ALU.mult, op1=ALU.add)\
                    .then_inc(S(f"gn{which}_stats"), 1)

            def group_var(n, src, which):
                after(n, f"gn{which}_mean")
                link(V.tensor_copy(gm[:, :], src[:, 0:2]))
                link(V.scalar_tensor_tensor(out=gt[:, 0:1], in0=gm[:, 0:1], scalar=gm[:, 0:1],
                                            in1=gm[:, 1:2], op0=ALU.mult, op1=ALU.subtract))
                V.tensor_scalar(gt[:, 0:1], gt[:, 0:1], -1.0, 1e-5, ALU.mult, ALU.add)\
                    .then_inc(S(f"gn{which}_var"), 1)

            def group_apply(n, x, which):
                after(n, f"gn{which}_rstd")
                xv = x[:, :].rearrange("p (h w) -> p h w", h=H)
                for i in range(2):
                    for up in range(2):
                        dy, dx = (2, 2) if not up else (2, 1) if i == 0 else (1, 2)
                        r = slice(C * up, C * up + C)
                        a = V.tensor_scalar(img[i][r, dy:dy + H, dx:dx + W], xv[r], gm[r, 0:1], gt[r, 1:2],
                                            ALU.subtract, ALU.mult)
                if which == 1:
                    a = V.tensor_scalar(xg[:, :], x[:, :], gm[:, 0:1], gt[:, 1:2], ALU.subtract, ALU.mult)
                a.then_inc(S(f"gn{which}_done"), 1)

            def layer_stats(t, st_, mv_, which):
                for i in range(NT):
                    a = V.bn_stats(st_[:, i, :], t[:, i, :])
                link(a)
                for i in range(NT):
                    a = V.bn_aggr(mv_[:, i, :], st_[:, i, :])
                link(a)
                V.tensor_scalar(mv_[:, :, 1], mv_[:, :, 1], 1e-5, None, ALU.add).then_inc(S(f"ln{which}_var"), 1)

            def layer_apply(n, t, mv_, gv_, out, which):
                after(n, f"ln{which}_rstd")
                for i in range(NT):
                    a = V.tensor_scalar(out[:, i, :], t[:, i, :], mv_[:, i, 0:1], gv_[:, i:i + 1],
                                        ALU.subtract, ALU.mult)
                if which < 5:
                    a.then_inc(S(f"xn{which}"), 1)
                else:
                    link(a)

            def front(n, image, mean_bank=SB_):
                dve.wait_ge(S("x_loaded"), image * 32 + 32)
                group_stats(xin, 1)
                yield
                group_var(n, mean_bank, 1)
                yield
                if type(image) is not int or image >= 2:
                    dve.wait_ge(S("moved"), image * 3 - 3)
                group_apply(n, xin, 1)
                V.tensor_scalar(xs[:, :], xin[:, :], bnc[:, 3:4], None, ALU.add).then_inc(S("x_free"), 1)
                yield
                yield
                after(n, "conv5")
                link(V.tensor_scalar(q0[:, :], SA[:, T:2 * T], 0.0, None, ALU.max))
                V.tensor_copy(kv1[:, :], SA[:, 0:T]).then_inc(S("kv1_copied"), 1)
                yield
                yield
                after(n, "kv_sum")
                V.tensor_tensor(kvm[:, :], SB_[:, 0:P], cst("blk8"), ALU.mult)
                V.tensor_scalar(ksm[:, :], cst("blk8"), SB_[:, P:P + 1], None, ALU.mult)\
                    .then_inc(S("kv_masked"), 1)
                yield
                after(n, "lin_out")
                link(V.tensor_scalar(den0[:, :], SA[:, T:2 * T], 1e-15, None, ALU.add))
                link(V.reciprocal(rec0[:, :], den0[:, :]))
                V.tensor_tensor(o0[:, :], SA[:, 0:T], rec0[:, :], ALU.mult).then_inc(S("o0_ready"), 1)
                yield
                after(n, "proj0")
                link(V.scalar_tensor_tensor(out=x1[:, :], in0=SB_[:, 0:T], scalar=bnc[:, 2:3], in1=xs[:, :],
                                            op0=ALU.mult, op1=ALU.add))
                group_stats(x1, 2)
                yield
                group_var(n, SA, 2)
                yield
                group_apply(n, x1, 2)
                yield
                after(n, "conv3")
                V.tensor_tensor(x1[0:C, :], SB_[0:C, 0:T], x1[0:C, :], ALU.add).then_inc(S("x2"), 1)
                yield
                after(n, "x2_turned")
                link(V.tensor_copy(t1n[:, :, :], tok(SA)))
                layer_stats(t1n, st, mv, 1)
                link(V.tensor_copy(all_t4[:, image, :, :], t1n[:, :, :]))
                yield
                layer_apply(n, t1n, mv, gv, xn, 1)
                yield
                yield
                after(n, "small")
                link(V.tensor_copy(sm[:, :, :], SB_[:, 0:NT * 68].rearrange("p (t c) -> p t c", t=NT)))
                dve.sem_inc(S("small_copied"), 1)
                for t in range(NT):
                    a = V.tensor_copy(sbc[:, t, :], sm[:, t, 67:68].broadcast_to((P, P)))
                a.then_inc(S("score_bc"), 1)
                after(n, "k_rope")
                if starts(image, -1):
                    dve.wait_ge(S("handed"), image * 5)
                V.tensor_tensor(k1n[C:P, :], SA[C:P, 0:T], cst("ktab")[C:P, :], ALU.mult)\
                    .then_inc(S("k_rotated"), 1)
                link(V.tensor_tensor(sq[:, :, :], sm[:, :, 0:64], sm[:, :, 0:64], ALU.mult))
                V.tensor_reduce(ms[:, 0, :], sq[:, :, 0:CQ], AX.X, ALU.add)
                link(V.tensor_reduce(ms[:, 1, :], sq[:, :, 32:32 + CKV], AX.X, ALU.add))
                V.tensor_scalar(ms[:, 0, :], ms[:, 0, :], 1.0 / CQ, 1e-6, ALU.mult, ALU.add)
                V.tensor_scalar(ms[:, 1, :], ms[:, 1, :], 1.0 / CKV, 1e-6, ALU.mult, ALU.add)\
                    .then_inc(S("rms_var"), 1)
                yield
                after(n, "gate_mean")
                link(V.tensor_copy(gl[:, :], SB_[:, 140:140 + BR]))
                dve.sem_inc(S("gate_read"), 1)
                link(V.tensor_reduce(gs[:, 3:4], gl[:, :], AX.X, ALU.max))
                V.tensor_scalar(gs[:, 4:5], gs[:, 3:4], -1.0, None, ALU.mult).then_inc(S("gate_max"), 1)
                after(n, "rms_rstd")
                V.tensor_tensor(cn[:, :, 0:CQ], sm[:, :, 0:CQ], rs[:, 0, :].unsqueeze(2).broadcast_to((P, NT, CQ)),
                                ALU.mult)
                V.tensor_tensor(cn[:, :, 32:64], sm[:, :, 32:64],
                                rs[:, 1, :].unsqueeze(2).broadcast_to((P, NT, CKV)), ALU.mult)\
                    .then_inc(S("cn_ready"), 1)
                yield
                after(n, "score_row")
                link(V.tensor_copy(srow[:, :], SA[:, 0:T]))
                for t in range(NT):
                    V.tensor_scalar(cmp_[:, t, :], srow[:, :], sm[:, t, 67:68], None, ALU.is_gt)
                    a = V.scalar_tensor_tensor(out=cmq_[:, t, :], in0=srow[:, :], scalar=sm[:, t, 67:68],
                                               in1=ties[:, t, :], op0=ALU.is_equal, op1=ALU.mult)
                link(a)
                link(V.tensor_tensor(cmp_[:, :, :], cmp_[:, :, :], cmq_[:, :, :], ALU.add))
                link(V.tensor_reduce(ranks[:, :], cmp_[:, :, :], AX.X, ALU.add))
                link(V.tensor_scalar(sel[:, :], ranks[:, :], float(KEEP), None, ALU.is_lt))
                V.tensor_scalar(gs[:, 7:8], sel[:, 0:1], float(T), None, ALU.mult).then_inc(S("selected"), 1)
                yield
                after(n, "gate_exp")
                link(V.tensor_reduce(gs[:, 5:6], gs[:, 0:BR], AX.X, ALU.add))
                link(V.reciprocal(gs[:, 6:7], gs[:, 5:6]))
                link(V.tensor_scalar(all_gates[:, image, :], gs[:, 0:BR], gs[:, 6:7], None, ALU.mult))
                after(n, "cnT")
                V.tensor_copy(k1n[32:64, :], cnT[32:64, :]).then_inc(S("k1n"), 1)
                after(n, "positions")
                link(V.tensor_copy(pos[:, :], SA[:, 0:2]))
                for t in range(NT):
                    a = V.tensor_scalar(pickm[:, t, :], cst("iota"), pos[:, t:t + 1], sel[:, t:t + 1],
                                        ALU.is_equal, ALU.mult)
                a.then_inc(S("pick_ready"), 1)
                yield
                yield

            def back_first(n, image):
                after(n, "attn_out")
                link(V.tensor_tensor(t2[:, :, :], tok(SC), all_t4[:, image, :, :], ALU.add))
                layer_stats(t2, st2, mv2, 2)

            def back(n, image):
                layer_apply(n, t2, mv2, gv2, xp, 2)
                yield
                yield
                after(n, "logits")
                link(V.tensor_reduce(c8[:, :, 0], SA[:, 0:NT * E].rearrange("p (t e) -> p t e", t=NT),
                                     AX.X, ALU.max))
                V.tensor_scalar(c8[:, :, 1], c8[:, :, 0], -1.0, None, ALU.mult).then_inc(S("logit_max"), 1)
                V.tensor_tensor(t2[:, :, :], t2[:, :, :], xp[:, :, :], ALU.add)
                yield
                dve.wait_ge(S("logit_exp"), image * 2 + 2)
                link(V.reciprocal(c8[:, :, 3], c8[:, :, 2]))
                link(V.tensor_tensor(pe8[:, :, :], pe8[:, :, :], c8[:, :, 3:4].broadcast_to((P, NT, E)), ALU.mult))
                for t in range(NT):
                    p_e = pe8[:, t, :].unsqueeze(2).broadcast_to((P, E, E))
                    p_j = pe8[:, t, :].unsqueeze(1).broadcast_to((P, E, E))
                    V.tensor_tensor(cg[:, t, :, :], p_j, p_e, ALU.is_gt)
                    a = V.tensor_tensor(ce[:, t, :, :], p_j, p_e, ALU.is_equal)
                link(a)
                link(V.tensor_tensor(ce[:, :, :, :], ce[:, :, :, :], first8.unsqueeze(1).broadcast_to((P, NT, E, E)),
                                     ALU.mult))
                link(V.tensor_tensor(cg[:, :, :, :], cg[:, :, :, :], ce[:, :, :, :], ALU.add))
                link(V.tensor_reduce(comb[:, :, :], cg[:, :, :, :], AX.X, ALU.add))
                link(V.scalar_tensor_tensor(out=comb[:, :, :], in0=comb[:, :, :], scalar=2.0, in1=pe8[:, :, :],
                                            op0=ALU.is_lt, op1=ALU.mult))
                link(V.tensor_reduce(c8[:, :, 4], comb[:, :, :], AX.X, ALU.add))
                link(V.tensor_scalar(c8[:, :, 5], c8[:, :, 4], 1e-12, None, ALU.max))
                link(V.reciprocal(c8[:, :, 6], c8[:, :, 5]))
                link(V.tensor_tensor(comb[:, :, :], comb[:, :, :], c8[:, :, 6:7].broadcast_to((P, NT, E)), ALU.mult))
                yield
                for t in range(NT):
                    dve.wait_ge(S("expert_out"), image * 2 + t + 1)
                    V.tensor_tensor(yb[:, t, :, :].rearrange("p e c -> p (e c)"), (SA, SC)[t][:, :], cst("b2"),
                                    ALU.add).then_inc(S("y_biased"), 1)
                yield
                dve.wait_ge(S("y_weighted"), image * 2 + 2)
                for t in range(NT):
                    a = V.tensor_reduce(ysum[:, t, :], yb[:, t, :, :].rearrange("p e c -> p c e"), AX.X, ALU.add)
                link(a)
                link(V.tensor_tensor(t3[:, :, :], t2[:, :, :], ysum[:, :, :], ALU.add))
                layer_stats(t3, st2, mv2, 3)
                yield
                layer_apply(n, t3, mv2, gv2, xp, 3)
                yield
                yield
                after(n, "qkv3")
                kvp = SB_[:, :].rearrange("p (g d) -> p g d", d=16)
                k3 = kv3[:, :, :, :].rearrange("p t g d -> p (t g) d")
                kq = kvq[:, :, :, :].rearrange("p t g d -> p (t g) d")
                bc = lambda i: n3[:, i, :].unsqueeze(2).broadcast_to((P, NT * 16, 16))
                link(V.tensor_reduce(n3[:, 0, :], kvp, AX.X, ALU.add))
                link(V.tensor_scalar(n3[:, 0, :], n3[:, 0, :], 1.0 / 16, None, ALU.mult))
                link(V.tensor_tensor(k3, kvp, bc(0), ALU.subtract))
                yield
                link(V.tensor_tensor(kq, k3, k3, ALU.mult))
                link(V.tensor_reduce(n3[:, 1, :], kq, AX.X, ALU.add))
                V.tensor_scalar(n3[:, 1, :], n3[:, 1, :], 1.0 / 16, 1e-5, ALU.mult, ALU.add)\
                    .then_inc(S("n3_var"), 1)
                yield
                link(V.tensor_tensor(t3[:, :, :], t3[:, :, :], cst("bout").unsqueeze(1).broadcast_to((P, NT, C)),
                                     ALU.add))
                after(n, "n3_rstd")
                V.tensor_tensor(kq, k3, bc(2), ALU.mult).then_inc(S("kv3_normed"), 1)
                yield
                after(n, "dots")
                V.tensor_tensor(dT[:, :], SA[:, 0:P], cst("blk16"), ALU.mult).then_inc(S("dots_masked"), 1)
                yield
                after(n, "dots_out")
                V.tensor_copy(m3[:, :], SA[:, P:P + C]).then_inc(S("m3"), 1)
                yield
                after(n, "attn3")
                link(V.tensor_tensor(t4[:, :, :], tok(SB_), t3[:, :, :], ALU.add))
                layer_stats(t4, st2, mv2, 4)
                yield
                layer_apply(n, t4, mv2, gv2, x4, 4)
                V.tensor_copy(all_t4[:, image, :, :], t4[:, :, :])
                dve.wait_ge(S("xn4"), n)
                link(V.tensor_copy(all_x4[:, image, :, :], x4[:, :, :]))
                yield
                yield

            first_front = front(1, 0, SC)
            for _ in range(3):
                next(first_front)
            dve.wait_ge(S("composed"), 1)
            for i, src in enumerate((ring[0], ring[1], heads[0], heads[1])):
                k = min(4, 13 - 4 * i)
                V.tensor_copy(wc_kv[:, 4 * i:4 * i + k, :], src[:, 0:k * P].rearrange("p (n m) -> p n m", n=k))
            V.tensor_copy(wc_q[:, 0:8, :], SA[:, :].rearrange("p (n m) -> p n m", n=8))
            link(V.tensor_copy(wc_q[:, 8:13, :], SB_[:, 0:5 * C].rearrange("p (n m) -> p n m", n=5)))
            dve.sem_inc(S("convolution"), 1)
            dve.wait_ge(S("absorbed"), 1)
            link(V.tensor_copy(w_q[0:CQ, :, NOPE:2 * NOPE],
                               PV[0:CQ, :].rearrange("p (h m) -> p h m", h=HEADS)))
            link(V.tensor_scalar(cst("w_kr"), cst("w_kr"), 1.0 / HEADS, None, ALU.mult))
            dve.wait_ge(S("masks"), 16)
            link(V.tensor_copy(masks[:, :], masks32))
            dve.sem_inc(S("prepared"), 1)

            def step(fresh, nxt, image, prev):
                restart()

                def side():
                    if fresh is not None:
                        yield from first_front if type(fresh) is int and fresh == 0 else front(fresh + 1, fresh)
                    elif prev is not None:
                        yield from idle(FRONT_STAGES if image is not None else OUT_ROUND + 1)
                    if prev is not None:
                        yield from back(prev + 1, prev)

                def units(of, u, kind, k):
                    mx_flat = mx[:, :, :].rearrange("p t c -> p (t c)")
                    src = heads[u % 2]
                    if kind in ("q", "kw", "ks"):
                        dve.wait_ge(S("unit_full"), of * UNITS + u + 1)
                        if kind == "q" and k == KEPT:
                            if starts(of, -1):
                                dve.wait_ge(S("moved"), of * 3)
                        elif kind == "q" and image is not None:
                            dve.wait_ge(S("scores"), image * SCORE_UNITS + 4 * k + 4)
                        dst, tab, w_ = {"q": (qT, "qtab", T), "kw": (kwT, "ktab", T), "ks": (ksT, "ktab", P)}[kind]
                        at = kept[("q", "kw", "ks").index(kind)] if k == KEPT else dst[:, 2 * k:2 * k + 2, :]
                        V.tensor_tensor(at,
                                             src[:, 0:2 * w_].rearrange("p (h t) -> p h t", h=2),
                                             cst(tab)[:, 0:w_].unsqueeze(1).broadcast_to((P, 2, w_)), ALU.mult)\
                            .then_inc(S("unit_free"), 1)
                    elif kind in MAX_PARTS:
                        dve.wait_ge(S("unit_full"), of * UNITS + u + 1)
                        first, apart, parts, keys = MAX_OUT[kind]
                        a = V.tensor_reduce(mx_flat[:, first:first + parts * apart]
                                            .rearrange("p (a b) -> p a b", a=parts)[:, :, 2 * k:2 * k + 2],
                                            src[:, 0:2 * parts * keys].rearrange("p (a h t) -> p a h t", h=2, t=keys),
                                            AX.X, ALU.max)
                        a.then_inc(S("unit_free"), 1)
                        if u == max(maxima_done.values()):
                            dve.wait_ge(S("unit_free"), of * UNITS + u + 1)
                            link(V.tensor_scalar(mh[:, :, 0:HB], mx[:, :, :], -1.0, None, ALU.mult))
                            V.scalar_tensor_tensor(out=mh[:, :, HB:2 * HB], in0=mx[:, :, :], scalar=-1.0,
                                                   in1=mh[:, :, 0:HB], op0=ALU.mult, op1=ALU.subtract)\
                                .then_inc(S("mh_ready"), 1)

                def branch(of, u):
                    g, br = u // 3, u % 3
                    dve.wait_ge(S("weighed"), of * 12 + u + 1)
                    if br == 0 and (g >= 2 or starts(of, -1)):
                        dve.wait_ge(S("o_summed"), of * 4 + g - 1)
                    link(V.reciprocal(rden[:, :], PV[:, T:2 * T]))
                    V.scalar_tensor_tensor(out=ob[:, g % 2, br, :], in0=PV[:, 0:T], scalar=gate[:, br:br + 1],
                                           in1=rden[:, :], op0=ALU.mult, op1=ALU.mult)\
                        .then_inc(S("branch_out"), 1)

                def weighed(r):
                    if prev is not None and r + ROUNDS in WEIGH_AT:
                        branch(prev, WEIGH_AT[r + ROUNDS])
                    if prev is not None and r == OUT_ROUND:
                        back_first(prev + 1, prev)
                    if image is not None and r == OUT_ROUND:
                        if starts(image, -1):
                            dve.wait_ge(S("branch_out"), image * 12)
                        link(V.tensor_copy(gate[:, :], all_gates[:, image, :]))
                    if image is not None and r in WEIGH_AT:
                        branch(image, WEIGH_AT[r])

                rounds(DVE_ORDER, None, weighed, units, nxt, image, prev, side())
                if image is not None and nxt is None:
                    dve.sem_inc(S("attention_done"), 1)

            run(dve, step)

            def fetch(b, parity):
                if type(b) is not int or b >= 2:
                    dve.wait_ge(S("x4_turned"), b - 1)
                V.tensor_copy(x4s[parity][:, :, :], all_x4[:, b, :, :]).then_inc(S("x4_fetched"), 1)

            def scale_weights(b, parity):
                link(V.tensor_copy(c8[:, 0, :], wd[:, b, :]))
                V.tensor_tensor(w2s[parity][:, :, :], f2, c8[:, 0, :].unsqueeze(2).broadcast_to((P, E, C)), ALU.mult)
                link(V.tensor_tensor(c8[0:E, 1, :], c8[0:E, 0, :], ident[0:E, 0:E], ALU.mult))
                link(V.tensor_reduce(rt[0:E, 0:1], c8[0:E, 1, :], AX.X, ALU.add))
                link(V.tensor_scalar(fb2s[parity][0:E, :], cst("fb2")[0:E, :], rt[0:E, 0:1], float(T),
                                     ALU.mult, ALU.mult))
                dve.sem_inc(S("f_in"), 1)

            def take_y(b):
                dve.wait_ge(S("f_out"), b + 1)
                V.tensor_copy(y_cm, SB_[:, 0:T]).then_inc(S("y_cm"), 1)

            def finish(b, parity):
                dve.wait_ge(S("y_turned"), b + 1)
                halves = PV[:, 0:T].rearrange("p (t e c) -> p t e c", t=NT, e=2)
                link(V.tensor_tensor(yf[:, :, :], halves[:, :, 0, :], all_x4[:, b, :, :], ALU.add))
                link(V.tensor_tensor(yf[:, :, :], halves[:, :, 1, :], yf[:, :, :], ALU.add))
                layer_stats(yf, st, mv, 5)
                layer_apply(b + 1, yf, mv, gv, yo, 5)
                link(V.tensor_tensor(yo[:, :, :], yo[:, :, :], cst("gamma").unsqueeze(1).broadcast_to((P, NT, C)),
                                     ALU.mult))
                link(V.tensor_tensor(yo[:, :, :], yo[:, :, :], cst("beta").unsqueeze(1).broadcast_to((P, NT, C)),
                                     ALU.add))
                if type(b) is not int or b >= 2:
                    dve.wait_ge(S("f_turned"), b)
                V.tensor_tensor(tf[parity][:, :, :], yo[:, :, :], all_t4[:, b, :, :], ALU.add)\
                    .then_inc(S("tf_ready"), 1)

            def turn(b, parity):
                if type(b) is not int or b >= 0:
                    restart()
                if there(b - 1 if type(b) is int else b):
                    take_y(b - 1)
                if type(b) is not int or 0 <= b and b + 2 < B:
                    fetch(b + 2, parity)
                if type(b) is not int or 0 <= b + 1 < B:
                    scale_weights(b + 1, 1 - parity)
                if there(b - 1 if type(b) is int else b):
                    finish(b - 1, 1 - parity)

            dve.wait_ge(S("final"), 16)
            restart()
            for parity in range(2):
                V.memset(x4c[parity], 0.0)
            dve.wait_ge(S("token_mean"), B)
            fetch(0, 0)
            R = slice(0, B)
            dve.wait_ge(S("route_logits"), 1)
            link(V.tensor_tensor(lr[R, :], SB_[R, 0:E], cst("br3")[R, :], ALU.add))
            link(V.tensor_reduce(rt[R, 0:1], lr[R, :], AX.X, ALU.max))
            V.tensor_scalar(rt[R, 1:2], rt[R, 0:1], -1.0, None, ALU.mult).then_inc(S("route_max"), 1)
            dve.wait_ge(S("route_exp"), 1)
            link(V.reciprocal(rt[R, 3:4], rt[R, 2:3]))
            V.tensor_scalar(rw[R, :], rw[R, :], rt[R, 3:4], None, ALU.mult).then_inc(S("route1"), 1)
            dve.wait_ge(S("route_load"), 1)
            capacity = float(-(-B * T * 5 // (4 * E)))
            link(V.tensor_scalar(load[R, :], SB_[R, 16:16 + E], float(T) * T, None, ALU.mult))
            link(V.tensor_scalar(r8[R, 0, :], load[R, :], capacity, None, ALU.max))
            link(V.reciprocal(r8[R, 1, :], r8[R, 0, :]))
            link(V.scalar_tensor_tensor(out=rw[R, :], in0=rw[R, :], scalar=capacity, in1=r8[R, 1, :],
                                        op0=ALU.mult, op1=ALU.mult))
            link(V.tensor_reduce(rt[R, 4:5], rw[R, :], AX.X, ALU.max))
            V.tensor_scalar(rt[R, 5:6], rt[R, 4:5], -1.0, None, ALU.mult).then_inc(S("route_max"), 1)
            dve.wait_ge(S("route_exp"), 2)
            link(V.reciprocal(rt[R, 7:8], rt[R, 6:7]))
            link(V.tensor_scalar(lr[R, :], lr[R, :], rt[R, 7:8], None, ALU.mult))
            p_e = lr[R, :].unsqueeze(2).broadcast_to((B, E, E))
            p_j = lr[R, :].unsqueeze(1).broadcast_to((B, E, E))
            V.tensor_tensor(r8[R], p_j, p_e, ALU.is_gt)
            link(V.tensor_tensor(r8b[R], p_j, p_e, ALU.is_equal))
            link(V.tensor_tensor(r8b[R], r8b[R], first8[R], ALU.mult))
            link(V.tensor_tensor(r8[R], r8[R], r8b[R], ALU.add))
            link(V.tensor_reduce(load[R, :], r8[R], AX.X, ALU.add))
            link(V.tensor_scalar(load[R, :], load[R, :], 2.0, None, ALU.is_lt))
            link(V.tensor_reduce(rt[R, 8:9], lr[R, :], AX.X, ALU.max))
            V.tensor_scalar(rt[R, 9:10], rt[R, 8:9], -1.0, None, ALU.mult).then_inc(S("route_max"), 1)
            dve.wait_ge(S("route_exp"), 3)
            link(V.tensor_tensor(rw[R, :], rw[R, :], load[R, :], ALU.mult))
            link(V.tensor_reduce(rt[R, 10:11], rw[R, :], AX.X, ALU.add))
            link(V.reciprocal(rt[R, 11:12], rt[R, 10:11]))
            link(V.tensor_scalar(rw[R, :], rw[R, :], rt[R, 11:12], float(T), ALU.mult, ALU.mult))
            V.tensor_tensor(wdiag[R], rw[R, :].unsqueeze(1).broadcast_to((B, B, E)),
                            ident[R, 0:B].unsqueeze(2).broadcast_to((B, B, E)), ALU.mult).then_inc(S("route2"), 1)
            dve.wait_ge(S("route_bc"), 1)
            link(V.tensor_copy(wd[:, :, :], PV[:, 0:B * E].rearrange("p (b e) -> p b e", b=B)))

            fetch(1, 1)
            second_loop(dve, turn)
def _shape_constants():
    f = np.float32
    i, j = np.arange(P)[:, None], np.arange(P)[None, :]
    k = {}
    k["ident"] = (i == j).astype(f)
    k["pairmean"] = 0.5 * (i // 2 == j // 2).astype(f)
    k["blk8"] = (i // 8 == j // 8).astype(f)
    k["blk16"] = (i // 16 == j // 16).astype(f) / T
    k["before"] = (i < j).astype(f)
    k["iota"] = np.broadcast_to(j, (P, P)).astype(f)
    key = np.arange(T)[None, :]
    k["ties"] = np.concatenate([(key < i + P * t).astype(f) for t in range(NT)], 1)
    e = np.arange(E)
    k["first8"] = np.broadcast_to((e[None, :] < e[:, None]).astype(f).reshape(1, E * E), (P, E * E))
    freq = 1.0 / 10000.0 ** (np.arange(0, ROPE, 2, dtype=f) / ROPE)
    ang = np.outer(np.arange(T, dtype=f), freq)
    cos, sin = np.cos(ang).T.astype(f), np.sin(ang).T.astype(f)
    c16, s16 = np.concatenate([cos, cos]), np.concatenate([-sin, sin])
    ones = np.ones((64, T), f)
    k["qtab"] = np.concatenate([ones, c16, c16, s16, s16])
    k["ktab"] = np.concatenate([ones, c16, s16, c16, s16])
    m = {"identb": (i == j).astype(f)}
    neg = lambda ok: np.where(ok, 0.0, NEG).astype(f)
    m["causal_s"] = neg(i >= j)
    m["causal_t"] = neg(j >= i)
    m["band_s"] = neg((i >= j) & (i - j < WINDOW))
    m["band_t"] = neg((j >= i) & (j - i < WINDOW))
    w = np.arange(BAND)[None, :]
    m["band_s1"] = neg((i + WINDOW >= w) & (i + WINDOW - w < WINDOW))
    m["band_t0"] = neg((w >= i) & (w - i < WINDOW))
    r = np.arange(HB)[None, :]
    m["pick"] = ((i == r) | (i == r + HB)).astype(f)
    return k, m


def _pack(table, parts):
    out = np.zeros((P, sum(table.values())), np.float32)
    at = 0
    for name, n in table.items():
        a = np.asarray(parts[name])
        out[:a.shape[0], at:at + n] = a.reshape(a.shape[0], n)
        at += n
    return out


def _swap(a):
    n = a.shape[-1] // 2
    return np.concatenate([a[..., n:], a[..., :n]], -1)


def _lay_out(x):
    z = lambda *s: np.zeros(s, np.float32)
    p, m = _shape_constants()
    order = np.arange(192).reshape(8, 3, 8).transpose(1, 0, 2).reshape(192)
    wi = x["L0_conv_w_qkv"].reshape(192, C)[order]
    dw = x["L0_conv_w_dw"].reshape(192, 5, 5)[order]
    pw = x["L0_conv_w_pw"].reshape(192, 8)[order]
    dwp = z(192, 26)
    for i, pair in enumerate(PAIRS5):
        dwp[:, 2 * i] = dw[:, pair[1], pair[2]]
        two = second_tap(pair, 5)
        if two:
            dwp[:, 2 * i + 1] = dw[:, two[0], two[1]]
    blocks = z(192, 192)
    for g in range(24):
        blocks[8 * g:8 * g + 8, 8 * g:8 * g + 8] = pw[8 * g:8 * g + 8].T
    p["w_q0"], p["w_kv0"] = wi[:64].T, wi[64:].T
    p["dw_q"], p["dw_kv"] = dwp[:64], dwp[64:]
    p["wi_q"], p["wi_kv"] = wi[:64], wi[64:]
    p["pw_q"], p["pw_kv"] = blocks[:64, :64], blocks[64:, 64:]
    wp = x["L0_conv_w_proj"].reshape(C, P).T
    p["proj0"] = np.concatenate([wp, wp], 1)
    bn = np.stack([x["L0_conv_bn_" + s] for s in ("gamma", "beta", "mean", "var")], 1)
    p["bn"] = np.concatenate([bn, bn], 0)
    w9 = x["L1_conv_weight"]
    conv1 = z(P, 5, C)
    for i, pair in enumerate(PAIRS3):
        conv1[:C, i] = w9[:, :, pair[1], pair[2]].T
        two = second_tap(pair, 3)
        if two:
            conv1[C:, i] = w9[:, :, two[0], two[1]].T
    p["conv1"] = conv1
    small = z(C, 68)
    small[:, 0:CQ], small[:, 32:64] = x["L2_attn_Wcq"], x["L2_attn_Wckv"]
    small[:, 64:67], small[:, 67:68] = x["L2_attn_Wgate"], x["L2_attn_W_imp"]
    p["w_small"] = small
    kr = x["L2_attn_Wk_rope"]
    p["w_kr"] = np.concatenate([z(C, 64), kr, _swap(kr), kr, _swap(kr)], 1)
    nw = z(P, 1)
    nw[0:CQ, 0], nw[32:64, 0] = x["L2_attn_q_norm_w"], x["L2_attn_kv_norm_w"]
    p["nw"] = nw
    qn = x["L2_attn_Wq_nope"].reshape(CQ, HEADS, NOPE)
    kn = x["L2_attn_Wk_nope"].reshape(CKV, HEADS, NOPE)
    p["wqn_t"], p["wkn_t"] = qn.transpose(2, 1, 0), kn.transpose(2, 1, 0)
    qr = x["L2_attn_Wq_rope"].reshape(CQ, HEADS, ROPE)
    p["w_q"] = np.concatenate([qn, z(CQ, HEADS, 32), qr, qr, _swap(qr), _swap(qr)], 2)
    wv1 = z(64, 512)
    wv1[32:64] = x["L2_attn_Wv"]
    p["w_v1"], p["w_v"] = wv1, np.concatenate([x["L2_attn_Wwin_v"], x["L2_attn_Wsel_v"]])
    k = np.concatenate([x["L2_attn_Wwin_k"], x["L2_attn_Wsel_k"]]).reshape(P, HEADS, HD)
    r = k[:, :, NOPE:]
    p["w_k"] = np.concatenate([k[:, :, :NOPE], z(P, HEADS, 32), r, _swap(r), r, _swap(r)], 2)
    p["w_p"] = x["L2_attn_Wproj"].reshape(4, P, C).transpose(1, 0, 2)
    p["r2"] = x["L2_ffn_router_w"].T
    p["w1"] = x["L2_ffn_w1"].transpose(1, 0, 2)
    p["b1"] = x["L2_ffn_b1"].reshape(4, P).T
    w2 = z(P, 4, 2, C)
    for e in range(E):
        w2[(e % 2) * C:(e % 2 + 1) * C, e // 2, e % 2] = x["L2_ffn_w2"][e]
    p["w2"] = w2
    p["b2"] = np.broadcast_to(x["L2_ffn_b2"].reshape(1, E * C), (P, E * C))
    wq = x["L3_attn_w_qkv"]
    p["q3"], p["kv3"], p["out3"] = wq[:, :P], wq[:, P:], x["L3_attn_w_out"]
    p["bout"] = np.broadcast_to(x["L3_attn_b_out"][None], (P, C))
    p["r3"] = x["L3_ffn_Wr"]
    p["br3"] = np.broadcast_to(x["L3_ffn_br"][None], (P, E))
    p["f1"] = x["L3_ffn_W1"].transpose(1, 0, 2)
    p["fb1"] = x["L3_ffn_b1"].T
    p["f2"] = x["L3_ffn_W2"].transpose(1, 0, 2)
    p["fb2"] = x["L3_ffn_b2"]
    p["gamma"] = np.broadcast_to(x["L3_ffn_gamma"][None], (P, C))
    p["beta"] = np.broadcast_to(x["L3_ffn_beta"][None], (P, C))
    return {
        "x": x["x"].reshape(B, C, T),
        "prep": _pack(PREP, p),
        "early": _pack(EARLY, p),
        "late": _pack(LATE, p),
        "masks": _pack(MASKS, m),
        "final": _pack(FINAL, p),
    }


def kernel(**inputs):
    import concourse.bacc as _bacc
    from concourse.bass_utils import run_bass_kernel_spmd as _run

    arrays = _lay_out({k: np.asarray(v) for k, v in inputs.items()})
    arrays = {k: np.ascontiguousarray(v) for k, v in arrays.items()}
    nc = _bacc.Bacc("TRN2", target_bir_lowering=False, num_devices=1)
    args = [nc.dram_tensor("in_" + k, v.shape, mybir.dt.from_np(v.dtype), kind="ExternalInput").ap()
            for k, v in arrays.items()]
    args.append(nc.dram_tensor("y", (B, C, T), F32, kind="ExternalOutput").ap())
    build(nc, *args)
    r = _run(nc, [{"in_" + k: v for k, v in arrays.items()}], core_ids=[0])
    return r.results[0]["y"].reshape(B, C, H, W)
```
